# Optimizing a Trainium2 kernel written in Bass

```python
import numpy as np
import jax
import jax.numpy as jnp

def _softmax(x, axis=-1):
    return jax.nn.softmax(x, axis=axis)

def _gelu(x):
    return jax.nn.gelu(x, approximate=True)

def _silu(x):
    return jax.nn.silu(x)

def _sigmoid(x):
    return jax.nn.sigmoid(x)

def _layernorm(x, axis=-1, eps=1e-05):
    m = jnp.mean(x, axis=axis, keepdims=True)
    v = jnp.var(x, axis=axis, keepdims=True)
    return (x - m) / jnp.sqrt(v + eps)

def _scatter_add(tgt, idx, src, axis=0):
    return tgt.at[idx].add(src)

def _segment_sum(src, seg, n):
    return jax.ops.segment_sum(src, seg, n)
kernel_name = 'mk_gnn_preln_d4_gnn_r32_6caad2'

def setup_inputs(seed: int=0):
    np.random.seed(seed)
    _w = jnp.asarray

    def _rec_inputs():
        import jax
        import jax.numpy as jnp
        _gk = jax.random.key(seed)
        x = -0.000202 + 1 * jax.random.normal(jax.random.fold_in(_gk, 1), (50000, 128), jnp.float32)
        src = jax.random.randint(jax.random.fold_in(_gk, 2), (50000,), 0, 50000, jnp.int32)
        dst = jnp.minimum((50000 * jax.random.uniform(jax.random.fold_in(_gk, 3), (50000,)) ** 2.0).astype(jnp.int32), 49999)
        _o = jnp.argsort(dst, stable=True)
        src = src[_o]
        dst = dst[_o]
        edge_attr_64 = 0.000167468 + 1.0002 * jax.random.normal(jax.random.fold_in(_gk, 11), (50000, 64), jnp.float32)
        edge_attr_8 = jax.random.uniform(jax.random.fold_in(_gk, 12), (50000, 8), jnp.float32, 0.0, 1)
        edge_type_8 = jax.random.randint(jax.random.fold_in(_gk, 14), (50000,), 0, 8, jnp.int32)
        edge_weight = jax.random.uniform(jax.random.fold_in(_gk, 15), (50000,), jnp.float32, 0.0, 0.999998)
        return (x, src, dst, edge_attr_64, edge_attr_8, edge_type_8, edge_weight)
    x, src, dst, edge_attr_64, edge_attr_8, edge_type_8, edge_weight = _rec_inputs()

    def _L0_gnn_setup():
        import jax, jax.numpy as jnp
        import numpy as np
        N_NODES = 50000
        N_EDGES = 18750
        D = 128
        R = 8
        EPS = 1e-05

        def layer_norm(x, g, b):
            mu = jnp.mean(x, axis=-1, keepdims=True)
            var = jnp.mean(jnp.square(x - mu), axis=-1, keepdims=True)
            return (x - mu) * jax.lax.rsqrt(var + EPS) * g + b

        def rgcn(x, src, dst, edge_attr, W, root, bias, num_nodes):
            E = src.shape[0]
            f = W.shape[-1]
            msg = jnp.zeros((E, f), dtype=x.dtype)
            for r in range(W.shape[0]):
                hr = x @ W[r]
                msg = msg + hr[src] * edge_attr[:, r][:, None]
            agg = jax.ops.segment_sum(msg, dst, num_segments=num_nodes)
            return agg + x @ root + bias
        key = jax.random.key(seed)
        ks = jax.random.split(key, 12)
        s = 1.0 / np.sqrt(D)
        return {'x': jax.random.normal(ks[0], (N_NODES, D), dtype=jnp.float32), 'edge_index': jax.random.randint(ks[1], (2, N_EDGES), 0, N_NODES, dtype=jnp.int64), 'edge_attr': jax.random.uniform(ks[2], (N_EDGES, R), dtype=jnp.float32), 'ln1_g': jnp.ones((D,), jnp.float32), 'ln1_b': jnp.zeros((D,), jnp.float32), 'W1': jax.random.normal(ks[3], (R, D, D), jnp.float32) * s, 'root1': jax.random.normal(ks[4], (D, D), jnp.float32) * s, 'b1': jnp.zeros((D,), jnp.float32), 'ln2_g': jnp.ones((D,), jnp.float32), 'ln2_b': jnp.zeros((D,), jnp.float32), 'W2': jax.random.normal(ks[5], (R, D, D), jnp.float32) * s, 'root2': jax.random.normal(ks[6], (D, D), jnp.float32) * s, 'b2': jnp.zeros((D,), jnp.float32)}
    _L0_gnn_all = _L0_gnn_setup()
    _L0_gnn_in = {k: v for k, v in _L0_gnn_all.items() if k in ('ln1_g', 'ln1_b', 'W1', 'root1', 'b1', 'ln2_g', 'ln2_b', 'W2', 'root2', 'b2')}
    del _L0_gnn_all

    def _L1_gnn_setup():
        import jax, jax.numpy as jnp
        import numpy as np
        N = 3125
        E = 50000
        D = 128
        H = 8
        HD = D // H
        T = 8

        def _layernorm(x, g, b, eps=1e-05):
            m = jnp.mean(x, axis=-1, keepdims=True)
            v = jnp.mean((x - m) ** 2, axis=-1, keepdims=True)
            return (x - m) * jax.lax.rsqrt(v + eps) * g + b
        key = jax.random.key(seed)
        ks = jax.random.split(key, 16)
        s = 0.02
        inp = {'x': jax.random.normal(ks[0], (N, D), jnp.float32), 'edge_index': jax.random.randint(ks[1], (2, E), 0, N, jnp.int32), 'edge_type': jax.random.randint(ks[2], (E,), 0, T, jnp.int32), 'Wq': jax.random.normal(ks[3], (D, D), jnp.float32) * s, 'bq': jnp.zeros((D,), jnp.float32), 'Wk': jax.random.normal(ks[4], (D, D), jnp.float32) * s, 'bk': jnp.zeros((D,), jnp.float32), 'Wv': jax.random.normal(ks[5], (D, D), jnp.float32) * s, 'bv': jnp.zeros((D,), jnp.float32), 'Wo': jax.random.normal(ks[6], (D, D), jnp.float32) * s, 'bo': jnp.zeros((D,), jnp.float32), 'edge_bias': jax.random.normal(ks[7], (T, H), jnp.float32) * s, 'W1': jax.random.normal(ks[8], (D, D), jnp.float32) * s, 'b1': jnp.zeros((D,), jnp.float32), 'W2': jax.random.normal(ks[9], (D, D), jnp.float32) * s, 'b2': jnp.zeros((D,), jnp.float32), 'g1': jnp.ones((D,), jnp.float32), 'be1': jnp.zeros((D,), jnp.float32), 'g2': jnp.ones((D,), jnp.float32), 'be2': jnp.zeros((D,), jnp.float32)}
        return inp
    _L1_gnn_all = _L1_gnn_setup()
    _L1_gnn_in = {k: v for k, v in _L1_gnn_all.items() if k in ('Wq', 'bq', 'Wk', 'bk', 'Wv', 'bv', 'Wo', 'bo', 'edge_bias', 'W1', 'b1', 'W2', 'b2', 'g1', 'be1', 'g2', 'be2')}
    del _L1_gnn_all

    def _L2_gnn_setup():
        import jax, jax.numpy as jnp
        import numpy as np
        N_NODES = 625
        N_EDGES = 20000
        HIDDEN = 128
        EDGE_DIM = 64

        def _gru_cell(m, h, Wih, Whh, bih, bhh):
            gi = m @ Wih.T + bih
            gh = h @ Whh.T + bhh
            i_r, i_z, i_n = jnp.split(gi, 3, axis=-1)
            h_r, h_z, h_n = jnp.split(gh, 3, axis=-1)
            r = jax.nn.sigmoid(i_r + h_r)
            z = jax.nn.sigmoid(i_z + h_z)
            n = jnp.tanh(i_n + r * h_n)
            return (1.0 - z) * n + z * h

        def _dmpnn_layer(x, src, dst, edge_attr, W_msg, Wih, Whh, bih, bhh):
            n_nodes = x.shape[0]
            msg = jnp.concatenate([x[src], edge_attr], axis=-1) @ W_msg.T
            agg = jax.ops.segment_sum(msg, dst, num_segments=n_nodes)
            return _gru_cell(agg, x, Wih, Whh, bih, bhh)
        key = jax.random.key(seed)
        ks = jax.random.split(key, 16)
        s_h = 1.0 / np.sqrt(HIDDEN)
        s_m = 1.0 / np.sqrt(HIDDEN + EDGE_DIM)
        return {'x': jax.random.normal(ks[0], (N_NODES, HIDDEN), jnp.float32), 'edge_index': jax.random.randint(ks[1], (2, N_EDGES), 0, N_NODES, jnp.int64), 'edge_attr': jax.random.normal(ks[2], (N_EDGES, EDGE_DIM), jnp.float32), 'W_msg1': jax.random.normal(ks[3], (HIDDEN, HIDDEN + EDGE_DIM), jnp.float32) * s_m, 'Wih1': jax.random.normal(ks[4], (3 * HIDDEN, HIDDEN), jnp.float32) * s_h, 'Whh1': jax.random.normal(ks[5], (3 * HIDDEN, HIDDEN), jnp.float32) * s_h, 'bih1': jnp.zeros((3 * HIDDEN,), jnp.float32), 'bhh1': jnp.zeros((3 * HIDDEN,), jnp.float32), 'W_msg2': jax.random.normal(ks[6], (HIDDEN, HIDDEN + EDGE_DIM), jnp.float32) * s_m, 'Wih2': jax.random.normal(ks[7], (3 * HIDDEN, HIDDEN), jnp.float32) * s_h, 'Whh2': jax.random.normal(ks[8], (3 * HIDDEN, HIDDEN), jnp.float32) * s_h, 'bih2': jnp.zeros((3 * HIDDEN,), jnp.float32), 'bhh2': jnp.zeros((3 * HIDDEN,), jnp.float32)}
    _L2_gnn_all = _L2_gnn_setup()
    _L2_gnn_in = {k: v for k, v in _L2_gnn_all.items() if k in ('W_msg1', 'Wih1', 'Whh1', 'bih1', 'bhh1', 'W_msg2', 'Wih2', 'Whh2', 'bih2', 'bhh2')}
    del _L2_gnn_all

    def _L3_gnn_setup():
        import jax, jax.numpy as jnp
        import numpy as np
        N = 50000
        E = 25000
        D = 128

        def _gru_step(W0, w_ih, w_hh, b_ih, b_hh):
            gi = W0 @ w_ih.T + b_ih
            gh = W0 @ w_hh.T + b_hh
            i_r, i_z, i_n = jnp.split(gi, 3, axis=-1)
            h_r, h_z, h_n = jnp.split(gh, 3, axis=-1)
            r = jax.nn.sigmoid(i_r + h_r)
            z = jax.nn.sigmoid(i_z + h_z)
            n = jnp.tanh(i_n + r * h_n)
            return (1.0 - z) * n + z * W0
        key = jax.random.key(seed)
        ks = jax.random.split(key, 10)
        s = 1.0 / np.sqrt(D)
        x = jax.random.normal(ks[0], (N, D), jnp.float32)
        edge_index = jax.random.randint(ks[1], (2, E), 0, N, dtype=jnp.int32)
        edge_weight = jax.random.uniform(ks[2], (E,), jnp.float32)
        W0 = jax.random.normal(ks[3], (D, D), jnp.float32) * s
        gru_w_ih = jax.random.normal(ks[4], (3 * D, D), jnp.float32) * s
        gru_w_hh = jax.random.normal(ks[5], (3 * D, D), jnp.float32) * s
        gru_b_ih = jax.random.normal(ks[6], (3 * D,), jnp.float32) * s
        gru_b_hh = jax.random.normal(ks[7], (3 * D,), jnp.float32) * s
        lin_w = jax.random.normal(ks[8], (D, D), jnp.float32) * s
        lin_b = jax.random.normal(ks[9], (D,), jnp.float32) * s
        return dict(x=x, edge_index=edge_index, edge_weight=edge_weight, W0=W0, gru_w_ih=gru_w_ih, gru_w_hh=gru_w_hh, gru_b_ih=gru_b_ih, gru_b_hh=gru_b_hh, lin_w=lin_w, lin_b=lin_b)
    _L3_gnn_all = _L3_gnn_setup()
    _L3_gnn_in = {k: v for k, v in _L3_gnn_all.items() if k in ('W0', 'gru_w_ih', 'gru_w_hh', 'gru_b_ih', 'gru_b_hh', 'lin_w', 'lin_b')}
    del _L3_gnn_all
    return {'x': x, 'src': src, 'dst': dst, 'edge_attr_64': edge_attr_64, 'edge_attr_8': edge_attr_8, 'edge_type_8': edge_type_8, 'edge_weight': edge_weight, 'L0_gnn_ln1_g': _L0_gnn_in['ln1_g'], 'L0_gnn_ln1_b': _L0_gnn_in['ln1_b'], 'L0_gnn_W1': _L0_gnn_in['W1'], 'L0_gnn_root1': _L0_gnn_in['root1'], 'L0_gnn_b1': _L0_gnn_in['b1'], 'L0_gnn_ln2_g': _L0_gnn_in['ln2_g'], 'L0_gnn_ln2_b': _L0_gnn_in['ln2_b'], 'L0_gnn_W2': _L0_gnn_in['W2'], 'L0_gnn_root2': _L0_gnn_in['root2'], 'L0_gnn_b2': _L0_gnn_in['b2'], 'L1_gnn_Wq': _L1_gnn_in['Wq'], 'L1_gnn_bq': _L1_gnn_in['bq'], 'L1_gnn_Wk': _L1_gnn_in['Wk'], 'L1_gnn_bk': _L1_gnn_in['bk'], 'L1_gnn_Wv': _L1_gnn_in['Wv'], 'L1_gnn_bv': _L1_gnn_in['bv'], 'L1_gnn_Wo': _L1_gnn_in['Wo'], 'L1_gnn_bo': _L1_gnn_in['bo'], 'L1_gnn_edge_bias': _L1_gnn_in['edge_bias'], 'L1_gnn_W1': _L1_gnn_in['W1'], 'L1_gnn_b1': _L1_gnn_in['b1'], 'L1_gnn_W2': _L1_gnn_in['W2'], 'L1_gnn_b2': _L1_gnn_in['b2'], 'L1_gnn_g1': _L1_gnn_in['g1'], 'L1_gnn_be1': _L1_gnn_in['be1'], 'L1_gnn_g2': _L1_gnn_in['g2'], 'L1_gnn_be2': _L1_gnn_in['be2'], 'L2_gnn_W_msg1': _L2_gnn_in['W_msg1'], 'L2_gnn_Wih1': _L2_gnn_in['Wih1'], 'L2_gnn_Whh1': _L2_gnn_in['Whh1'], 'L2_gnn_bih1': _L2_gnn_in['bih1'], 'L2_gnn_bhh1': _L2_gnn_in['bhh1'], 'L2_gnn_W_msg2': _L2_gnn_in['W_msg2'], 'L2_gnn_Wih2': _L2_gnn_in['Wih2'], 'L2_gnn_Whh2': _L2_gnn_in['Whh2'], 'L2_gnn_bih2': _L2_gnn_in['bih2'], 'L2_gnn_bhh2': _L2_gnn_in['bhh2'], 'L3_gnn_W0': _L3_gnn_in['W0'], 'L3_gnn_gru_w_ih': _L3_gnn_in['gru_w_ih'], 'L3_gnn_gru_w_hh': _L3_gnn_in['gru_w_hh'], 'L3_gnn_gru_b_ih': _L3_gnn_in['gru_b_ih'], 'L3_gnn_gru_b_hh': _L3_gnn_in['gru_b_hh'], 'L3_gnn_lin_w': _L3_gnn_in['lin_w'], 'L3_gnn_lin_b': _L3_gnn_in['lin_b']}

def reference(x, src, dst, edge_attr_64, edge_attr_8, edge_type_8, edge_weight, L0_gnn_ln1_g, L0_gnn_ln1_b, L0_gnn_W1, L0_gnn_root1, L0_gnn_b1, L0_gnn_ln2_g, L0_gnn_ln2_b, L0_gnn_W2, L0_gnn_root2, L0_gnn_b2, L1_gnn_Wq, L1_gnn_bq, L1_gnn_Wk, L1_gnn_bk, L1_gnn_Wv, L1_gnn_bv, L1_gnn_Wo, L1_gnn_bo, L1_gnn_edge_bias, L1_gnn_W1, L1_gnn_b1, L1_gnn_W2, L1_gnn_b2, L1_gnn_g1, L1_gnn_be1, L1_gnn_g2, L1_gnn_be2, L2_gnn_W_msg1, L2_gnn_Wih1, L2_gnn_Whh1, L2_gnn_bih1, L2_gnn_bhh1, L2_gnn_W_msg2, L2_gnn_Wih2, L2_gnn_Whh2, L2_gnn_bih2, L2_gnn_bhh2, L3_gnn_W0, L3_gnn_gru_w_ih, L3_gnn_gru_w_hh, L3_gnn_gru_b_ih, L3_gnn_gru_b_hh, L3_gnn_lin_w, L3_gnn_lin_b):
    import jax
    import jax.numpy as jnp

    def _L0_gnn_ref(x, edge_index, edge_attr, ln1_g, ln1_b, W1, root1, b1, ln2_g, ln2_b, W2, root2, b2):
        import jax, jax.numpy as jnp
        import numpy as np
        N_NODES = 50000
        N_EDGES = 18750
        D = 128
        R = 8
        EPS = 1e-05

        def layer_norm(x, g, b):
            mu = jnp.mean(x, axis=-1, keepdims=True)
            var = jnp.mean(jnp.square(x - mu), axis=-1, keepdims=True)
            return (x - mu) * jax.lax.rsqrt(var + EPS) * g + b

        def rgcn(x, src, dst, edge_attr, W, root, bias, num_nodes):
            E = src.shape[0]
            f = W.shape[-1]
            msg = jnp.zeros((E, f), dtype=x.dtype)
            for r in range(W.shape[0]):
                hr = x @ W[r]
                msg = msg + hr[src] * edge_attr[:, r][:, None]
            agg = jax.ops.segment_sum(msg, dst, num_segments=num_nodes)
            return agg + x @ root + bias
        src, dst = (edge_index[0], edge_index[1])
        identity = x
        out = jax.nn.gelu(layer_norm(x, ln1_g, ln1_b), approximate=False)
        out = rgcn(out, src, dst, edge_attr, W1, root1, b1, x.shape[0])
        out = jax.nn.gelu(layer_norm(out, ln2_g, ln2_b), approximate=False)
        out = rgcn(out, src, dst, edge_attr, W2, root2, b2, x.shape[0])
        return out + identity

    def _L1_gnn_ref(x, edge_index, edge_type, Wq, bq, Wk, bk, Wv, bv, Wo, bo, edge_bias, W1, b1, W2, b2, g1, be1, g2, be2):
        import jax, jax.numpy as jnp
        import numpy as np
        N = 3125
        E = 50000
        D = 128
        H = 8
        HD = D // H
        T = 8

        def _layernorm(x, g, b, eps=1e-05):
            m = jnp.mean(x, axis=-1, keepdims=True)
            v = jnp.mean((x - m) ** 2, axis=-1, keepdims=True)
            return (x - m) * jax.lax.rsqrt(v + eps) * g + b
        n = x.shape[0]
        scale = HD ** (-0.5)
        Q = (x @ Wq + bq).reshape(n, H, HD)
        K = (x @ Wk + bk).reshape(n, H, HD)
        V = (x @ Wv + bv).reshape(n, H, HD)
        src, dst = (edge_index[0], edge_index[1])
        attn = jnp.sum(Q[dst] * K[src], axis=-1) * scale + edge_bias[edge_type]
        mx = jax.ops.segment_max(attn, dst, num_segments=n)
        ex = jnp.exp(attn - mx[dst])
        sm = jax.ops.segment_sum(ex, dst, num_segments=n)
        a = ex / (sm[dst] + 1e-16)
        out = jax.ops.segment_sum(a[..., None] * V[src], dst, num_segments=n)
        out = out.reshape(n, D) @ Wo + bo
        x = _layernorm(x + out, g1, be1)
        ffn = jax.nn.gelu(x @ W1 + b1, approximate=False) @ W2 + b2
        return _layernorm(x + ffn, g2, be2)

    def _L2_gnn_ref(x, edge_index, edge_attr, W_msg1, Wih1, Whh1, bih1, bhh1, W_msg2, Wih2, Whh2, bih2, bhh2):
        import jax, jax.numpy as jnp
        import numpy as np
        N_NODES = 625
        N_EDGES = 20000
        HIDDEN = 128
        EDGE_DIM = 64

        def _gru_cell(m, h, Wih, Whh, bih, bhh):
            gi = m @ Wih.T + bih
            gh = h @ Whh.T + bhh
            i_r, i_z, i_n = jnp.split(gi, 3, axis=-1)
            h_r, h_z, h_n = jnp.split(gh, 3, axis=-1)
            r = jax.nn.sigmoid(i_r + h_r)
            z = jax.nn.sigmoid(i_z + h_z)
            n = jnp.tanh(i_n + r * h_n)
            return (1.0 - z) * n + z * h

        def _dmpnn_layer(x, src, dst, edge_attr, W_msg, Wih, Whh, bih, bhh):
            n_nodes = x.shape[0]
            msg = jnp.concatenate([x[src], edge_attr], axis=-1) @ W_msg.T
            agg = jax.ops.segment_sum(msg, dst, num_segments=n_nodes)
            return _gru_cell(agg, x, Wih, Whh, bih, bhh)
        src, dst = (edge_index[0], edge_index[1])
        x = _dmpnn_layer(x, src, dst, edge_attr, W_msg1, Wih1, Whh1, bih1, bhh1)
        x = _dmpnn_layer(x, src, dst, edge_attr, W_msg2, Wih2, Whh2, bih2, bhh2)
        return x

    def _L3_gnn_ref(x, edge_index, edge_weight, W0, gru_w_ih, gru_w_hh, gru_b_ih, gru_b_hh, lin_w, lin_b):
        import jax, jax.numpy as jnp
        import numpy as np
        N = 50000
        E = 25000
        D = 128

        def _gru_step(W0, w_ih, w_hh, b_ih, b_hh):
            gi = W0 @ w_ih.T + b_ih
            gh = W0 @ w_hh.T + b_hh
            i_r, i_z, i_n = jnp.split(gi, 3, axis=-1)
            h_r, h_z, h_n = jnp.split(gh, 3, axis=-1)
            r = jax.nn.sigmoid(i_r + h_r)
            z = jax.nn.sigmoid(i_z + h_z)
            n = jnp.tanh(i_n + r * h_n)
            return (1.0 - z) * n + z * W0
        n_nodes = x.shape[0]
        W = _gru_step(W0, gru_w_ih, gru_w_hh, gru_b_ih, gru_b_hh)
        src, dst = (edge_index[0], edge_index[1])
        loop = jnp.arange(n_nodes, dtype=edge_index.dtype)
        row = jnp.concatenate([src, loop])
        col = jnp.concatenate([dst, loop])
        w = jnp.concatenate([edge_weight, jnp.ones((n_nodes,), x.dtype)])
        deg = jax.ops.segment_sum(w, col, num_segments=n_nodes)
        dinv = jnp.where(deg > 0, jax.lax.rsqrt(deg), 0.0)
        norm = dinv[row] * w * dinv[col]
        xw = x @ W
        msgs = norm[:, None] * xw[row]
        h = jax.ops.segment_sum(msgs, col, num_segments=n_nodes)
        h = jax.nn.relu(h)
        return h @ lin_w.T + lin_b
    edge_index = jnp.stack([src, dst])
    h = jnp.maximum(_layernorm(x, axis=-1), 0.0)
    x = x + _L0_gnn_ref(h, edge_index, edge_attr_8, L0_gnn_ln1_g, L0_gnn_ln1_b, L0_gnn_W1, L0_gnn_root1, L0_gnn_b1, L0_gnn_ln2_g, L0_gnn_ln2_b, L0_gnn_W2, L0_gnn_root2, L0_gnn_b2)
    h = jnp.maximum(_layernorm(x, axis=-1), 0.0)
    x = x + _L1_gnn_ref(h, edge_index, edge_type_8, L1_gnn_Wq, L1_gnn_bq, L1_gnn_Wk, L1_gnn_bk, L1_gnn_Wv, L1_gnn_bv, L1_gnn_Wo, L1_gnn_bo, L1_gnn_edge_bias, L1_gnn_W1, L1_gnn_b1, L1_gnn_W2, L1_gnn_b2, L1_gnn_g1, L1_gnn_be1, L1_gnn_g2, L1_gnn_be2)
    h = jnp.maximum(_layernorm(x, axis=-1), 0.0)
    x = x + _L2_gnn_ref(h, edge_index, edge_attr_64, L2_gnn_W_msg1, L2_gnn_Wih1, L2_gnn_Whh1, L2_gnn_bih1, L2_gnn_bhh1, L2_gnn_W_msg2, L2_gnn_Wih2, L2_gnn_Whh2, L2_gnn_bih2, L2_gnn_bhh2)
    h = jnp.maximum(_layernorm(x, axis=-1), 0.0)
    x = x + _L3_gnn_ref(h, edge_index, edge_weight, L3_gnn_W0, L3_gnn_gru_w_ih, L3_gnn_gru_w_hh, L3_gnn_gru_b_ih, L3_gnn_gru_b_hh, L3_gnn_lin_w, L3_gnn_lin_b)
    return x

_drawn_inputs = setup_inputs


def setup_inputs(seed=0):
    import zlib

    import numpy as np

    out = dict(_drawn_inputs(seed))
    spreads = {'L0_gnn_ln1_g': (1.0, 0.2),
     'L0_gnn_ln1_b': (0.0, 0.1),
     'L0_gnn_b1': (0.0, 0.1),
     'L0_gnn_ln2_g': (1.0, 0.2),
     'L0_gnn_ln2_b': (0.0, 0.1),
     'L0_gnn_b2': (0.0, 0.1),
     'L1_gnn_bq': (0.0, 2.0),
     'L1_gnn_bk': (0.0, 2.0),
     'L1_gnn_bv': (0.0, 0.8),
     'L1_gnn_bo': (0.0, 0.1),
     'L1_gnn_b1': (0.0, 0.8),
     'L1_gnn_b2': (0.0, 0.469),
     'L1_gnn_g1': (1.0, 0.2),
     'L1_gnn_be1': (0.0, 0.285),
     'L1_gnn_g2': (1.0, 0.2),
     'L1_gnn_be2': (0.0, 0.274),
     'L2_gnn_bih1': (0.0, 0.8),
     'L2_gnn_bhh1': (0.0, 0.8),
     'L2_gnn_bih2': (0.0, 0.574),
     'L2_gnn_bhh2': (0.0, 0.8)}
    factors = {'L1_gnn_Wq': 8.0,
     'L1_gnn_Wk': 8.0,
     'L1_gnn_Wv': 4.428,
     'L1_gnn_Wo': 3.847,
     'L1_gnn_edge_bias': 64.0,
     'L1_gnn_W1': 7.011,
     'L1_gnn_W2': 6.249}
    for name, (base, spread) in spreads.items():
        noise = np.random.default_rng([zlib.crc32(name.encode()), seed]).standard_normal(out[name].shape)
        drawn = base * np.exp(spread * noise) if base else spread * noise
        out[name] = jnp.asarray(drawn.astype(out[name].dtype))
    for name, factor in factors.items():
        out[name] = (out[name] * factor).astype(out[name].dtype)
    return out
```

```python
from contextlib import ExitStack

import concourse.bass as bass
from concourse import mybir

P = 128
D = 128
RELATIONS = 8
HEADS = 8
HEAD_DIM = D // HEADS
EDGE_DIM = 64
B = 4
SLOTS = 4
EPS = 1e-5
ROUND = 12582912.0
FAR = 1.5e38

F32 = mybir.dt.float32
F16 = mybir.dt.float16
I32 = mybir.dt.int32
ALU = mybir.AluOpType
ACT = mybir.ActivationFunctionType
AX = mybir.AxisListType

SRC, DST, EDGE, TYPE, WEIGHT, SAME, REL, FIELDS = 0, 1, 2, 3, 4, 5, 8, 16


class At:

    def __init__(self, turn, slot):
        self.turn, self.s = turn, slot
        self.b = turn * SLOTS + slot

    def back(self, k):
        s = (self.s - k) % SLOTS
        return At(self.turn + (self.s - k - s) // SLOTS, s)

    def has(self, k):
        return not isinstance(self.turn, int) or self.b >= k

    def columns(self):
        return bass.ds(self.b * B, B)


class Steps:

    def __init__(self, nc, name, *steps):
        self.sem, self.steps, self.at_step = nc.alloc_semaphore(name), steps, 0

    def did(self, step):
        assert self.steps[self.at_step % len(self.steps)] == step, (step, self.at_step)
        self.at_step += 1
        return self.sem, 1

    def after(self, at, step):
        return self.sem, at.b * len(self.steps) + (self.steps.index(step) + 1)


class Moves:

    def __init__(self, nc, name, n):
        self.sems, self.n = [nc.alloc_semaphore(f"{name}{s}") for s in range(SLOTS)], n

    def did(self, at):
        return self.sems[at.s], 16

    def after(self, at):
        return self.sems[at.s], (at.turn + 1) * (16 * self.n)

    def all_of(self, eng, turns):
        for sem in self.sems:
            eng.wait_ge(sem, turns * 16 * self.n)


def batches(eng, turns, *stages):
    lags = max(lag for _, lag in stages)
    peeled = 2 if lags <= SLOTS else 3

    def each(at):
        for stage, lag in stages:
            if at.has(lag) and not (isinstance(at.turn, int) and at.b - lag >= SLOTS * turns):
                stage(at.back(lag))

    for b in range(peeled * SLOTS):
        each(At(b // SLOTS, b % SLOTS))
    with eng.Fori(peeled, turns) as turn:
        for slot in range(SLOTS):
            each(At(turn, slot))
    for b in range(SLOTS * turns, SLOTS * turns + lags):
        each(At(b // SLOTS, b % SLOTS))


class Pass:

    def __init__(self, nc, name):
        self.nc, self.name, self.ctx, self.sems = nc, name, ExitStack(), []

    def __enter__(self):
        self.ctx.__enter__()
        return self

    def __exit__(self, *e):
        self.ctx.__exit__(*e)
        if e[0] is None:
            self.nc.clear_and_free_semaphores(self.sems)
            self.nc.all_engine_barrier()

    def sb(self, name, shape, dt=F32):
        return self.ctx.enter_context(self.nc.sbuf_tensor(f"{self.name}_{name}", shape, dt))

    def ps(self, name, shape, dt=F32):
        return self.ctx.enter_context(self.nc.psum_tensor(f"{self.name}_{name}", shape, dt))

    def slots(self, name, shape, dt=F32):
        return [self.sb(f"{name}{s}", shape, dt) for s in range(SLOTS)]

    def sem(self, name):
        sem = self.nc.alloc_semaphore(f"{self.name}_{name}")
        self.sems.append(sem)
        return sem

    def steps(self, name, *steps):
        out = Steps(self.nc, f"{self.name}_{name}", *steps)
        self.sems.append(out.sem)
        return out

    def moves(self, name, n):
        out = Moves(self.nc, f"{self.name}_{name}", n)
        self.sems += out.sems
        return out


class Graph:

    def __init__(self, nc, ctx, T):
        self.T, self.turns = T, T // (SLOTS * B)
        assert T % (SLOTS * B) == 0 and self.turns > 3

        def sb(name, shape, dt=F32):
            return ctx.enter_context(nc.sbuf_tensor(name, shape, dt))

        self.record = sb("record", [P, T, FIELDS])
        self.src = sb("src_of_edge", [P, T], I32)
        self.dst = sb("dst_of_edge", [P, T], I32)
        self.edge = sb("edge_of_place", [P, T], I32)
        self.end = sb("end_of_node", [P, T], I32)
        self.first_end = sb("first_end", [P, 1], I32)
        self.ident = sb("ident", [P, P])
        self.before = sb("before", [P, P])
        self.ones = sb("ones", [P, P])
        self.carries = sb("carries", [P, P])
        self.far_before = sb("far_before", [P, P])
        self.far_after = sb("far_after", [P, P])
        self.in_first = sb("in_first", [P, T])
        self.in_last = sb("in_last", [P, T])
        self.far_flag = sb("far_flag", [P, T])
        self.far_flag_back = sb("far_flag_back", [P, T])
        self.attention = sb("attention", [P, T, HEADS])
        self.degree = sb("degree", [P, T])


def columns_of(table, T):
    return table[0:P * T].rearrange("(p t) f -> p t f", t=T)


def sort_edges(nc, g, src, dst, edge_type, edge_weight, edge_attr_8, records):
    T = g.T
    with Pass(nc, "sort") as w:
        dst_i, src_i, type_i = (w.sb(n, [P, T], I32) for n in ("dst_i", "src_i", "type_i"))
        edge_i = w.sb("edge_i", [P, T], I32)
        weight = w.sb("weight", [P, T])
        attr = w.sb("attr", [P, T, RELATIONS])
        dst_f = w.sb("dst_f", [P, T])
        digits = w.sb("digits", [P, T, 2])
        iota_i = w.sb("iota_i", [P, max(T, P)], I32)
        iota = w.sb("iota", [P, max(T, P)], F16)
        ident16 = w.sb("ident16", [P, P], F16)
        zeros16 = w.sb("zeros16", [P, max(T, P)], F16)
        count, upto, spare = (w.sb(n, [P, T]) for n in ("count", "upto", "spare"))
        free = [w.sb(f"free{k}", [P, T]) for k in range(2)]
        loaded, made, derived, chain = (w.sem(n) for n in ("loaded", "made", "derived", "chain"))

        with nc.Block() as block:

            @block.sync
            def _(sp):
                for out, table in ((dst_i, dst), (src_i, src), (type_i, edge_type), (weight, edge_weight)):
                    sp.dma_start(out[:, :], table.rearrange("(p t) -> p t", t=T)).then_inc(loaded, 16)
                sp.dma_start(attr[:, :, :], columns_of(edge_attr_8, T)).then_inc(loaded, 16)
                sp.wait_ge(loaded, 5 * 16)

            @block.gpsimd
            def _(pool):
                pool.iota(iota_i[:, :], pattern=[[1, max(T, P)]], base=0, channel_multiplier=0).then_inc(made, 1)
                pool.iota(edge_i[:, :], pattern=[[1, T]], base=0, channel_multiplier=T).then_inc(made, 1)
                pool.memset(g.ones[:, :], 1.0).then_inc(made, 1)
                pool.wait_ge(made, 3)
                pool.affine_select(out=g.ident[:, :], in_=g.ones[:, :], pattern=[[-1, P]], compare_op=ALU.is_equal,
                                   fill=0.0, base=0, channel_multiplier=1).then_inc(made, 1)
                pool.affine_select(out=g.before[:, :], in_=g.ones[:, :], pattern=[[1, P]], compare_op=ALU.is_gt,
                                   fill=0.0, base=0, channel_multiplier=-1).then_inc(made, 1)

            @block.vector
            def _(dve):
                n = 0

                def then(ins):
                    nonlocal n
                    n += 1
                    ins.then_inc(chain, 1)
                    dve.wait_ge(chain, n)

                dve.memset(zeros16[:, :], 0.0).then_inc(derived, 1)
                dve.memset(g.record[:, :, :], 0.0).then_inc(derived, 1)
                dve.wait_ge(made, 5)
                dve.wait_ge(loaded, 5 * 16)
                dve.tensor_copy(iota[:, :], iota_i[:, :]).then_inc(derived, 1)
                dve.tensor_copy(ident16[:, :], g.ident[:, :]).then_inc(derived, 1)
                then(dve.tensor_copy(dst_f[:, :], dst_i[:, :]))
                then(dve.tensor_scalar(spare[:, :], dst_f[:, :], 1.0 / T, 0.5 / T - 0.5, ALU.mult, ALU.add))
                then(dve.tensor_scalar(upto[:, :], spare[:, :], ROUND, None, ALU.add))
                then(dve.tensor_scalar(digits[:, :, 0], upto[:, :], ROUND, None, ALU.subtract))
                then(dve.scalar_tensor_tensor(digits[:, :, 1], digits[:, :, 0], -float(T), dst_f[:, :], ALU.mult, ALU.add))
                dve.wait_ge(derived, 2)
                for field, table in ((SRC, src_i), (DST, dst_i), (EDGE, edge_i), (TYPE, type_i), (WEIGHT, weight)):
                    dve.tensor_copy(g.record[:, :, field], table[:, :]).then_inc(derived, 1)
                dve.tensor_copy(g.record[:, :, REL:REL + RELATIONS], attr[:, :, :]).then_inc(derived, 1)

        one_hi, one_lo = w.slots("one_hi", [P, B, P], F16), w.slots("one_lo", [P, B, T], F16)
        digit = w.slots("digit", [P, B, 2])
        total = w.ps("total", [P, T])

        def one_hots(dve, digit_ready, steps, pe_used):
            def stage(at):
                dve.wait_ge(*digit_ready.after(at, "digit"))
                if at.has(SLOTS):
                    dve.wait_ge(*pe_used(at.back(SLOTS)))
                for j in range(B):
                    dve.tensor_scalar(one_hi[at.s][:, j, :], iota[:, 0:P], digit[at.s][:, j, 0:1], None, ALU.is_equal)
                    last = dve.tensor_scalar(one_lo[at.s][:, j, :], iota[:, 0:T], digit[at.s][:, j, 1:2], None,
                                             ALU.is_equal)
                last.then_inc(*steps.did("one_hots"))
            return stage

        act_c = w.steps("act_c", "digit")
        dve_c = w.steps("dve_c", "one_hots")
        pe_c = w.steps("pe_c", "counted")
        zeroed, scanned, offset = w.sem("zeroed"), w.sem("scanned"), w.sem("offset")
        with nc.Block() as block:

            @block.scalar
            def _(act):
                def stage(at):
                    if at.has(SLOTS):
                        act.wait_ge(*dve_c.after(at.back(SLOTS), "one_hots"))
                    act.copy(digit[at.s][:, :, :], digits[:, at.columns(), :]).then_inc(*act_c.did("digit"))
                batches(act, g.turns, (stage, 0))

            @block.vector
            def _(dve):
                batches(dve, g.turns, (one_hots(dve, act_c, dve_c, lambda at: pe_c.after(at, "counted")), 0))
                dve.wait_ge(*pe_c.after(At(g.turns - 1, SLOTS - 1), "counted"))
                dve.wait_ge(zeroed, 2)
                dve.tensor_copy(count[:, :], total[:, :]).then_inc(scanned, 1)
                dve.memset(spare[:, :], 1.0).then_inc(scanned, 1)
                dve.wait_ge(scanned, 2)
                dve.tensor_tensor_scan(upto[:, :], spare[:, :], count[:, :], 0.0, ALU.mult, ALU.add).then_inc(scanned, 1)
                dve.wait_ge(offset, 1)
                dve.wait_ge(scanned, 3)
                dve.tensor_scalar(dst_f[:, :], upto[:, :], total[:, 0:1], -1.0, ALU.add, ALU.add).then_inc(scanned, 1)
                dve.wait_ge(scanned, 4)
                dve.scalar_tensor_tensor(free[0][:, :], dst_f[:, :], 1.0, count[:, :], ALU.add, ALU.subtract).then_inc(scanned, 1)
                dve.tensor_scalar(spare[:, :], count[:, :], 0.0, None, ALU.is_equal).then_inc(scanned, 1)
                dve.tensor_scalar(upto[:, :], dst_f[:, :], -1.0, float(P * T), ALU.mult, ALU.add).then_inc(scanned, 1)
                dve.wait_ge(scanned, 7)
                dve.tensor_tensor(spare[:, :], spare[:, :], upto[:, :], ALU.mult).then_inc(scanned, 1)
                dve.wait_ge(scanned, 8)
                dve.tensor_tensor(g.end[:, :], spare[:, :], dst_f[:, :], ALU.add).then_inc(scanned, 1)

            @block.tensor
            def _(pe):
                pe.matmul(total[:, :], zeros16[:, 0:P], zeros16[:, 0:T], start=True, stop=False,
                          skip_group_check=True).then_inc(zeroed, 1)

                def stage(at):
                    pe.wait_ge(*dve_c.after(at, "one_hots"))
                    for j in range(B):
                        last = pe.matmul(total[:, :], one_hi[at.s][:, j, :], one_lo[at.s][:, j, :],
                                         start=False, stop=False, skip_group_check=True)
                    last.then_inc(*pe_c.did("counted"))
                batches(pe, g.turns, (stage, 0))
                pe.matmul(total[:, :], zeros16[:, 0:P], zeros16[:, 0:T], start=False, stop=True,
                          skip_group_check=True).then_inc(zeroed, 1)
                pe.wait_ge(scanned, 3)
                pe.matmul(total[:, 0:1], g.before[:, :], upto[:, T - 1:T], start=True, stop=True).then_inc(offset, 1)

        hi_t = w.slots("hi_t", [P, B, P])
        pairs16 = w.slots("pairs16", [P, B, P], F16)
        row = w.slots("row", [P, B, FIELDS])
        place, place_i = w.slots("place", [P, B]), w.slots("place_i", [P, B], I32)
        junk = w.sb("junk", [P, T])
        hi_ps = w.ps("hi_ps", [P, B, P], F16)
        same_ps = w.ps("same_ps", [P, B, P])
        more_ps = [w.ps(f"more_ps{k}", [P, T]) for k in range(2)]
        at_ps = [w.ps(f"at_ps{k}", [P, T]) for k in range(2)]
        act_r = w.steps("act_r", "digit", "row", "hi_t")
        dve_a = w.steps("dve_a", "one_hots")
        dve_p = w.steps("dve_p", "pairs")
        dve_r = w.steps("dve_r", *[f"{x}{j}" for j in range(B) for x in ("free", "place")], "place_i")
        pe_t = w.steps("pe_t", "hi_ps", "same_ps")
        pe_r = w.steps("pe_r", *[f"{x}{j}" for j in range(B) for x in ("more", "at")])
        stored = w.moves("stored", B)
        gate = w.sem("gate")
        with nc.Block() as block:

            @block.scalar
            def _(act):
                def early(at):
                    if at.has(SLOTS):
                        act.wait_ge(*dve_a.after(at.back(SLOTS), "one_hots"))
                    act.copy(digit[at.s][:, :, :], digits[:, at.columns(), :]).then_inc(*act_r.did("digit"))
                    if at.has(SLOTS):
                        act.wait_ge(*stored.after(at.back(SLOTS)))
                    act.copy(row[at.s][:, :, :], g.record[:, at.columns(), :]).then_inc(*act_r.did("row"))
                    act.wait_ge(*pe_t.after(at, "hi_ps"))
                    if at.has(SLOTS):
                        act.wait_ge(*pe_r.after(at.back(SLOTS), f"at{B - 1}"))
                    act.copy(hi_t[at.s][:, :, :], hi_ps[:, :, :]).then_inc(*act_r.did("hi_t"))
                batches(act, g.turns, (early, 0))

            @block.vector
            def _(dve):
                def pairs(at):
                    dve.wait_ge(*pe_t.after(at, "same_ps"))
                    if at.has(SLOTS):
                        dve.wait_ge(*pe_r.after(at.back(SLOTS), f"at{B - 1}"))
                    dve.tensor_tensor(pairs16[at.s][:, :, :], same_ps[:, :, :],
                                      g.before[:, :].unsqueeze(1).to_broadcast([P, B, P]),
                                      ALU.mult).then_inc(*dve_p.did("pairs"))

                def places(at):
                    if at.has(SLOTS):
                        dve.wait_ge(*stored.after(at.back(SLOTS)))
                    for j in range(B):
                        dve.wait_ge(*pe_r.after(at, f"more{j}"))
                        if j:
                            dve.wait_ge(*dve_r.after(at, f"free{j - 1}"))
                            dve.wait_ge(*pe_r.after(at, f"at{j - 1}"))
                        elif at.has(1):
                            dve.wait_ge(*dve_r.after(at.back(1), f"free{B - 1}"))
                            dve.wait_ge(*pe_r.after(at.back(1), f"at{B - 1}"))
                        dve.tensor_tensor(free[(j + 1) % 2][:, :], more_ps[j % 2][:, :], free[j % 2][:, :],
                                          ALU.add).then_inc(*dve_r.did(f"free{j}"))
                        dve.wait_ge(*pe_r.after(at, f"at{j}"))
                        if j:
                            dve.wait_ge(*dve_r.after(at, f"place{j - 1}"))
                        dve.tensor_tensor_reduce(out=junk[:, :], in0=at_ps[j % 2][:, :], in1=one_lo[at.s][:, j, :],
                                                 scale=1.0, scalar=0.0, op0=ALU.mult, op1=ALU.add,
                                                 accum_out=place[at.s][:, j:j + 1]).then_inc(*dve_r.did(f"place{j}"))
                    dve.wait_ge(*dve_r.after(at, f"place{B - 1}"))
                    dve.tensor_copy(place_i[at.s][:, :], place[at.s][:, :]).then_inc(*dve_r.did("place_i"))
                batches(dve, g.turns, (one_hots(dve, act_r, dve_a, lambda at: pe_r.after(at, f"at{B - 1}")), 0),
                        (pairs, 0), (places, 1))

            @block.tensor
            def _(pe):
                def turn(at):
                    pe.wait_ge(*dve_a.after(at, "one_hots"))
                    if at.has(1):
                        pe.wait_ge(*act_r.after(at.back(1), "hi_t"))
                    for j in range(B):
                        last = pe.transpose(hi_ps[:, j, :], one_hi[at.s][:, j, :], ident16[:, :])
                    last.then_inc(*pe_t.did("hi_ps"))
                    pe.wait_ge(*act_r.after(at, "hi_t"))
                    if at.has(1):
                        pe.wait_ge(*dve_p.after(at.back(1), "pairs"))
                    for j in range(B):
                        last = pe.matmul(same_ps[:, j, :], hi_t[at.s][:, j, :], hi_t[at.s][:, j, :], start=True, stop=True)
                    last.then_inc(*pe_t.did("same_ps"))

                def lookup(at):
                    pe.wait_ge(*dve_p.after(at, "pairs"))
                    for j in range(B):
                        if j >= 2:
                            pe.wait_ge(*dve_r.after(at, f"free{j - 2}"))
                        elif at.has(1):
                            pe.wait_ge(*dve_r.after(at.back(1), f"free{j + B - 2}"))
                        pe.matmul(more_ps[j % 2][:, :], one_hi[at.s][:, j, :], one_lo[at.s][:, j, :],
                                  start=True, stop=True).then_inc(*pe_r.did(f"more{j}"))
                        if j:
                            pe.wait_ge(*dve_r.after(at, f"free{j - 1}"))
                        elif at.has(1):
                            pe.wait_ge(*dve_r.after(at.back(1), f"free{B - 1}"))
                        if j >= 2:
                            pe.wait_ge(*dve_r.after(at, f"place{j - 2}"))
                        elif at.has(1):
                            pe.wait_ge(*dve_r.after(at.back(1), f"place{j + B - 2}"))
                        pe.matmul(at_ps[j % 2][:, :], hi_t[at.s][:, j, :], free[j % 2][:, :], start=True, stop=False)
                        pe.matmul(at_ps[j % 2][:, :], pairs16[at.s][:, j, :], one_lo[at.s][:, j, :],
                                  start=False, stop=True).then_inc(*pe_r.did(f"at{j}"))
                batches(pe, g.turns, (turn, 0), (lookup, 1))

            @block.gpsimd
            def _(pool):
                def scatter(at):
                    pool.wait_ge(*act_r.after(at, "row"))
                    pool.wait_ge(*dve_r.after(at, "place_i"))
                    pool.sem_inc(gate, 1)
                    for j in range(B):
                        pool.indirect_dma_start(
                            out=records[:, :], out_offset=bass.IndirectOffsetOnAxis(ap=place_i[at.s][:, j:j + 1], axis=0),
                            in_=row[at.s][:, j, :], in_offset=None).then_inc(*stored.did(at))
                batches(pool, g.turns, (scatter, 0))
                stored.all_of(pool, g.turns)


def read_order(nc, g, records):
    T = g.T
    with Pass(nc, "order") as w:
        loaded, chain, ready, spread = (w.sem(n) for n in ("loaded", "chain", "ready", "spread"))
        spare, other = w.sb("spare", [P, T]), w.sb("other", [P, T])
        place_i = w.sb("place_i", [P, 1], I32)
        place = w.sb("place", [P, 1])
        number = w.sb("number", [P, 1])
        diag = [w.sb(f"diag{k}", [P, P]) for k in range(2)]
        mask = w.sb("mask", [P, P])
        after = w.sb("after", [P, P])
        first_ps, last_ps = w.ps("first_ps", [P, P]), w.ps("last_ps", [P, P])
        with nc.Block() as block:

            @block.sync
            def _(sp):
                sp.dma_start(g.record[:, :, :], columns_of(records, T)).then_inc(loaded, 16)

            @block.gpsimd
            def _(pool):
                pool.iota(place_i[:, :], pattern=[[1, 1]], base=-1, channel_multiplier=T).then_inc(ready, 1)
                pool.affine_select(out=after[:, :], in_=g.ones[:, :], pattern=[[-1, P]], compare_op=ALU.is_gt,
                                   fill=0.0, base=0, channel_multiplier=1).then_inc(ready, 1)

            @block.tensor
            def _(pe):
                pe.wait_ge(spread, 1)
                pe.matmul(first_ps[:, :], g.ones[:, :], diag[0][:, :], start=True, stop=True)
                pe.matmul(last_ps[:, :], g.ones[:, :], diag[1][:, :], start=True, stop=True).then_inc(spread, 1)

            @block.vector
            def _(dve):
                n = 0

                def then(ins):
                    nonlocal n
                    n += 1
                    ins.then_inc(chain, 1)
                    dve.wait_ge(chain, n)

                dve.wait_ge(loaded, 16)
                dve.wait_ge(ready, 2)
                target = g.record[:, :, DST]
                first, last = g.record[:, 0, DST:DST + 1], g.record[:, T - 1, DST:DST + 1]
                then(dve.tensor_copy(g.src[:, :], g.record[:, :, SRC]))
                then(dve.tensor_copy(g.dst[:, :], target))
                then(dve.tensor_copy(g.edge[:, :], g.record[:, :, EDGE]))
                then(dve.memset(g.record[:, 0, SAME:SAME + 1], 0.0))
                then(dve.tensor_tensor(g.record[:, 1:T, SAME], g.record[:, 1:T, DST], g.record[:, 0:T - 1, DST],
                                       ALU.is_equal))
                then(dve.tensor_scalar(g.far_flag[:, :], g.record[:, :, SAME], 1.0, FAR, ALU.subtract, ALU.mult))
                then(dve.tensor_copy(g.far_flag_back[:, 0:T - 1], g.far_flag[:, 1:T]))
                then(dve.memset(g.far_flag_back[:, T - 1:T], -FAR))
                then(dve.tensor_scalar(spare[:, :], target, first, None, ALU.is_equal))
                then(dve.tensor_scalar(other[:, :], target, last, None, ALU.is_equal))
                then(dve.tensor_reduce(number[:, :], spare[:, :], AX.X, ALU.add))
                then(dve.tensor_scalar(g.in_first[:, :], spare[:, :], 1.0, FAR, ALU.subtract, ALU.mult))
                then(dve.tensor_scalar(g.in_last[:, :], other[:, :], 1.0, FAR, ALU.subtract, ALU.mult))
                then(dve.tensor_copy(place[:, :], place_i[:, :]))
                then(dve.tensor_tensor(g.first_end[:, :], place[:, :], number[:, :], ALU.add))
                then(dve.tensor_scalar(diag[0][:, :], g.ident[:, :], first, None, ALU.mult))
                dve.tensor_scalar(diag[1][:, :], g.ident[:, :], last, None, ALU.mult).then_inc(spread, 1)
                dve.wait_ge(spread, 2)
                then(dve.scalar_tensor_tensor(g.carries[:, :], first_ps[:, :], last, g.before[:, :],
                                              ALU.is_equal, ALU.mult))
                then(dve.scalar_tensor_tensor(mask[:, :], last_ps[:, :], first, after[:, :], ALU.is_equal, ALU.mult))
                then(dve.tensor_scalar(g.far_before[:, :], mask[:, :], 1.0, FAR, ALU.subtract, ALU.mult))
                then(dve.scalar_tensor_tensor(mask[:, :], first_ps[:, :], last, g.before[:, :], ALU.is_equal, ALU.mult))
                then(dve.tensor_scalar(g.far_after[:, :], mask[:, :], 1.0, FAR, ALU.subtract, ALU.mult))


def gatherer(pool, w, g, gate, gathered, free_after, *sources):
    copied = w.steps("numbers", *[f"numbers{k}" for k in range(len(sources))])
    numbers = [w.slots(f"numbers{k}_", [P, B], I32) for k in range(len(sources))]

    def stage(at):
        if at.has(SLOTS):
            pool.wait_ge(*gathered.after(at.back(SLOTS)))
            for wait in free_after(at.back(SLOTS)):
                pool.wait_ge(*wait)
            pool.sem_inc(gate, 1)
        for k, (_, rows, _, _, _) in enumerate(sources):
            pool.tensor_copy(numbers[k][at.s][:, :], rows[:, at.columns()]).then_inc(*copied.did(f"numbers{k}"))
        pool.wait_ge(*copied.after(at, f"numbers{len(sources) - 1}"))
        pool.sem_inc(gate, 1)
        for j in range(B):
            for k, (table, _, slots, a, b) in enumerate(sources):
                pool.indirect_dma_start(
                    out=slots[at.s][:, j, a:b], out_offset=None, in_=table[:, :],
                    in_offset=bass.IndirectOffsetOnAxis(ap=numbers[k][at.s][:, j:j + 1], axis=0),
                ).then_inc(*gathered.did(at))
    return stage


def record_copier(act, g, fields, copied, free_after):

    def stage(at):
        if at.has(SLOTS):
            act.wait_ge(*free_after(at.back(SLOTS)))
        act.copy(fields[at.s][:, :, :], g.record[:, at.columns(), :]).then_inc(*copied.did("record"))
    return stage


def running_sums(dve, at, sums, fields, message, did, after):
    for j in range(B):
        if j:
            before = sums[at.s][:, j - 1, :]
            dve.wait_ge(*after(at, f"sum{j - 1}"))
        else:
            before = sums[at.s - 1][:, B - 1, :]
            if at.has(1):
                dve.wait_ge(*after(at.back(1), f"sum{B - 1}"))
        dve.scalar_tensor_tensor(sums[at.s][:, j, :], before, fields[at.s][:, j, SAME:SAME + 1], message(j),
                                 ALU.mult, ALU.add).then_inc(*did(f"sum{j}"))


SUMS = tuple(f"sum{j}" for j in range(B))


def carry_over(nc, w, g, tail, sums_table, width):
    carry_ps = w.ps("carry_ps", [P, width])
    fixed = w.sb("fixed", [P, width])
    summed, got, fix, put = (w.sem(n) for n in ("summed", "got", "fix", "put"))
    with nc.Block() as block:

        @block.tensor
        def _(pe):
            pe.matmul(carry_ps[:, :], g.carries[:, :], tail, start=True, stop=True).then_inc(summed, 1)

        @block.gpsimd
        def _(pool):
            pool.indirect_dma_start(out=fixed[:, :], out_offset=None, in_=sums_table[:, :],
                                    in_offset=bass.IndirectOffsetOnAxis(ap=g.first_end[:, :], axis=0)).then_inc(got, 16)
            pool.wait_ge(fix, 1)
            pool.indirect_dma_start(out=sums_table[:, :],
                                    out_offset=bass.IndirectOffsetOnAxis(ap=g.first_end[:, :], axis=0),
                                    in_=fixed[:, :], in_offset=None).then_inc(put, 16)
            pool.wait_ge(put, 16)

        @block.vector
        def _(dve):
            dve.wait_ge(got, 16)
            dve.wait_ge(summed, 1)
            dve.tensor_tensor(fixed[:, :], carry_ps[:, :], fixed[:, :], ALU.add).then_inc(fix, 1)


def clear_row(nc, w, g, table, width):
    zero = w.sb("zero", [1, width])
    set_, stored = w.sem("zero_set"), w.sem("zero_stored")
    with nc.Block() as block:

        @block.vector
        def _(dve):
            dve.memset(zero[:, :], 0.0).then_inc(set_, 1)

        @block.sync
        def _(sp):
            sp.wait_ge(set_, 1)
            sp.dma_start(table[P * g.T:P * g.T + 1, :], zero[:, :]).then_inc(stored, 16)
            sp.wait_ge(stored, 16)


def relational_sums(nc, name, g, table, weights, sums_table):
    T, half = g.T, RELATIONS // 2
    with Pass(nc, name) as w:
        clear_row(nc, w, g, sums_table, D)
        wide = w.sb("weights", [P, RELATIONS, D])
        rows, rows_t = w.slots("rows", [P, B, D]), w.slots("rows_t", [P, B, D])
        fields, sums = w.slots("fields", [P, B, FIELDS]), w.slots("sums", [P, B, D])
        parts = w.sb("parts", [P, 2, D])
        messages = w.slots("messages", [P, B, D])
        t_ps = [w.ps(f"t_ps{s}", [P, B, D]) for s in range(2)]
        y_ps = [[w.ps(f"y_ps{h}{k}", [P, half, D]) for k in range(2)] for h in range(2)]
        loaded, cleared, gate = w.sem("loaded"), w.sem("cleared"), w.sem("gate")
        gathered, stored = w.moves("gathered", B), w.moves("stored", 1)
        act_s = w.steps("act", "record")
        act_t = w.steps("act_t", "rows_t")
        pe_t = w.steps("pe_t", "t_ps")
        pe_y = w.steps("pe_y", *[f"y{c}{h}" for c in (0, 2) for h in range(2)])
        names = []
        for c in (0, 2):
            for h in range(2):
                names += [f"part{c + k}_{h * half + r}" for r in range(half) for k in range(2)]
        dve_m = w.steps("dve_m", *names)
        dve_s = w.steps("dve_s", *SUMS)
        with nc.Block() as block:

            @block.sync
            def _(sp):
                sp.dma_start(wide[:, :, :], weights.rearrange("r k f -> k r f")).then_inc(loaded, 16)

                def store(at):
                    sp.wait_ge(*dve_s.after(at, SUMS[-1]))
                    sp.dma_start(columns_of(sums_table, T)[:, at.columns(), :], sums[at.s][:, :, :]).then_inc(*stored.did(at))
                batches(sp, g.turns, (store, 0))
                stored.all_of(sp, g.turns)

            @block.gpsimd
            def _(pool):
                batches(pool, g.turns, (gatherer(pool, w, g, gate, gathered, lambda at: [pe_t.after(at, "t_ps")],
                                                 (table, g.src, rows, 0, D)), 0))

            @block.tensor
            def _(pe):
                def turn(at):
                    pe.wait_ge(*gathered.after(at))
                    if at.has(2):
                        pe.wait_ge(*act_t.after(at.back(2), "rows_t"))
                    for j in range(B):
                        last = pe.transpose(t_ps[at.s % 2][:, j, :], rows[at.s][:, j, :], g.ident[:, :])
                    last.then_inc(*pe_t.did("t_ps"))

                def products(at):
                    pe.wait_ge(loaded, 16)
                    pe.wait_ge(*act_t.after(at, "rows_t"))
                    for c in (0, 2):
                        for h in range(2):
                            done = f"part{(c + 2) % 4 + 1}_{h * half + half - 1}"
                            if c:
                                pe.wait_ge(*dve_m.after(at, done))
                            elif at.has(1):
                                pe.wait_ge(*dve_m.after(at.back(1), done))
                            for k in range(2):
                                last = pe.matmul(y_ps[h][k][:, :, :], rows_t[at.s][:, c + k, :],
                                                 wide[:, h * half:(h + 1) * half, :], start=True, stop=True)
                            last.then_inc(*pe_y.did(f"y{c}{h}"))
                batches(pe, g.turns, (turn, 0), (products, 1))

            @block.scalar
            def _(act):
                def transposed(at):
                    act.wait_ge(*pe_t.after(at, "t_ps"))
                    if at.has(SLOTS):
                        act.wait_ge(*pe_y.after(at.back(SLOTS), "y21"))
                    act.copy(rows_t[at.s][:, :, :], t_ps[at.s % 2][:, :, :]).then_inc(*act_t.did("rows_t"))
                batches(act, g.turns, (record_copier(act, g, fields, act_s, lambda at: dve_s.after(at, SUMS[-1])), 0),
                        (transposed, 0))

            @block.vector
            def _(dve):
                dve.memset(sums[SLOTS - 1][:, B - 1, :], 0.0).then_inc(cleared, 1)
                dve.wait_ge(cleared, 1)

                def stage(at):
                    dve.wait_ge(*act_s.after(at, "record"))
                    before = None
                    for c in (0, 2):
                        for h in range(2):
                            dve.wait_ge(*pe_y.after(at, f"y{c}{h}"))
                            for r in range(half):
                                for k in range(2):
                                    rel, j = h * half + r, c + k
                                    scale = fields[at.s][:, j, REL + rel:REL + rel + 1]
                                    out = messages[at.s][:, j, :]
                                    did = dve_m.did(f"part{j}_{rel}")
                                    if rel == 0:
                                        if at.has(SLOTS):
                                            dve.wait_ge(*dve_s.after(at.back(SLOTS), SUMS[j]))
                                        dve.tensor_scalar(out, y_ps[h][k][:, r, :], scale, None, ALU.mult).then_inc(*did)
                                    else:
                                        dve.wait_ge(*dve_m.after(at, f"part{j}_{rel - 1}"))
                                        dve.scalar_tensor_tensor(out, y_ps[h][k][:, r, :], scale, out,
                                                                 ALU.mult, ALU.add).then_inc(*did)
                    if at.has(SLOTS):
                        dve.wait_ge(*stored.after(at.back(SLOTS)))
                    dve.wait_ge(*dve_m.after(at, f"part{B - 1}_{RELATIONS - 1}"))
                    running_sums(dve, at, sums, fields, lambda j: messages[at.s][:, j, :], dve_s.did, dve_s.after)
                batches(dve, g.turns, (stage, 0))
        carry_over(nc, w, g, sums[SLOTS - 1][:, B - 1, :], sums_table, D)


def row_sums(nc, name, g, sources, width, sums_table, product=None):
    T = g.T
    with Pass(nc, name) as w:
        clear_row(nc, w, g, sums_table, width)
        got_width = max(b for _, _, _, b in sources)
        rows = w.slots("rows", [P, B, got_width])
        messages = w.slots("messages", [P, B, width]) if product else rows
        fields, sums = w.slots("fields", [P, B, FIELDS]), w.slots("sums", [P, B, width])
        cleared, gate = w.sem("cleared"), w.sem("gate")
        gathered, stored = w.moves("gathered", B * len(sources)), w.moves("stored", 1)
        act_s = w.steps("act", "record")
        dve_s = w.steps("dve_s", *SUMS)
        dve_m = w.steps("dve_m", "message")
        with nc.Block() as block:

            @block.sync
            def _(sp):
                def store(at):
                    sp.wait_ge(*dve_s.after(at, SUMS[-1]))
                    sp.dma_start(columns_of(sums_table, T)[:, at.columns(), :], sums[at.s][:, :, :]).then_inc(*stored.did(at))
                batches(sp, g.turns, (store, 0))
                stored.all_of(sp, g.turns)

            @block.gpsimd
            def _(pool):
                batches(pool, g.turns, (gatherer(
                    pool, w, g, gate, gathered,
                    lambda at: [dve_m.after(at, "message") if product else dve_s.after(at, SUMS[-1])],
                    *[(table, numbers, rows, a, b) for table, numbers, a, b in sources]), 0))

            @block.scalar
            def _(act):
                batches(act, g.turns, (record_copier(act, g, fields, act_s, lambda at: dve_s.after(at, SUMS[-1])), 0))

            @block.vector
            def _(dve):
                dve.memset(sums[SLOTS - 1][:, B - 1, :], 0.0).then_inc(cleared, 1)
                dve.wait_ge(cleared, 1)

                def stage(at):
                    dve.wait_ge(*act_s.after(at, "record"))
                    dve.wait_ge(*gathered.after(at))
                    if product:
                        if at.has(SLOTS):
                            dve.wait_ge(*dve_s.after(at.back(SLOTS), SUMS[-1]))
                        product(dve, at, rows[at.s], fields[at.s], messages[at.s]).then_inc(*dve_m.did("message"))
                        dve.wait_ge(*dve_m.after(at, "message"))
                    if at.has(SLOTS):
                        dve.wait_ge(*stored.after(at.back(SLOTS)))
                    running_sums(dve, at, sums, fields, lambda j: messages[at.s][:, j, :], dve_s.did, dve_s.after)
                batches(dve, g.turns, (stage, 0))
        carry_over(nc, w, g, sums[SLOTS - 1][:, B - 1, :], sums_table, width)


def attended_message(g):

    def product(dve, at, rows, fields, message):
        share = g.attention[:, at.columns(), :]
        dve.tensor_tensor(message[:, :, 0:D].rearrange("p b (h d) -> p b h d", h=HEADS),
                          rows[:, :, :].rearrange("p b (h d) -> p b h d", h=HEADS),
                          share.unsqueeze(3).to_broadcast([P, B, HEADS, HEAD_DIM]), ALU.mult)
        dve.tensor_copy(message[:, :, D:D + HEADS], share)
        return dve.tensor_copy(message[:, :, D + HEADS:D + HEADS + 1], fields[:, :, WEIGHT:WEIGHT + 1])
    return product


def weighted_message(dve, at, rows, fields, message):
    for j in range(B):
        last = dve.tensor_scalar(message[:, j, :], rows[:, j, :], fields[:, j, WEIGHT:WEIGHT + 1], None, ALU.mult)
    return last


def edge_scores(nc, g, queries, keys):
    with Pass(nc, "scores") as w:
        q, k = w.slots("q", [P, B, D]), w.slots("k", [P, B, D])
        both = w.slots("both", [P, B, D])
        gate, gathered = w.sem("gate"), w.moves("gathered", 2 * B)
        dve_s = w.steps("dve", "product", "score")
        with nc.Block() as block:

            @block.gpsimd
            def _(pool):
                batches(pool, g.turns, (gatherer(pool, w, g, gate, gathered, lambda at: [dve_s.after(at, "product")],
                                                 (queries, g.dst, q, 0, D), (keys, g.src, k, 0, D)), 0))

            @block.vector
            def _(dve):
                def multiply(at):
                    dve.wait_ge(*gathered.after(at))
                    if at.has(1):
                        dve.wait_ge(*dve_s.after(at.back(1), "score"))
                    dve.tensor_tensor(both[at.s][:, :, :], q[at.s][:, :, :], k[at.s][:, :, :],
                                      ALU.mult).then_inc(*dve_s.did("product"))
                    dve.wait_ge(*dve_s.after(at, "product"))
                    dve.tensor_reduce(g.attention[:, at.columns(), :].rearrange("p b h -> p (b h)"),
                                      both[at.s][:, :, :].rearrange("p b (h d) -> p (b h) d", h=HEADS),
                                      AX.X, ALU.add).then_inc(*dve_s.did("score"))
                batches(dve, g.turns, (multiply, 0))


def softmax_weights(nc, g, edge_bias):
    T = g.T
    with Pass(nc, "softmax") as w:
        bias = w.sb("bias", [P, HEADS, HEADS])
        is_type = w.sb("is_type", [P, T])
        forth, back = w.sb("forth", [P, T]), w.sb("back", [P, T])
        diag, seen = w.sb("diag", [P, P]), w.sb("seen", [P, P])
        carry = w.sb("carry", [P, 1])
        loaded, chain, spread, ready = (w.sem(n) for n in ("loaded", "chain", "spread", "ready"))
        tails_ps = w.ps("tails_ps", [P, P])
        with nc.Block() as block:

            @block.sync
            def _(sp):
                sp.dma_start(bias[:, :, :], edge_bias.partition_broadcast(P)).then_inc(loaded, 16)

            @block.tensor
            def _(pe):
                for n in range(2 * HEADS):
                    pe.wait_ge(ready, n + 1)
                    pe.matmul(tails_ps[:, :], g.ones[:, :], diag[:, :], start=True, stop=True).then_inc(spread, 1)

            @block.vector
            def _(dve):
                n = 0

                def then(ins):
                    nonlocal n
                    n += 1
                    ins.then_inc(chain, 1)
                    dve.wait_ge(chain, n)

                dve.wait_ge(loaded, 16)
                then(dve.tensor_scalar(g.attention[:, :, :], g.attention[:, :, :], HEAD_DIM ** -0.5, None, ALU.mult))
                for kind in range(8):
                    then(dve.tensor_scalar(is_type[:, :], g.record[:, :, TYPE], float(kind), None, ALU.is_equal))
                    for h in range(HEADS):
                        score = g.attention[:, :, h]
                        then(dve.scalar_tensor_tensor(score, is_type[:, :], bias[:, kind, h:h + 1], score,
                                                      ALU.mult, ALU.add))
                seen_tails = 0
                for h in range(HEADS):
                    score = g.attention[:, :, h]
                    then(dve.tensor_tensor_scan(forth[:, :], g.far_flag[:, :], score, -FAR, ALU.add, ALU.max))
                    then(dve.tensor_tensor_scan(back[:, ::-1], g.far_flag_back[:, ::-1], score[:, ::-1], -FAR,
                                                ALU.add, ALU.max))
                    for largest, end, far, where in ((forth, T - 1, g.far_before, g.in_first),
                                                     (back, 0, g.far_after, g.in_last)):
                        dve.tensor_scalar(diag[:, :], g.ident[:, :], largest[:, end:end + 1], None,
                                          ALU.mult).then_inc(ready, 1)
                        seen_tails += 1
                        dve.wait_ge(spread, seen_tails)
                        then(dve.tensor_tensor(seen[:, :], tails_ps[:, :], far[:, :], ALU.add))
                        then(dve.tensor_reduce(carry[:, :], seen[:, :], AX.X, ALU.max))
                        then(dve.scalar_tensor_tensor(largest[:, :], where[:, :], carry[:, 0:1], largest[:, :],
                                                      ALU.add, ALU.max))
                    then(dve.tensor_tensor(forth[:, :], forth[:, :], back[:, :], ALU.max))
                    then(dve.tensor_tensor(score, score, forth[:, :], ALU.subtract))
                dve.wait_ge(chain, n)
                dve.sem_inc(ready, 1)

            @block.scalar
            def _(act):
                act.wait_ge(ready, 2 * HEADS + 1)
                act.activation(g.attention[:, :, :], g.attention[:, :, :], ACT.Exp).then_inc(spread, 1)
                act.wait_ge(spread, 2 * HEADS + 1)


class Norm:

    def __init__(self, w, name):
        self.stats = w.slots(f"{name}_stats", [P, B, 6])
        self.moments = w.slots(f"{name}_moments", [P, B, 2])
        self.variance = w.slots(f"{name}_variance", [P, B])
        self.scale = w.slots(f"{name}_scale", [P, B])
        self.shift = w.slots(f"{name}_shift", [P, B])
        self.minus_half = w.sb(f"{name}_minus_half", [P, B])
        self.gate, self.set = w.sem(f"{name}_gate"), w.sem(f"{name}_set")
        self.measured = w.steps(f"{name}_measured", "stats", "moments", "variance")
        self.rooted = w.steps(f"{name}_rooted", "scale")
        self.shifted = w.steps(f"{name}_shifted", "shift")

    def prepare(self, dve):
        dve.memset(self.minus_half[:, :], -0.5).then_inc(self.set, 1)

    def take_moments(self, dve, at, rows):
        for j in range(B):
            last = dve.bn_stats(self.stats[at.s][:, j, :], rows[:, j, :])
        last.then_inc(*self.measured.did("stats"))
        dve.wait_ge(*self.measured.after(at, "stats"))
        dve.sem_inc(self.gate, 1)
        for j in range(B):
            last = dve.bn_aggr(self.moments[at.s][:, j, :], self.stats[at.s][:, j, :])
        last.then_inc(*self.measured.did("moments"))
        dve.wait_ge(*self.measured.after(at, "moments"))
        if at.has(SLOTS):
            dve.wait_ge(*self.rooted.after(at.back(SLOTS), "scale"))
        dve.tensor_scalar(self.variance[at.s][:, :], self.moments[at.s][:, :, 1], EPS, None,
                          ALU.add).then_inc(*self.measured.did("variance"))

    def root(self, pool, at, scale_used):
        if at.has(SLOTS):
            pool.wait_ge(*scale_used(at.back(SLOTS)))
        else:
            pool.wait_ge(self.set, 1)
        pool.wait_ge(*self.measured.after(at, "variance"))
        pool.tensor_tensor(self.scale[at.s][:, :], self.variance[at.s][:, :], self.minus_half[:, :],
                           ALU.pow).then_inc(*self.rooted.did("scale"))

    def make_shift(self, dve, at, shift_used):
        dve.wait_ge(*self.rooted.after(at, "scale"))
        if at.has(SLOTS):
            dve.wait_ge(*shift_used(at.back(SLOTS)))
        dve.scalar_tensor_tensor(self.shift[at.s][:, :], self.moments[at.s][:, :, 0], -1.0, self.scale[at.s][:, :],
                                 ALU.mult, ALU.mult).then_inc(*self.shifted.did("shift"))

    def relu(self, act, at, out, rows):
        act.wait_ge(*self.shifted.after(at, "shift"))
        for j in range(B):
            last = act.activation(out[:, j, :], rows[:, j, :], ACT.Relu, bias=self.shift[at.s][:, j:j + 1],
                                  scale=self.scale[at.s][:, j:j + 1])
        return last


class Affine:

    def __init__(self, w, name, norm, gain, offset):
        self.norm, self.source = norm, (gain, offset)
        self.gain, self.offset = w.sb(f"{name}_gain", [P, D]), w.sb(f"{name}_offset", [P, D])
        self.loaded = w.sem(f"{name}_loaded")
        self.steps = w.steps(name, "scaled", "gained", "offset")

    def load(self, sp):
        for out, vector in zip((self.gain, self.offset), self.source):
            sp.dma_start(out[:, :], vector.partition_broadcast(P)).then_inc(self.loaded, 16)

    def apply(self, dve, at, out, rows):
        dve.wait_ge(*self.norm.rooted.after(at, "scale"))
        for j in range(B):
            last = dve.tensor_scalar(out[:, j, :], rows[:, j, :], self.norm.moments[at.s][:, j, 0:1],
                                     self.norm.scale[at.s][:, j:j + 1], ALU.subtract, ALU.mult)
        last.then_inc(*self.steps.did("scaled"))
        dve.wait_ge(*self.steps.after(at, "scaled"))
        dve.tensor_tensor(out[:, :, :], out[:, :, :], over_batch(self.gain), ALU.mult).then_inc(*self.steps.did("gained"))
        dve.wait_ge(*self.steps.after(at, "gained"))
        dve.tensor_tensor(out[:, :, :], out[:, :, :], over_batch(self.offset), ALU.add).then_inc(*self.steps.did("offset"))


def over_batch(vector):
    return vector[:, :].unsqueeze(1).to_broadcast([P, B, vector.shape[-1]])


def transpose_rows(pe, g, out, rows, width=D):
    for j in range(B):
        last = pe.transpose(out[:, j, :], rows[:, j, :], g.ident[:, :])
    return last


def rows_times(pe, out, rows_t, weight, bias, ones):
    pe.matmul(out[:, :, :], ones[0:1, :], bias[0:1, :, :], start=True, stop=False, skip_group_check=True)
    for j in range(B):
        last = pe.matmul(out[:, j, :], rows_t[:, j, :], weight, start=False, stop=True, skip_group_check=True)
    return last


def batch_bias(sp, out, vector, loaded):
    sp.dma_start(out[0:1, :, :], vector.unsqueeze(0).unsqueeze(0).to_broadcast([1, B, D])).then_inc(loaded, 16)


def embed(nc, g, x, gain, offset, x_plus_h, table):
    T = g.T
    with Pass(nc, "embed") as w:
        rows, h, both = w.slots("rows", [P, B, D]), w.slots("h", [P, B, D]), w.slots("both", [P, B, D])
        out, inner = w.slots("out", [P, B, D]), w.slots("inner", [P, B, D])
        first, second = Norm(w, "first"), Norm(w, "second")
        affine = Affine(w, "affine", second, gain, offset)
        got, stored, stored_out = w.moves("got", 1), w.moves("stored", 1), w.moves("stored_out", 1)
        act_h, act_o = w.steps("act_h", "h"), w.steps("act_o", "out")
        dve_b = w.steps("dve", "both")
        with nc.Block() as block:

            @block.sync
            def _(sp):
                affine.load(sp)

                def load(at):
                    if at.has(SLOTS):
                        sp.wait_ge(*dve_b.after(at.back(SLOTS), "both"))
                    sp.dma_start(rows[at.s][:, :, :], columns_of(x, T)[:, at.columns(), :]).then_inc(*got.did(at))

                def store_both(at):
                    sp.wait_ge(*dve_b.after(at, "both"))
                    sp.dma_start(columns_of(x_plus_h, T)[:, at.columns(), :], both[at.s][:, :, :]).then_inc(*stored.did(at))

                def store_out(at):
                    sp.wait_ge(*act_o.after(at, "out"))
                    sp.dma_start(columns_of(table, T)[:, at.columns(), :], out[at.s][:, :, :]).then_inc(*stored_out.did(at))
                batches(sp, g.turns, (load, 0), (store_both, 3), (store_out, 4))
                stored.all_of(sp, g.turns)
                stored_out.all_of(sp, g.turns)

            @block.gpsimd
            def _(pool):
                batches(pool, g.turns, (lambda at: second.root(pool, at, lambda a: affine.steps.after(a, "scaled")), 2),
                        (lambda at: first.root(pool, at, lambda a: act_h.after(a, "h")), 0))

            @block.vector
            def _(dve):
                first.prepare(dve)
                second.prepare(dve)
                dve.wait_ge(affine.loaded, 2 * 16)

                def moments(at):
                    dve.wait_ge(*got.after(at))
                    first.take_moments(dve, at, rows[at.s])

                def shift(at):
                    first.make_shift(dve, at, lambda a: act_h.after(a, "h"))

                def add(at):
                    dve.wait_ge(*act_h.after(at, "h"))
                    if at.has(SLOTS):
                        dve.wait_ge(*stored.after(at.back(SLOTS)))
                    dve.tensor_tensor(both[at.s][:, :, :], rows[at.s][:, :, :], h[at.s][:, :, :],
                                      ALU.add).then_inc(*dve_b.did("both"))
                    second.take_moments(dve, at, h[at.s])

                def apply(at):
                    if at.has(SLOTS):
                        dve.wait_ge(*act_o.after(at.back(SLOTS), "out"))
                    affine.apply(dve, at, inner[at.s], h[at.s])
                batches(dve, g.turns, (apply, 3), (add, 2), (shift, 1), (moments, 0))

            @block.scalar
            def _(act):
                def relu(at):
                    if at.has(SLOTS):
                        act.wait_ge(*affine.steps.after(at.back(SLOTS), "scaled"))
                        act.wait_ge(*second.measured.after(at.back(SLOTS), "stats"))
                    first.relu(act, at, h[at.s], rows[at.s]).then_inc(*act_h.did("h"))

                def gelu(at):
                    act.wait_ge(*affine.steps.after(at, "offset"))
                    if at.has(SLOTS):
                        act.wait_ge(*stored_out.after(at.back(SLOTS)))
                    act.activation(out[at.s][:, :, :], inner[at.s][:, :, :], ACT.Gelu).then_inc(*act_o.did("out"))
                batches(act, g.turns, (gelu, 3), (relu, 1))


def between(nc, g, sums_table, table, root, bias, gain, offset, out_table):
    T = g.T
    with Pass(nc, "between") as w:
        weight, bias_row = w.sb("root", [P, D]), w.sb("bias", [1, B, D])
        sums, rows, rows_t = (w.slots(n, [P, B, D]) for n in ("sums", "rows", "rows_t"))
        conv, inner, out = (w.slots(n, [P, B, D]) for n in ("conv", "inner", "out"))
        t_ps = [w.ps(f"t_ps{k}", [P, B, D]) for k in range(2)]
        root_ps = [w.ps(f"root_ps{k}", [P, B, D]) for k in range(2)]
        norm = Norm(w, "norm")
        affine = Affine(w, "affine", norm, gain, offset)
        got, stored, gathered = w.moves("got", 1), w.moves("stored", 1), w.moves("gathered", B)
        loaded, gate = w.sem("loaded"), w.sem("gate")
        pe_s = w.steps("pe_t", "t_ps")
        pe_r = w.steps("pe_r", "root_ps")
        act_t, act_o = w.steps("act_t", "rows_t"), w.steps("act_o", "out")
        dve_c = w.steps("dve", "conv")
        with nc.Block() as block:

            @block.sync
            def _(sp):
                affine.load(sp)
                sp.dma_start(weight[:, :], root).then_inc(loaded, 16)
                batch_bias(sp, bias_row, bias, loaded)

                def load(at):
                    if at.has(SLOTS):
                        sp.wait_ge(*pe_s.after(at.back(SLOTS), "t_ps"))
                    sp.dma_start(rows[at.s][:, :, :], columns_of(table, T)[:, at.columns(), :]).then_inc(*got.did(at))

                def store(at):
                    sp.wait_ge(*act_o.after(at, "out"))
                    sp.dma_start(columns_of(out_table, T)[:, at.columns(), :], out[at.s][:, :, :]).then_inc(*stored.did(at))
                batches(sp, g.turns, (load, 0), (store, 3))
                stored.all_of(sp, g.turns)

            @block.gpsimd
            def _(pool):
                gather = gatherer(pool, w, g, gate, gathered, lambda at: [dve_c.after(at, "conv")],
                                  (sums_table, g.end, sums, 0, D))
                batches(pool, g.turns, (gather, 0),
                        (lambda at: norm.root(pool, at, lambda a: affine.steps.after(a, "scaled")), 2))

            @block.tensor
            def _(pe):
                def turn(at):
                    pe.wait_ge(*got.after(at))
                    if at.has(2):
                        pe.wait_ge(*act_t.after(at.back(2), "rows_t"))
                    transpose_rows(pe, g, t_ps[at.s % 2], rows[at.s]).then_inc(*pe_s.did("t_ps"))

                def product(at):
                    pe.wait_ge(loaded, 2 * 16)
                    pe.wait_ge(*act_t.after(at, "rows_t"))
                    if at.has(2):
                        pe.wait_ge(*dve_c.after(at.back(2), "conv"))
                    rows_times(pe, root_ps[at.s % 2], rows_t[at.s], weight[:, :], bias_row, g.ones).then_inc(*pe_r.did("root_ps"))
                batches(pe, g.turns, (turn, 0), (product, 1))

            @block.scalar
            def _(act):
                def copy(at):
                    act.wait_ge(*pe_s.after(at, "t_ps"))
                    if at.has(SLOTS):
                        act.wait_ge(*pe_r.after(at.back(SLOTS), "root_ps"))
                    act.copy(rows_t[at.s][:, :, :], t_ps[at.s % 2][:, :, :]).then_inc(*act_t.did("rows_t"))

                def gelu(at):
                    act.wait_ge(*affine.steps.after(at, "offset"))
                    if at.has(SLOTS):
                        act.wait_ge(*stored.after(at.back(SLOTS)))
                    act.activation(out[at.s][:, :, :], inner[at.s][:, :, :], ACT.Gelu).then_inc(*act_o.did("out"))
                batches(act, g.turns, (copy, 0), (gelu, 3))

            @block.vector
            def _(dve):
                norm.prepare(dve)
                dve.wait_ge(affine.loaded, 2 * 16)

                def add(at):
                    dve.wait_ge(*pe_r.after(at, "root_ps"))
                    dve.wait_ge(*gathered.after(at))
                    dve.tensor_tensor(conv[at.s][:, :, :], root_ps[at.s % 2][:, :, :], sums[at.s][:, :, :],
                                      ALU.add).then_inc(*dve_c.did("conv"))
                    dve.wait_ge(*dve_c.after(at, "conv"))
                    norm.take_moments(dve, at, conv[at.s])

                def apply(at):
                    if at.has(SLOTS):
                        dve.wait_ge(*act_o.after(at.back(SLOTS), "out"))
                    affine.apply(dve, at, inner[at.s], conv[at.s])
                batches(dve, g.turns, (apply, 3), (add, 1))


def project(nc, g, sums_table, table, root, bias, x_plus_h, w_qkv, b_qkv, x_table, h_table, q_table, k_table, v_table):
    T = g.T
    with Pass(nc, "project") as w:
        weight, bias_row = w.sb("root", [P, D]), w.sb("bias", [1, B, D])
        wide, wide_bias = w.sb("w_qkv", [P, 3 * D]), w.sb("b_qkv", [P, 3 * D])
        sums, rows, rows_t, old = (w.slots(n, [P, B, D]) for n in ("sums", "rows", "rows_t", "old"))
        new, h, h_t = (w.slots(n, [P, B, D]) for n in ("new", "h", "h_t"))
        qkv = w.slots("qkv", [P, B, 3 * D])
        t_ps, root_ps, h_ps = (w.ps(n, [P, B, D]) for n in ("t_ps", "root_ps", "h_ps"))
        qkv_ps = [w.ps(f"qkv_ps{j}", [P, 3 * D]) for j in range(B)]
        norm = Norm(w, "norm")
        got, gathered = w.moves("got", 2), w.moves("gathered", B)
        stored, stored_h, stored_q = w.moves("stored", 1), w.moves("stored_h", 1), w.moves("stored_q", 3)
        loaded, gate = w.sem("loaded"), w.sem("gate")
        pe_t, pe_r, pe_h = w.steps("pe_t", "t_ps"), w.steps("pe_r", "root_ps"), w.steps("pe_h", "h_ps")
        pe_q = w.steps("pe_q", *[f"qkv_ps{j}" for j in range(B)])
        act_t, act_h, act_ht = w.steps("act_t", "rows_t"), w.steps("act_h", "h"), w.steps("act_ht", "h_t")
        dve_x = w.steps("dve_x", "conv", "new")
        dve_q = w.steps("dve_q", *[f"qkv{j}" for j in range(B)])
        with nc.Block() as block:

            @block.sync
            def _(sp):
                sp.dma_start(weight[:, :], root).then_inc(loaded, 16)
                batch_bias(sp, bias_row, bias, loaded)
                for k in range(3):
                    sp.dma_start(wide[:, k * D:(k + 1) * D], w_qkv[k]).then_inc(loaded, 16)
                    sp.dma_start(wide_bias[:, k * D:(k + 1) * D], b_qkv[k].partition_broadcast(P)).then_inc(loaded, 16)

                def load(at):
                    if at.has(SLOTS):
                        sp.wait_ge(*pe_t.after(at.back(SLOTS), "t_ps"))
                    sp.dma_start(rows[at.s][:, :, :], columns_of(table, T)[:, at.columns(), :]).then_inc(*got.did(at))
                    if at.has(SLOTS):
                        sp.wait_ge(*dve_x.after(at.back(SLOTS), "new"))
                    sp.dma_start(old[at.s][:, :, :], columns_of(x_plus_h, T)[:, at.columns(), :]).then_inc(*got.did(at))

                def store(at):
                    sp.wait_ge(*dve_x.after(at, "new"))
                    sp.dma_start(columns_of(x_table, T)[:, at.columns(), :], new[at.s][:, :, :]).then_inc(*stored.did(at))

                def store_h(at):
                    sp.wait_ge(*act_h.after(at, "h"))
                    sp.dma_start(columns_of(h_table, T)[:, at.columns(), :], h[at.s][:, :, :]).then_inc(*stored_h.did(at))

                def store_q(at):
                    sp.wait_ge(*dve_q.after(at, f"qkv{B - 1}"))
                    for k, out in enumerate((q_table, k_table, v_table)):
                        sp.dma_start(columns_of(out, T)[:, at.columns(), :],
                                     qkv[at.s][:, :, k * D:(k + 1) * D]).then_inc(*stored_q.did(at))
                batches(sp, g.turns, (load, 0), (store, 2), (store_h, 3), (store_q, 4))
                for moves in (stored, stored_h, stored_q):
                    moves.all_of(sp, g.turns)

            @block.gpsimd
            def _(pool):
                gather = gatherer(pool, w, g, gate, gathered, lambda at: [dve_x.after(at, "conv")],
                                  (sums_table, g.end, sums, 0, D))
                batches(pool, g.turns, (gather, 0), (lambda at: norm.root(pool, at, lambda a: act_h.after(a, "h")), 2))

            @block.tensor
            def _(pe):
                def turn(at):
                    pe.wait_ge(*got.after(at))
                    if at.has(1):
                        pe.wait_ge(*act_t.after(at.back(1), "rows_t"))
                    transpose_rows(pe, g, t_ps, rows[at.s]).then_inc(*pe_t.did("t_ps"))

                def product(at):
                    pe.wait_ge(loaded, 8 * 16)
                    pe.wait_ge(*act_t.after(at, "rows_t"))
                    if at.has(1):
                        pe.wait_ge(*dve_x.after(at.back(1), "conv"))
                    rows_times(pe, root_ps, rows_t[at.s], weight[:, :], bias_row, g.ones).then_inc(*pe_r.did("root_ps"))

                def turn_h(at):
                    pe.wait_ge(*act_h.after(at, "h"))
                    if at.has(1):
                        pe.wait_ge(*act_ht.after(at.back(1), "h_t"))
                    transpose_rows(pe, g, h_ps, h[at.s]).then_inc(*pe_h.did("h_ps"))

                def heads(at):
                    pe.wait_ge(*act_ht.after(at, "h_t"))
                    for j in range(B):
                        if at.has(1):
                            pe.wait_ge(*dve_q.after(at.back(1), f"qkv{j}"))
                        pe.matmul(qkv_ps[j][:, :], h_t[at.s][:, j, :], wide[:, :], start=True,
                                  stop=True).then_inc(*pe_q.did(f"qkv_ps{j}"))
                batches(pe, g.turns, (turn, 0), (product, 1), (turn_h, 3), (heads, 4))

            @block.scalar
            def _(act):
                def copy(at):
                    act.wait_ge(*pe_t.after(at, "t_ps"))
                    if at.has(SLOTS):
                        act.wait_ge(*pe_r.after(at.back(SLOTS), "root_ps"))
                    act.copy(rows_t[at.s][:, :, :], t_ps[:, :, :]).then_inc(*act_t.did("rows_t"))

                def relu(at):
                    if at.has(SLOTS):
                        act.wait_ge(*stored_h.after(at.back(SLOTS)))
                        act.wait_ge(*pe_h.after(at.back(SLOTS), "h_ps"))
                    norm.relu(act, at, h[at.s], new[at.s]).then_inc(*act_h.did("h"))

                def copy_h(at):
                    act.wait_ge(*pe_h.after(at, "h_ps"))
                    if at.has(SLOTS):
                        act.wait_ge(*pe_q.after(at.back(SLOTS), f"qkv_ps{B - 1}"))
                    act.copy(h_t[at.s][:, :, :], h_ps[:, :, :]).then_inc(*act_ht.did("h_t"))
                batches(act, g.turns, (copy, 0), (relu, 2), (copy_h, 3))

            @block.vector
            def _(dve):
                norm.prepare(dve)
                dve.wait_ge(loaded, 8 * 16)

                def add(at):
                    dve.wait_ge(*pe_r.after(at, "root_ps"))
                    dve.wait_ge(*gathered.after(at))
                    dve.wait_ge(*got.after(at))
                    if at.has(SLOTS):
                        dve.wait_ge(*stored.after(at.back(SLOTS)))
                        dve.wait_ge(*act_h.after(at.back(SLOTS), "h"))
                    dve.tensor_tensor(new[at.s][:, :, :], root_ps[:, :, :], sums[at.s][:, :, :],
                                      ALU.add).then_inc(*dve_x.did("conv"))
                    dve.wait_ge(*dve_x.after(at, "conv"))
                    dve.tensor_tensor(new[at.s][:, :, :], new[at.s][:, :, :], old[at.s][:, :, :],
                                      ALU.add).then_inc(*dve_x.did("new"))
                    dve.wait_ge(*dve_x.after(at, "new"))
                    norm.take_moments(dve, at, new[at.s])

                def shift(at):
                    norm.make_shift(dve, at, lambda a: act_h.after(a, "h"))

                def evacuate(at):
                    if at.has(SLOTS):
                        dve.wait_ge(*stored_q.after(at.back(SLOTS)))
                    for j in range(B):
                        dve.wait_ge(*pe_q.after(at, f"qkv_ps{j}"))
                        dve.tensor_tensor(qkv[at.s][:, j, :], qkv_ps[j][:, :], wide_bias[:, :],
                                          ALU.add).then_inc(*dve_q.did(f"qkv{j}"))
                batches(dve, g.turns, (evacuate, 4), (shift, 2), (add, 1))


def attend(nc, g, sums_table, h_table, x_table, wo, bo, w1, b1, w2, b2, g1, be1, g2, be2, new_x, new_h):
    T, width = g.T, D + HEADS + 1
    with Pass(nc, "attend") as w:
        wo_sb, w1_sb, w2_sb = (w.sb(n, [P, D]) for n in ("wo", "w1", "w2"))
        bo_row, b2_row, b1_col = w.sb("bo", [1, B, D]), w.sb("b2", [1, B, D]), w.sb("b1", [P, 1])
        sums = w.slots("sums", [P, B, width])
        share = w.slots("share", [P, B, HEADS])
        heads, heads_t, h_in, x_in = (w.slots(n, [P, B, D]) for n in ("heads", "heads_t", "h_in", "x_in"))
        pre_y, y, y_t, u_t = (w.slots(n, [P, B, D]) for n in ("pre_y", "y", "y_t", "u_t"))
        pre_z, z, x_out, h_out = (w.slots(n, [P, B, D]) for n in ("pre_z", "z", "x_out", "h_out"))
        heads_ps, o_ps, y_ps, u_ps, v_ps = (w.ps(n, [P, B, D]) for n in ("heads_ps", "o_ps", "y_ps", "u_ps", "v_ps"))
        norm_y, norm_z, norm_x = Norm(w, "norm_y"), Norm(w, "norm_z"), Norm(w, "norm_x")
        to_y, to_z = Affine(w, "to_y", norm_y, g1, be1), Affine(w, "to_z", norm_z, g2, be2)
        got_h, got_x, gathered = w.moves("got_h", 1), w.moves("got_x", 1), w.moves("gathered", B)
        stored_x, stored_h = w.moves("stored_x", 1), w.moves("stored_h", 1)
        loaded, gate = w.sem("loaded"), w.sem("gate")
        dve_h = w.steps("dve_h", "degree", "guarded", "share", "heads")
        dve_y, dve_z, dve_x = w.steps("dve_y", "pre_y"), w.steps("dve_z", "pre_z"), w.steps("dve_x", "x_out")
        pe_h, pe_o, pe_y = w.steps("pe_h", "heads_ps"), w.steps("pe_o", "o_ps"), w.steps("pe_y", "y_ps")
        pe_u, pe_v = w.steps("pe_u", "u_ps"), w.steps("pe_v", "v_ps")
        act_h, act_y, act_u, act_x = (w.steps(f"act_{n}", n) for n in ("heads_t", "y_t", "u_t", "h_out"))
        with nc.Block() as block:

            @block.sync
            def _(sp):
                to_y.load(sp)
                to_z.load(sp)
                for out, weight in ((wo_sb, wo), (w1_sb, w1), (w2_sb, w2)):
                    sp.dma_start(out[:, :], weight).then_inc(loaded, 16)
                batch_bias(sp, bo_row, bo, loaded)
                batch_bias(sp, b2_row, b2, loaded)
                sp.dma_start(b1_col[:, :], b1.unsqueeze(1)).then_inc(loaded, 16)

                def load_h(at):
                    if at.has(SLOTS):
                        sp.wait_ge(*dve_y.after(at.back(SLOTS), "pre_y"))
                    sp.dma_start(h_in[at.s][:, :, :], columns_of(h_table, T)[:, at.columns(), :]).then_inc(*got_h.did(at))

                def load_x(at):
                    if at.has(SLOTS):
                        sp.wait_ge(*dve_x.after(at.back(SLOTS), "x_out"))
                    sp.dma_start(x_in[at.s][:, :, :], columns_of(x_table, T)[:, at.columns(), :]).then_inc(*got_x.did(at))

                def store_x(at):
                    sp.wait_ge(*dve_x.after(at, "x_out"))
                    sp.dma_start(columns_of(new_x, T)[:, at.columns(), :], x_out[at.s][:, :, :]).then_inc(*stored_x.did(at))

                def store_h(at):
                    sp.wait_ge(*act_x.after(at, "h_out"))
                    sp.dma_start(columns_of(new_h, T)[:, at.columns(), :], h_out[at.s][:, :, :]).then_inc(*stored_h.did(at))
                batches(sp, g.turns, (load_h, 0), (load_x, 3), (store_x, 7), (store_h, 8))
                stored_x.all_of(sp, g.turns)
                stored_h.all_of(sp, g.turns)

            @block.gpsimd
            def _(pool):
                gather = gatherer(pool, w, g, gate, gathered, lambda at: [dve_h.after(at, "heads")],
                                  (sums_table, g.end, sums, 0, width))
                batches(pool, g.turns, (gather, 0),
                        (lambda at: norm_x.root(pool, at, lambda a: act_x.after(a, "h_out")), 6),
                        (lambda at: norm_z.root(pool, at, lambda a: to_z.steps.after(a, "scaled")), 5),
                        (lambda at: norm_y.root(pool, at, lambda a: to_y.steps.after(a, "scaled")), 3))

            @block.tensor
            def _(pe):
                def turn_heads(at):
                    pe.wait_ge(*dve_h.after(at, "heads"))
                    if at.has(1):
                        pe.wait_ge(*act_h.after(at.back(1), "heads_t"))
                    transpose_rows(pe, g, heads_ps, heads[at.s]).then_inc(*pe_h.did("heads_ps"))

                def times_wo(at):
                    pe.wait_ge(loaded, 6 * 16)
                    pe.wait_ge(*act_h.after(at, "heads_t"))
                    if at.has(1):
                        pe.wait_ge(*dve_y.after(at.back(1), "pre_y"))
                    rows_times(pe, o_ps, heads_t[at.s], wo_sb[:, :], bo_row, g.ones).then_inc(*pe_o.did("o_ps"))

                def turn_y(at):
                    pe.wait_ge(*to_y.steps.after(at, "offset"))
                    if at.has(1):
                        pe.wait_ge(*act_y.after(at.back(1), "y_t"))
                    transpose_rows(pe, g, y_ps, y[at.s]).then_inc(*pe_y.did("y_ps"))

                def times_w1(at):
                    pe.wait_ge(*act_y.after(at, "y_t"))
                    if at.has(1):
                        pe.wait_ge(*act_u.after(at.back(1), "u_t"))
                    pe.matmul(u_ps[:, :, :], w1_sb[:, :], y_t[at.s][:, :, :], start=True, stop=True).then_inc(*pe_u.did("u_ps"))

                def times_w2(at):
                    pe.wait_ge(*act_u.after(at, "u_t"))
                    if at.has(1):
                        pe.wait_ge(*dve_z.after(at.back(1), "pre_z"))
                    rows_times(pe, v_ps, u_t[at.s], w2_sb[:, :], b2_row, g.ones).then_inc(*pe_v.did("v_ps"))
                batches(pe, g.turns, (turn_heads, 1), (times_wo, 2), (times_w2, 5), (turn_y, 4), (times_w1, 4))

            @block.scalar
            def _(act):
                def copy_heads(at):
                    act.wait_ge(*pe_h.after(at, "heads_ps"))
                    if at.has(SLOTS):
                        act.wait_ge(*pe_o.after(at.back(SLOTS), "o_ps"))
                    act.copy(heads_t[at.s][:, :, :], heads_ps[:, :, :]).then_inc(*act_h.did("heads_t"))

                def copy_y(at):
                    act.wait_ge(*pe_y.after(at, "y_ps"))
                    if at.has(SLOTS):
                        act.wait_ge(*pe_u.after(at.back(SLOTS), "u_ps"))
                    act.copy(y_t[at.s][:, :, :], y_ps[:, :, :]).then_inc(*act_y.did("y_t"))

                def gelu(at):
                    act.wait_ge(loaded, 6 * 16)
                    act.wait_ge(*pe_u.after(at, "u_ps"))
                    if at.has(SLOTS):
                        act.wait_ge(*pe_v.after(at.back(SLOTS), "v_ps"))
                    act.activation(u_t[at.s][:, :, :], u_ps[:, :, :], ACT.Gelu, bias=b1_col[:, :]).then_inc(*act_u.did("u_t"))

                def relu(at):
                    if at.has(SLOTS):
                        act.wait_ge(*stored_h.after(at.back(SLOTS)))
                    norm_x.relu(act, at, h_out[at.s], x_out[at.s]).then_inc(*act_x.did("h_out"))
                batches(act, g.turns, (copy_heads, 1), (copy_y, 4), (gelu, 4), (relu, 7))

            @block.vector
            def _(dve):
                for norm in (norm_y, norm_z, norm_x):
                    norm.prepare(dve)
                for affine in (to_y, to_z):
                    dve.wait_ge(affine.loaded, 2 * 16)

                def mean_of_values(at):
                    dve.wait_ge(*gathered.after(at))
                    if at.has(SLOTS):
                        dve.wait_ge(*pe_h.after(at.back(SLOTS), "heads_ps"))
                    dve.tensor_copy(g.degree[:, at.columns()], sums[at.s][:, :, D + HEADS]).then_inc(*dve_h.did("degree"))
                    dve.tensor_scalar(share[at.s][:, :, :], sums[at.s][:, :, D:D + HEADS], 1e-16, None,
                                      ALU.add).then_inc(*dve_h.did("guarded"))
                    dve.wait_ge(*dve_h.after(at, "guarded"))
                    dve.reciprocal(share[at.s][:, :, :], share[at.s][:, :, :]).then_inc(*dve_h.did("share"))
                    dve.wait_ge(*dve_h.after(at, "share"))
                    dve.tensor_tensor(heads[at.s][:, :, :].rearrange("p b (h d) -> p b h d", h=HEADS),
                                      sums[at.s][:, :, 0:D].rearrange("p b (h d) -> p b h d", h=HEADS),
                                      share[at.s][:, :, :].unsqueeze(3).to_broadcast([P, B, HEADS, HEAD_DIM]),
                                      ALU.mult).then_inc(*dve_h.did("heads"))

                def add_h(at):
                    dve.wait_ge(*pe_o.after(at, "o_ps"))
                    dve.wait_ge(*got_h.after(at))
                    dve.tensor_tensor(pre_y[at.s][:, :, :], o_ps[:, :, :], h_in[at.s][:, :, :],
                                      ALU.add).then_inc(*dve_y.did("pre_y"))
                    dve.wait_ge(*dve_y.after(at, "pre_y"))
                    norm_y.take_moments(dve, at, pre_y[at.s])

                def make_y(at):
                    if at.has(SLOTS):
                        dve.wait_ge(*pe_y.after(at.back(SLOTS), "y_ps"))
                    to_y.apply(dve, at, y[at.s], pre_y[at.s])

                def add_y(at):
                    dve.wait_ge(*pe_v.after(at, "v_ps"))
                    dve.wait_ge(*to_y.steps.after(at, "offset"))
                    dve.tensor_tensor(pre_z[at.s][:, :, :], v_ps[:, :, :], y[at.s][:, :, :],
                                      ALU.add).then_inc(*dve_z.did("pre_z"))
                    dve.wait_ge(*dve_z.after(at, "pre_z"))
                    norm_z.take_moments(dve, at, pre_z[at.s])

                def make_x(at):
                    to_z.apply(dve, at, z[at.s], pre_z[at.s])
                    dve.wait_ge(*to_z.steps.after(at, "offset"))
                    dve.wait_ge(*got_x.after(at))
                    if at.has(SLOTS):
                        dve.wait_ge(*stored_x.after(at.back(SLOTS)))
                        dve.wait_ge(*act_x.after(at.back(SLOTS), "h_out"))
                    dve.tensor_tensor(x_out[at.s][:, :, :], x_in[at.s][:, :, :], z[at.s][:, :, :],
                                      ALU.add).then_inc(*dve_x.did("x_out"))
                    dve.wait_ge(*dve_x.after(at, "x_out"))
                    norm_x.take_moments(dve, at, x_out[at.s])

                def shift(at):
                    norm_x.make_shift(dve, at, lambda a: act_x.after(a, "h_out"))
                batches(dve, g.turns, (mean_of_values, 1), (shift, 7), (make_x, 6), (add_y, 5), (make_y, 4), (add_h, 2))


def gated_unit(nc, name, g, sums_table, width, edge_sums, h_table, w_msg_t, w_ih_t, w_hh_t, b_ih, b_hh, out_table):
    T = g.T
    first = width > D
    with Pass(nc, name) as w:
        msg_x, msg_e = w.sb("msg_x", [P, D]), w.sb("msg_e", [EDGE_DIM, D])
        w_ih, w_hh = w.sb("w_ih", [P, 3 * D]), w.sb("w_hh", [P, 3 * D])
        bias_i, bias_h, bias = w.sb("bias_i", [P, 3]), w.sb("bias_h", [P, 3]), w.sb("bias_sum", [P, 3])
        sums, h = w.slots("sums", [P, B, width]), w.slots("h", [P, B, D])
        edges = None if first else w.slots("edges", [P, B, EDGE_DIM])
        s_t, h_t, m_t = (w.slots(n, [P, B, D]) for n in ("s_t", "h_t", "m_t"))
        e_t = w.slots("e_t", [EDGE_DIM, B, D])
        reset, keep, inner, new = (w.slots(n, [P, B, D]) for n in ("reset", "keep", "inner", "new"))
        cand, out = w.slots("cand", [P, B, D]), w.slots("out", [P, B, D])
        s_ps, h_ps, m_ps, r_ps, z_ps, i_ps, n_ps = (w.ps(n, [P, B, D]) for n in
                                                    ("s_ps", "h_ps", "m_ps", "r_ps", "z_ps", "i_ps", "n_ps"))
        shared_ps = w.ps("shared_ps", [P, B, D])
        got, got_e, gathered = w.moves("got", 1), w.moves("got_e", 1), w.moves("gathered", B)
        stored, stored_e = w.moves("stored", 1), w.moves("stored_e", 1)
        loaded, gate, biased, pe_gate = (w.sem(n) for n in ("loaded", "gate", "biased", "pe_gate"))
        pe_t = w.steps("pe_t", "s_ps", "h_ps", "e_ps")
        pe_m, pe_o = w.steps("pe_m", "m_ps"), w.steps("pe_o", "out_ps")
        pe_g = w.steps("pe_g", "r_ps", "z_ps", "n_ps", "i_ps")
        act_t, act_m = w.steps("act_t", "s_t", "e_t"), w.steps("act_m", "m_t")
        act_g, act_c = w.steps("act_g", "reset", "keep"), w.steps("act_c", "cand")
        dve_h, dve_i = w.steps("dve_h", "h_t"), w.steps("dve_i", "gated", "inner")
        dve_n, dve_o = w.steps("dve_n", "apart", "kept", "new"), w.steps("dve_o", "out")
        n_loads = 6

        with nc.Block() as block:

            @block.sync
            def _(sp):
                sp.dma_start(msg_x[:, :], w_msg_t[0:D, :]).then_inc(loaded, 16)
                sp.dma_start(msg_e[:, :], w_msg_t[D:D + EDGE_DIM, :]).then_inc(loaded, 16)
                sp.dma_start(w_ih[:, :], w_ih_t).then_inc(loaded, 16)
                sp.dma_start(w_hh[:, :], w_hh_t).then_inc(loaded, 16)
                sp.dma_start(bias_i[:, :], b_ih).then_inc(loaded, 16)
                sp.dma_start(bias_h[:, :], b_hh).then_inc(loaded, 16)

                def load(at):
                    if at.has(SLOTS):
                        sp.wait_ge(*pe_t.after(at.back(SLOTS), "e_ps"))
                    sp.dma_start(h[at.s][:, :, :], columns_of(h_table, T)[:, at.columns(), :]).then_inc(*got.did(at))
                    if not first:
                        sp.dma_start(edges[at.s][:, :, :], columns_of(edge_sums, T)[:, at.columns(), :]).then_inc(*got_e.did(at))

                def store_edges(at):
                    sp.wait_ge(*gathered.after(at))
                    sp.dma_start(columns_of(edge_sums, T)[:, at.columns(), :], sums[at.s][:, :, D:width]).then_inc(*stored_e.did(at))

                def store(at):
                    sp.wait_ge(*dve_o.after(at, "out"))
                    sp.dma_start(columns_of(out_table, T)[:, at.columns(), :], out[at.s][:, :, :]).then_inc(*stored.did(at))
                if first:
                    batches(sp, g.turns, (load, 0), (store_edges, 1), (store, 4))
                    stored_e.all_of(sp, g.turns)
                else:
                    batches(sp, g.turns, (load, 0), (store, 4))
                stored.all_of(sp, g.turns)

            @block.gpsimd
            def _(pool):
                free = lambda at: [pe_t.after(at, "e_ps")] + ([stored_e.after(at)] if first else [])
                batches(pool, g.turns, (gatherer(pool, w, g, gate, gathered, free, (sums_table, g.end, sums, 0, width)), 0))

            @block.tensor
            def _(pe):
                def turn(at):
                    pe.wait_ge(*gathered.after(at))
                    if at.has(1):
                        pe.wait_ge(*act_t.after(at.back(1), "s_t"))
                    for j in range(B):
                        last = pe.transpose(s_ps[:, j, :], sums[at.s][:, j, 0:D], g.ident[:, :])
                    last.then_inc(*pe_t.did("s_ps"))
                    pe.wait_ge(*got.after(at))
                    if at.has(1):
                        pe.wait_ge(*dve_h.after(at.back(1), "h_t"))
                    transpose_rows(pe, g, h_ps, h[at.s]).then_inc(*pe_t.did("h_ps"))
                    if at.has(4):
                        pe.wait_ge(*dve_o.after(at.back(4), "out"))
                    if at.has(1):
                        pe.wait_ge(*act_t.after(at.back(1), "e_t"))
                    if not first:
                        pe.wait_ge(*got_e.after(at))
                    pe.sem_inc(pe_gate, 1)
                    for j in range(B):
                        last = pe.transpose(shared_ps[0:EDGE_DIM, j, :],
                                            sums[at.s][:, j, D:width] if first else edges[at.s][:, j, :], g.ident[:, :])
                    last.then_inc(*pe_t.did("e_ps"))

                def message(at):
                    pe.wait_ge(loaded, n_loads * 16)
                    pe.wait_ge(*act_t.after(at, "e_t"))
                    if at.has(1):
                        pe.wait_ge(*act_m.after(at.back(1), "m_t"))
                    pe.matmul(m_ps[:, :, :], msg_x[:, :], s_t[at.s][:, :, :], start=True, stop=False)
                    pe.matmul(m_ps[:, :, :], msg_e[:, :], e_t[at.s][:, :, :], start=False, stop=True).then_inc(*pe_m.did("m_ps"))

                def gates(at):
                    pe.wait_ge(*dve_h.after(at, "h_t"))
                    pe.wait_ge(*act_m.after(at, "m_t"))
                    for k, (ps, used) in enumerate(((r_ps, lambda a: act_g.after(a, "reset")),
                                                    (z_ps, lambda a: act_g.after(a, "keep")))):
                        if at.has(1):
                            pe.wait_ge(*used(at.back(1)))
                        pe.matmul(ps[:, :, :], w_hh[:, k * D:(k + 1) * D], h_t[at.s][:, :, :], start=True, stop=False)
                        pe.matmul(ps[:, :, :], w_ih[:, k * D:(k + 1) * D], m_t[at.s][:, :, :], start=False,
                                  stop=True).then_inc(*pe_g.did("rz"[k] + "_ps"))
                    if at.has(1):
                        pe.wait_ge(*dve_i.after(at.back(1), "gated"))
                    pe.matmul(n_ps[:, :, :], w_hh[:, 2 * D:3 * D], h_t[at.s][:, :, :], start=True,
                              stop=True).then_inc(*pe_g.did("n_ps"))
                    if at.has(1):
                        pe.wait_ge(*dve_i.after(at.back(1), "inner"))
                    pe.matmul(i_ps[:, :, :], w_ih[:, 2 * D:3 * D], m_t[at.s][:, :, :], start=True,
                              stop=True).then_inc(*pe_g.did("i_ps"))

                def turn_back(at, newest):
                    pe.wait_ge(*dve_n.after(at, "new"))
                    pe.wait_ge(*act_t.after(newest, "e_t"))
                    if at.has(1):
                        pe.wait_ge(*dve_o.after(at.back(1), "out"))
                    transpose_rows(pe, g, shared_ps, new[at.s]).then_inc(*pe_o.did("out_ps"))

                def back_stage(at):
                    if isinstance(at.turn, int):
                        turn_back(at, At(*divmod(min(at.b + 3, SLOTS * g.turns - 1), SLOTS)))
                    else:
                        turn_back(at, at.back(-3))
                batches(pe, g.turns, (turn, 0), (message, 1), (gates, 2), (back_stage, 3))

            @block.scalar
            def _(act):
                def copy(at):
                    act.wait_ge(*pe_t.after(at, "s_ps"))
                    if at.has(SLOTS):
                        act.wait_ge(*pe_m.after(at.back(SLOTS), "m_ps"))
                    act.copy(s_t[at.s][:, :, :], s_ps[:, :, :]).then_inc(*act_t.did("s_t"))
                    act.wait_ge(*pe_t.after(at, "e_ps"))
                    act.copy(e_t[at.s][:, :, :], shared_ps[0:EDGE_DIM, :, :]).then_inc(*act_t.did("e_t"))

                def copy_m(at):
                    act.wait_ge(*pe_m.after(at, "m_ps"))
                    if at.has(SLOTS):
                        act.wait_ge(*pe_g.after(at.back(SLOTS), "i_ps"))
                    act.copy(m_t[at.s][:, :, :], m_ps[:, :, :]).then_inc(*act_m.did("m_t"))

                def gates(at):
                    act.wait_ge(biased, 1)
                    for k, (out_, ps, step, last_use) in enumerate(((reset, r_ps, "r_ps", dve_i.after), (keep, z_ps, "z_ps", dve_n.after))):
                        act.wait_ge(*pe_g.after(at, step))
                        if at.has(SLOTS):
                            act.wait_ge(*last_use(at.back(SLOTS), ("gated", "kept")[k]))
                        act.activation(out_[at.s][:, :, :], ps[:, :, :], ACT.Sigmoid,
                                       bias=bias[:, k:k + 1]).then_inc(*act_g.did(("reset", "keep")[k]))

                def candidate(at):
                    act.wait_ge(*dve_i.after(at, "inner"))
                    if at.has(SLOTS):
                        act.wait_ge(*dve_n.after(at.back(SLOTS), "new"))
                    act.activation(cand[at.s][:, :, :], inner[at.s][:, :, :], ACT.Tanh, bias=bias_i[:, 2:3]).then_inc(*act_c.did("cand"))
                batches(act, g.turns, (copy, 0), (copy_m, 1), (gates, 2), (candidate, 2))

            @block.vector
            def _(dve):
                dve.wait_ge(loaded, n_loads * 16)
                dve.tensor_tensor(bias[:, :], bias_i[:, :], bias_h[:, :], ALU.add).then_inc(biased, 1)

                def copy(at):
                    dve.wait_ge(*pe_t.after(at, "h_ps"))
                    if at.has(SLOTS):
                        dve.wait_ge(*pe_g.after(at.back(SLOTS), "n_ps"))
                        dve.wait_ge(*dve_n.after(at.back(SLOTS), "apart"))
                    dve.tensor_copy(h_t[at.s][:, :, :], h_ps[:, :, :]).then_inc(*dve_h.did("h_t"))

                def gated(at):
                    dve.wait_ge(*act_g.after(at, "reset"))
                    dve.wait_ge(*pe_g.after(at, "i_ps"))
                    if at.has(SLOTS):
                        dve.wait_ge(*act_c.after(at.back(SLOTS), "cand"))
                    dve.scalar_tensor_tensor(inner[at.s][:, :, :], n_ps[:, :, :], bias_h[:, 2:3], reset[at.s][:, :, :],
                                             ALU.add, ALU.mult).then_inc(*dve_i.did("gated"))
                    dve.wait_ge(*dve_i.after(at, "gated"))
                    dve.tensor_tensor(inner[at.s][:, :, :], i_ps[:, :, :], inner[at.s][:, :, :],
                                      ALU.add).then_inc(*dve_i.did("inner"))

                def mix(at):
                    dve.wait_ge(*act_c.after(at, "cand"))
                    if at.has(SLOTS):
                        dve.wait_ge(*pe_o.after(at.back(SLOTS), "out_ps"))
                    dve.tensor_tensor(new[at.s][:, :, :], h_t[at.s][:, :, :], cand[at.s][:, :, :],
                                      ALU.subtract).then_inc(*dve_n.did("apart"))
                    dve.wait_ge(*dve_n.after(at, "apart"))
                    dve.tensor_tensor(new[at.s][:, :, :], new[at.s][:, :, :], keep[at.s][:, :, :],
                                      ALU.mult).then_inc(*dve_n.did("kept"))
                    dve.wait_ge(*dve_n.after(at, "kept"))
                    dve.tensor_tensor(new[at.s][:, :, :], new[at.s][:, :, :], cand[at.s][:, :, :],
                                      ALU.add).then_inc(*dve_n.did("new"))

                def copy_out(at):
                    dve.wait_ge(*pe_o.after(at, "out_ps"))
                    if at.has(SLOTS):
                        dve.wait_ge(*stored.after(at.back(SLOTS)))
                    dve.tensor_copy(out[at.s][:, :, :], shared_ps[:, :, :]).then_inc(*dve_o.did("out"))
                batches(dve, g.turns, (copy, 0), (copy_out, 4), (gated, 2), (mix, 3))


def evolve_weight(nc, g, w0, w0_t, w_ih_t, w_hh_t, b_ih, b_hh, weight, inverse_root):
    T = g.T
    with Pass(nc, "evolve") as w:
        w0_sb, w0_t_sb = w.sb("w0", [P, D]), w.sb("w0_t", [P, D])
        w_ih, w_hh = w.sb("w_ih", [P, 3 * D]), w.sb("w_hh", [P, 3 * D])
        bias_i, bias_h = w.sb("bias_i", [P, 3 * D]), w.sb("bias_h", [P, 3 * D])
        gate_i, gate_h = w.sb("gate_i", [P, 3 * D]), w.sb("gate_h", [P, 3 * D])
        cand = w.sb("cand", [P, D])
        power, some = w.sb("power", [P, T]), w.sb("some", [P, T])
        i_ps, h_ps = w.ps("i_ps", [P, 3 * D]), w.ps("h_ps", [P, 3 * D])
        loaded, chain, product, ready, squashed, rooted = (w.sem(n) for n in (
            "loaded", "chain", "product", "ready", "squashed", "rooted"))
        with nc.Block() as block:

            @block.sync
            def _(sp):
                for out, table in ((w0_sb, w0), (w0_t_sb, w0_t), (w_ih, w_ih_t), (w_hh, w_hh_t)):
                    sp.dma_start(out[:, :], table).then_inc(loaded, 16)
                for out, vector in ((bias_i, b_ih), (bias_h, b_hh)):
                    sp.dma_start(out[:, :], vector.partition_broadcast(P)).then_inc(loaded, 16)

            @block.tensor
            def _(pe):
                pe.wait_ge(loaded, 6 * 16)
                pe.matmul(i_ps[:, :], w0_t_sb[:, :], w_ih[:, :], start=True, stop=True)
                pe.matmul(h_ps[:, :], w0_t_sb[:, :], w_hh[:, :], start=True, stop=True).then_inc(product, 1)

            @block.gpsimd
            def _(pool):
                pool.wait_ge(ready, 2)
                pool.tensor_tensor(inverse_root[:, :], g.degree[:, :], power[:, :], ALU.pow).then_inc(rooted, 1)

            @block.scalar
            def _(act):
                act.wait_ge(ready, 3)
                act.activation(gate_i[:, 0:2 * D], gate_i[:, 0:2 * D], ACT.Sigmoid).then_inc(squashed, 1)
                act.wait_ge(ready, 4)
                act.activation(cand[:, :], cand[:, :], ACT.Tanh).then_inc(squashed, 1)

            @block.vector
            def _(dve):
                n = 0

                def then(ins):
                    nonlocal n
                    n += 1
                    ins.then_inc(chain, 1)
                    dve.wait_ge(chain, n)

                then(dve.tensor_scalar(g.degree[:, :], g.degree[:, :], 1.0, None, ALU.add))
                then(dve.tensor_scalar(some[:, :], g.degree[:, :], 0.0, None, ALU.is_gt))
                dve.memset(power[:, :], -0.5).then_inc(ready, 1)
                dve.tensor_scalar(g.degree[:, :], g.degree[:, :], 1e-30, None, ALU.max).then_inc(ready, 1)
                dve.wait_ge(rooted, 1)
                then(dve.tensor_tensor(inverse_root[:, :], inverse_root[:, :], some[:, :], ALU.mult))
                dve.wait_ge(product, 1)
                dve.wait_ge(loaded, 6 * 16)
                then(dve.tensor_tensor(gate_i[:, :], i_ps[:, :], bias_i[:, :], ALU.add))
                then(dve.tensor_tensor(gate_h[:, :], h_ps[:, :], bias_h[:, :], ALU.add))
                dve.tensor_tensor(gate_i[:, 0:2 * D], gate_i[:, 0:2 * D], gate_h[:, 0:2 * D], ALU.add).then_inc(ready, 1)
                dve.wait_ge(squashed, 1)
                then(dve.tensor_tensor(cand[:, :], gate_i[:, 0:D], gate_h[:, 2 * D:3 * D], ALU.mult))
                dve.tensor_tensor(cand[:, :], cand[:, :], gate_i[:, 2 * D:3 * D], ALU.add).then_inc(ready, 1)
                dve.wait_ge(squashed, 2)
                then(dve.tensor_tensor(weight[:, :], w0_sb[:, :], cand[:, :], ALU.subtract))
                then(dve.tensor_tensor(weight[:, :], weight[:, :], gate_i[:, D:2 * D], ALU.mult))
                then(dve.tensor_tensor(weight[:, :], weight[:, :], cand[:, :], ALU.add))


def evolve_rows(nc, g, x_table, unit_table, weight, inverse_root, new_x, rows_table):
    T = g.T
    with Pass(nc, "rows") as w:
        old, unit, new, h, h_t, out = (w.slots(n, [P, B, D]) for n in ("old", "unit", "new", "h", "h_t", "out"))
        h_ps = [w.ps(f"h_ps{k}", [P, B, D]) for k in range(2)]
        out_ps = [w.ps(f"out_ps{k}", [P, B, D]) for k in range(2)]
        norm = Norm(w, "norm")
        got, stored, stored_x = w.moves("got", 2), w.moves("stored", 1), w.moves("stored_x", 1)
        pe_h, pe_o = w.steps("pe_h", "h_ps"), w.steps("pe_o", "out_ps")
        act_h, act_t, act_o = w.steps("act_h", "h"), w.steps("act_t", "h_t"), w.steps("act_o", "out")
        dve_x = w.steps("dve_x", "new")
        with nc.Block() as block:

            @block.sync
            def _(sp):
                def load(at):
                    if at.has(SLOTS):
                        sp.wait_ge(*dve_x.after(at.back(SLOTS), "new"))
                    for out_, table in ((old, x_table), (unit, unit_table)):
                        sp.dma_start(out_[at.s][:, :, :], columns_of(table, T)[:, at.columns(), :]).then_inc(*got.did(at))

                def store_x(at):
                    sp.wait_ge(*dve_x.after(at, "new"))
                    sp.dma_start(columns_of(new_x, T)[:, at.columns(), :], new[at.s][:, :, :]).then_inc(*stored_x.did(at))

                def store(at):
                    sp.wait_ge(*act_o.after(at, "out"))
                    sp.dma_start(columns_of(rows_table, T)[:, at.columns(), :], out[at.s][:, :, :]).then_inc(*stored.did(at))
                batches(sp, g.turns, (load, 0), (store_x, 2), (store, 4))
                stored_x.all_of(sp, g.turns)
                stored.all_of(sp, g.turns)

            @block.gpsimd
            def _(pool):
                batches(pool, g.turns, (lambda at: norm.root(pool, at, lambda a: act_h.after(a, "h")), 0))

            @block.tensor
            def _(pe):
                def turn(at):
                    pe.wait_ge(*act_h.after(at, "h"))
                    if at.has(2):
                        pe.wait_ge(*act_t.after(at.back(2), "h_t"))
                    transpose_rows(pe, g, h_ps[at.s % 2], h[at.s]).then_inc(*pe_h.did("h_ps"))

                def product(at):
                    pe.wait_ge(*act_t.after(at, "h_t"))
                    if at.has(2):
                        pe.wait_ge(*act_o.after(at.back(2), "out"))
                    for j in range(B):
                        last = pe.matmul(out_ps[at.s % 2][:, j, :], h_t[at.s][:, j, :], weight[:, :], start=True, stop=True)
                    last.then_inc(*pe_o.did("out_ps"))
                batches(pe, g.turns, (turn, 1), (product, 2))

            @block.scalar
            def _(act):
                def relu(at):
                    if at.has(SLOTS):
                        act.wait_ge(*pe_h.after(at.back(SLOTS), "h_ps"))
                    norm.relu(act, at, h[at.s], new[at.s]).then_inc(*act_h.did("h"))

                def copy(at):
                    act.wait_ge(*pe_h.after(at, "h_ps"))
                    if at.has(SLOTS):
                        act.wait_ge(*pe_o.after(at.back(SLOTS), "out_ps"))
                    act.copy(h_t[at.s][:, :, :], h_ps[at.s % 2][:, :, :]).then_inc(*act_t.did("h_t"))

                def scaled(at):
                    act.wait_ge(*pe_o.after(at, "out_ps"))
                    if at.has(SLOTS):
                        act.wait_ge(*stored.after(at.back(SLOTS)))
                    for j in range(B):
                        last = act.activation(out[at.s][:, j, :], out_ps[at.s % 2][:, j, :], ACT.Copy,
                                              scale=inverse_root[:, bass.ds(at.b * B + j, 1)])
                    last.then_inc(*act_o.did("out"))
                batches(act, g.turns, (relu, 1), (copy, 2), (scaled, 3))

            @block.vector
            def _(dve):
                norm.prepare(dve)

                def add(at):
                    dve.wait_ge(*got.after(at))
                    if at.has(SLOTS):
                        dve.wait_ge(*stored_x.after(at.back(SLOTS)))
                        dve.wait_ge(*act_h.after(at.back(SLOTS), "h"))
                    dve.tensor_tensor(new[at.s][:, :, :], old[at.s][:, :, :], unit[at.s][:, :, :],
                                      ALU.add).then_inc(*dve_x.did("new"))
                    dve.wait_ge(*dve_x.after(at, "new"))
                    norm.take_moments(dve, at, new[at.s])

                def shift(at):
                    norm.make_shift(dve, at, lambda a: act_h.after(a, "h"))
                batches(dve, g.turns, (shift, 1), (add, 0))


def finish(nc, g, sums_table, rows_table, x_table, inverse_root, lin_w_t, lin_b, out):
    T = g.T
    with Pass(nc, "finish") as w:
        weight, bias_row = w.sb("weight", [P, D]), w.sb("bias", [1, B, D])
        sums, own, old, both, h, h_t, new = (w.slots(n, [P, B, D]) for n in
                                             ("sums", "own", "old", "both", "h", "h_t", "new"))
        h_ps = [w.ps(f"h_ps{k}", [P, B, D]) for k in range(2)]
        out_ps = [w.ps(f"out_ps{k}", [P, B, D]) for k in range(2)]
        loaded, gate = w.sem("loaded"), w.sem("gate")
        got, gathered, stored = w.moves("got", 2), w.moves("gathered", B), w.moves("stored", 1)
        pe_h, pe_o = w.steps("pe_h", "h_ps"), w.steps("pe_o", "out_ps")
        act_h, act_t = w.steps("act_h", "h"), w.steps("act_t", "h_t")
        dve_b, dve_n = w.steps("dve_b", "both"), w.steps("dve_n", "new")
        with nc.Block() as block:

            @block.sync
            def _(sp):
                sp.dma_start(weight[:, :], lin_w_t).then_inc(loaded, 16)
                batch_bias(sp, bias_row, lin_b, loaded)

                def load(at):
                    if at.has(SLOTS):
                        sp.wait_ge(*dve_n.after(at.back(SLOTS), "new"))
                    for out_, table in ((own, rows_table), (old, x_table)):
                        sp.dma_start(out_[at.s][:, :, :], columns_of(table, T)[:, at.columns(), :]).then_inc(*got.did(at))

                def store(at):
                    sp.wait_ge(*dve_n.after(at, "new"))
                    sp.dma_start(columns_of(out, T)[:, at.columns(), :], new[at.s][:, :, :]).then_inc(*stored.did(at))
                batches(sp, g.turns, (load, 0), (store, 3))
                stored.all_of(sp, g.turns)

            @block.gpsimd
            def _(pool):
                batches(pool, g.turns, (gatherer(pool, w, g, gate, gathered, lambda at: [dve_b.after(at, "both")],
                                                 (sums_table, g.end, sums, 0, D)), 0))

            @block.tensor
            def _(pe):
                def turn(at):
                    pe.wait_ge(*act_h.after(at, "h"))
                    if at.has(2):
                        pe.wait_ge(*act_t.after(at.back(2), "h_t"))
                    transpose_rows(pe, g, h_ps[at.s % 2], h[at.s]).then_inc(*pe_h.did("h_ps"))

                def product(at):
                    pe.wait_ge(loaded, 2 * 16)
                    pe.wait_ge(*act_t.after(at, "h_t"))
                    if at.has(2):
                        pe.wait_ge(*dve_n.after(at.back(2), "new"))
                    rows_times(pe, out_ps[at.s % 2], h_t[at.s], weight[:, :], bias_row, g.ones).then_inc(*pe_o.did("out_ps"))
                batches(pe, g.turns, (turn, 0), (product, 1))

            @block.scalar
            def _(act):
                def relu(at):
                    act.wait_ge(*dve_b.after(at, "both"))
                    if at.has(SLOTS):
                        act.wait_ge(*pe_h.after(at.back(SLOTS), "h_ps"))
                    for j in range(B):
                        last = act.activation(h[at.s][:, j, :], both[at.s][:, j, :], ACT.Relu,
                                              scale=inverse_root[:, bass.ds(at.b * B + j, 1)])
                    last.then_inc(*act_h.did("h"))

                def copy(at):
                    act.wait_ge(*pe_h.after(at, "h_ps"))
                    if at.has(SLOTS):
                        act.wait_ge(*pe_o.after(at.back(SLOTS), "out_ps"))
                    act.copy(h_t[at.s][:, :, :], h_ps[at.s % 2][:, :, :]).then_inc(*act_t.did("h_t"))
                batches(act, g.turns, (relu, 0), (copy, 0))

            @block.vector
            def _(dve):
                def add(at):
                    dve.wait_ge(*gathered.after(at))
                    dve.wait_ge(*got.after(at))
                    if at.has(SLOTS):
                        dve.wait_ge(*act_h.after(at.back(SLOTS), "h"))
                    dve.tensor_tensor(both[at.s][:, :, :], sums[at.s][:, :, :], own[at.s][:, :, :],
                                      ALU.add).then_inc(*dve_b.did("both"))

                def add_x(at):
                    dve.wait_ge(*pe_o.after(at, "out_ps"))
                    if at.has(SLOTS):
                        dve.wait_ge(*stored.after(at.back(SLOTS)))
                    dve.tensor_tensor(new[at.s][:, :, :], out_ps[at.s % 2][:, :, :], old[at.s][:, :, :],
                                      ALU.add).then_inc(*dve_n.did("new"))
                batches(dve, g.turns, (add, 0), (add_x, 2))


def graph_layers(nc, a, T, out):
    rows = P * T

    def table(name, width, more=0):
        return nc.dram_tensor(name, (rows + more, width), F32, kind="Internal").ap()

    with ExitStack() as ctx:
        g = Graph(nc, ctx, T)
        weight = ctx.enter_context(nc.sbuf_tensor("evolved_weight", [P, D], F32))
        inverse_root = ctx.enter_context(nc.sbuf_tensor("inverse_root", [P, T], F32))
        records = table("records", FIELDS)
        sort_edges(nc, g, a["src"], a["dst"], a["edge_type_8"], a["edge_weight"], a["edge_attr_8"], records)
        read_order(nc, g, records)

        x_plus_h, conv1, conv2, sums = (table(n, D) for n in ("x_plus_h", "conv1", "conv2", "unused"))
        sums_a, sums_b = table("sums_a", D, 1), table("sums_b", D, 1)
        embed(nc, g, a["x"], a["L0_gnn_ln1_g"], a["L0_gnn_ln1_b"], x_plus_h, conv1)
        relational_sums(nc, "conv_a", g, conv1, a["L0_gnn_W1"], sums_a)
        between(nc, g, sums_a, conv1, a["L0_gnn_root1"], a["L0_gnn_b1"], a["L0_gnn_ln2_g"], a["L0_gnn_ln2_b"], conv2)
        relational_sums(nc, "conv_b", g, conv2, a["L0_gnn_W2"], sums_b)

        x1, h1, queries, keys, values = (table(n, D) for n in ("x1", "h1", "queries", "keys", "values"))
        project(nc, g, sums_b, conv2, a["L0_gnn_root2"], a["L0_gnn_b2"], x_plus_h,
                [a["L1_gnn_Wq"], a["L1_gnn_Wk"], a["L1_gnn_Wv"]], [a["L1_gnn_bq"], a["L1_gnn_bk"], a["L1_gnn_bv"]],
                x1, h1, queries, keys, values)
        edge_scores(nc, g, queries, keys)
        softmax_weights(nc, g, a["L1_gnn_edge_bias"])
        attended = table("attended", D + HEADS + 1, 1)
        row_sums(nc, "attended", g, [(values, g.src, 0, D)], D + HEADS + 1, attended, attended_message(g))
        x2, h2 = table("x2", D), table("h2", D)
        attend(nc, g, attended, h1, x1, *[a[f"L1_gnn_{n}"] for n in ("Wo", "bo", "W1", "b1", "W2", "b2", "g1", "be1", "g2", "be2")],
               x2, h2)

        wide, narrow = table("sums_wide", D + EDGE_DIM, 1), table("sums_narrow", D, 1)
        edge_sums, unit1, unit2 = table("edge_sums", EDGE_DIM), table("unit1", D), table("unit2", D)
        row_sums(nc, "passed_a", g, [(h2, g.src, 0, D), (a["edge_attr_64"], g.edge, D, D + EDGE_DIM)], D + EDGE_DIM, wide)
        for name, sums_table, width, h_in, k, h_out in (("unit_a", wide, D + EDGE_DIM, h2, 1, unit1),
                                                        ("unit_b", narrow, D, unit1, 2, unit2)):
            if k == 2:
                row_sums(nc, "passed_b", g, [(unit1, g.src, 0, D)], D, narrow)
            gated_unit(nc, name, g, sums_table, width, edge_sums, h_in,
                       *[a[f"L2_gnn_{n}{k}"] for n in ("W_msg", "Wih", "Whh", "bih", "bhh")], h_out)

        x3, evolved, sums_e = table("x3", D), table("evolved", D), table("sums_e", D, 1)
        evolve_weight(nc, g, a["L3_gnn_W0"], a["W0_t"], a["L3_gnn_gru_w_ih"], a["L3_gnn_gru_w_hh"],
                      a["L3_gnn_gru_b_ih"], a["L3_gnn_gru_b_hh"], weight, inverse_root)
        evolve_rows(nc, g, x2, unit2, weight, inverse_root, x3, evolved)
        row_sums(nc, "evolved", g, [(evolved, g.src, 0, D)], D, sums_e, weighted_message)
        finish(nc, g, sums_e, evolved, x3, inverse_root, a["L3_gnn_lin_w"], a["L3_gnn_lin_b"], out)


def laid_out(inputs):
    import numpy as np

    a = {k: np.asarray(v) for k, v in inputs.items()}
    nodes, edges = a["x"].shape[0], a["src"].shape[0]
    assert a["x"].shape[1] == D and a["edge_attr_8"].shape[1] == RELATIONS and a["edge_attr_64"].shape[1] == EDGE_DIM
    unit = SLOTS * B
    T = -(-max(nodes + 1, edges) // (P * unit)) * unit
    for k in ("x", "src", "dst", "edge_type_8", "edge_weight", "edge_attr_8", "edge_attr_64"):
        padded = np.zeros((P * T,) + a[k].shape[1:], a[k].dtype)
        padded[:len(a[k])] = a[k]
        a[k] = padded
    a["dst"][edges:] = P * T - 1
    a["W0_t"] = a["L3_gnn_W0"].T
    for k in ("L2_gnn_W_msg1", "L2_gnn_W_msg2", "L2_gnn_Wih1", "L2_gnn_Wih2", "L2_gnn_Whh1", "L2_gnn_Whh2",
              "L3_gnn_gru_w_ih", "L3_gnn_gru_w_hh", "L3_gnn_lin_w"):
        a[k] = a[k].T
    for k in ("L2_gnn_bih1", "L2_gnn_bih2", "L2_gnn_bhh1", "L2_gnn_bhh2"):
        a[k] = a[k].reshape(3, D).T
    return {k: np.ascontiguousarray(v) for k, v in a.items()}, T


def kernel(**inputs):
    import concourse.bacc as bacc
    from concourse.bass_utils import run_bass_kernel_spmd

    arrays, T = laid_out(inputs)
    nc = bacc.Bacc("TRN2", target_bir_lowering=False, num_devices=1)
    a = {k: nc.dram_tensor(f"in_{k}", v.shape, mybir.dt.from_np(v.dtype), kind="ExternalInput").ap()
         for k, v in arrays.items()}
    out = nc.dram_tensor("out", (P * T, D), F32, kind="ExternalOutput").ap()
    graph_layers(nc, a, T, out)
    result = run_bass_kernel_spmd(nc, [{f"in_{k}": v for k, v in arrays.items()}], core_ids=[0])
    return result.results[0]["out"][:inputs["x"].shape[0]]
```

```python
from contextlib import ExitStack

import concourse.bass as bass
from concourse import mybir

P = 128
D = 128
RELATIONS = 8
HEADS = 8
HEAD_DIM = D // HEADS
EDGE_DIM = 64
B = 4
SLOTS = 4
EPS = 1e-5
ROUND = 12582912.0
FAR = 1.5e38

F32 = mybir.dt.float32
F16 = mybir.dt.float16
BF16 = mybir.dt.bfloat16
I32 = mybir.dt.int32
ALU = mybir.AluOpType
ACT = mybir.ActivationFunctionType
AX = mybir.AxisListType

SRC, DST, TYPE, WEIGHT, SAME, REL, FIELDS = 0, 1, 2, 3, 4, 8, 16
RECORD = FIELDS + EDGE_DIM


class At:

    def __init__(self, turn, slot):
        self.turn, self.s = turn, slot
        self.b = turn * SLOTS + slot

    def back(self, k):
        s = (self.s - k) % SLOTS
        return At(self.turn + (self.s - k - s) // SLOTS, s)

    def has(self, k):
        return not isinstance(self.turn, int) or self.b >= k

    def columns(self):
        return bass.ds(self.b * B, B)


class Steps:

    def __init__(self, nc, name, *steps):
        self.sem, self.steps, self.at_step = nc.alloc_semaphore(name), steps, 0

    def did(self, step):
        assert self.steps[self.at_step % len(self.steps)] == step, (step, self.at_step)
        self.at_step += 1
        return self.sem, 1

    def after(self, at, step):
        return self.sem, at.b * len(self.steps) + (self.steps.index(step) + 1)


class Moves:

    def __init__(self, nc, name, n):
        self.sems, self.n = [nc.alloc_semaphore(f"{name}{s}") for s in range(SLOTS)], n

    def did(self, at):
        return self.sems[at.s], 16

    def after(self, at):
        return self.sems[at.s], (at.turn + 1) * (16 * self.n)

    def all_of(self, eng, turns):
        for sem in self.sems:
            eng.wait_ge(sem, turns * 16 * self.n)


def batches(eng, turns, *stages):
    lags = max(lag for _, lag in stages)
    peeled = 2 if lags <= SLOTS else 3

    def each(at):
        for stage, lag in stages:
            if at.has(lag) and not (isinstance(at.turn, int) and at.b - lag >= SLOTS * turns):
                stage(at.back(lag))

    for b in range(peeled * SLOTS):
        each(At(b // SLOTS, b % SLOTS))
    with eng.Fori(peeled, turns) as turn:
        for slot in range(SLOTS):
            each(At(turn, slot))
    for b in range(SLOTS * turns, SLOTS * turns + lags):
        each(At(b // SLOTS, b % SLOTS))


class Pass:

    def __init__(self, nc, name):
        self.nc, self.name, self.ctx, self.sems = nc, name, ExitStack(), []

    def __enter__(self):
        self.ctx.__enter__()
        return self

    def __exit__(self, *e):
        self.ctx.__exit__(*e)
        if e[0] is None:
            self.nc.clear_and_free_semaphores(self.sems)
            self.nc.all_engine_barrier()

    def sb(self, name, shape, dt=F32):
        return self.ctx.enter_context(self.nc.sbuf_tensor(f"{self.name}_{name}", shape, dt))

    def ps(self, name, shape, dt=F32):
        return self.ctx.enter_context(self.nc.psum_tensor(f"{self.name}_{name}", shape, dt))

    def slots(self, name, shape, dt=F32):
        return [self.sb(f"{name}{s}", shape, dt) for s in range(SLOTS)]

    def sem(self, name):
        sem = self.nc.alloc_semaphore(f"{self.name}_{name}")
        self.sems.append(sem)
        return sem

    def steps(self, name, *steps):
        out = Steps(self.nc, f"{self.name}_{name}", *steps)
        self.sems.append(out.sem)
        return out

    def moves(self, name, n):
        out = Moves(self.nc, f"{self.name}_{name}", n)
        self.sems += out.sems
        return out


class Graph:

    def __init__(self, nc, ctx, T):
        self.T, self.turns = T, T // (SLOTS * B)
        assert T % (SLOTS * B) == 0 and self.turns > 3

        def sb(name, shape, dt=F32):
            return ctx.enter_context(nc.sbuf_tensor(name, shape, dt))

        self.record = sb("record", [P, T, FIELDS])
        self.src = sb("src_of_edge", [P, T], I32)
        self.dst = sb("dst_of_edge", [P, T], I32)
        self.end = sb("end_of_node", [P, T], I32)
        self.first_end = sb("first_end", [P, 1], I32)
        self.ident = sb("ident", [P, P])
        self.before = sb("before", [P, P])
        self.ones = sb("ones", [P, P])
        self.carries = sb("carries", [P, P])
        self.far_before = sb("far_before", [P, P])
        self.far_after = sb("far_after", [P, P])
        self.in_first = sb("in_first", [P, T])
        self.in_last = sb("in_last", [P, T])
        self.far_flag = sb("far_flag", [P, T])
        self.far_flag_back = sb("far_flag_back", [P, T])
        self.attention = sb("attention", [P, T, HEADS])
        self.degree = sb("degree", [P, T])


def columns_of(table, T):
    return table[0:P * T].rearrange("(p t) f -> p t f", t=T)


def sort_edges(nc, g, src, dst, edge_type, edge_weight, edge_attr_8, edge_attr_64, records, embedding):
    T = g.T
    with Pass(nc, "sort") as w:
        dst_i, src_i, type_i = (w.sb(n, [P, T], I32) for n in ("dst_i", "src_i", "type_i"))
        weight = w.sb("weight", [P, T])
        attr = w.sb("attr", [P, T, RELATIONS])
        dst_f = w.sb("dst_f", [P, T])
        digits = w.sb("digits", [P, T, 2])
        iota_i = w.sb("iota_i", [P, max(T, P)], I32)
        iota = w.sb("iota", [P, max(T, P)], F16)
        ident16 = w.sb("ident16", [P, P], F16)
        zeros16 = w.sb("zeros16", [P, max(T, P)], F16)
        count, upto, spare = (w.sb(n, [P, T]) for n in ("count", "upto", "spare"))
        free = [w.sb(f"free{k}", [P, T]) for k in range(2)]
        loaded, made, derived, chain = (w.sem(n) for n in ("loaded", "made", "derived", "chain"))

        with nc.Block() as block:

            @block.sync
            def _(sp):
                for out, table in ((dst_i, dst), (src_i, src), (type_i, edge_type), (weight, edge_weight)):
                    sp.dma_start(out[:, :], table.rearrange("(p t) -> p t", t=T)).then_inc(loaded, 16)
                sp.dma_start(attr[:, :, :], columns_of(edge_attr_8, T)).then_inc(loaded, 16)
                sp.wait_ge(loaded, 5 * 16)

            @block.gpsimd
            def _(pool):
                pool.iota(iota_i[:, :], pattern=[[1, max(T, P)]], base=0, channel_multiplier=0).then_inc(made, 1)
                pool.memset(g.ones[:, :], 1.0).then_inc(made, 1)
                pool.wait_ge(made, 2)
                pool.affine_select(out=g.ident[:, :], in_=g.ones[:, :], pattern=[[-1, P]], compare_op=ALU.is_equal,
                                   fill=0.0, base=0, channel_multiplier=1).then_inc(made, 1)
                pool.affine_select(out=g.before[:, :], in_=g.ones[:, :], pattern=[[1, P]], compare_op=ALU.is_gt,
                                   fill=0.0, base=0, channel_multiplier=-1).then_inc(made, 1)

            @block.vector
            def _(dve):
                n = 0

                def then(ins):
                    nonlocal n
                    n += 1
                    ins.then_inc(chain, 1)
                    dve.wait_ge(chain, n)

                dve.memset(zeros16[:, :], 0.0).then_inc(derived, 1)
                dve.memset(g.record[:, :, :], 0.0).then_inc(derived, 1)
                dve.wait_ge(made, 4)
                dve.wait_ge(loaded, 5 * 16)
                dve.tensor_copy(iota[:, :], iota_i[:, :]).then_inc(derived, 1)
                dve.tensor_copy(ident16[:, :], g.ident[:, :]).then_inc(derived, 1)
                then(dve.tensor_copy(dst_f[:, :], dst_i[:, :]))
                then(dve.tensor_scalar(spare[:, :], dst_f[:, :], 1.0 / T, 0.5 / T - 0.5, ALU.mult, ALU.add))
                then(dve.tensor_scalar(upto[:, :], spare[:, :], ROUND, None, ALU.add))
                then(dve.tensor_scalar(digits[:, :, 0], upto[:, :], ROUND, None, ALU.subtract))
                then(dve.scalar_tensor_tensor(digits[:, :, 1], digits[:, :, 0], -float(T), dst_f[:, :], ALU.mult, ALU.add))
                dve.wait_ge(derived, 2)
                for field, table in ((SRC, src_i), (DST, dst_i), (TYPE, type_i), (WEIGHT, weight)):
                    dve.tensor_copy(g.record[:, :, field], table[:, :]).then_inc(derived, 1)
                dve.tensor_copy(g.record[:, :, REL:REL + RELATIONS], attr[:, :, :]).then_inc(derived, 1)

        one_hi, one_lo = w.slots("one_hi", [P, B, P], F16), w.slots("one_lo", [P, B, T], F16)
        digit = w.slots("digit", [P, B, 2])
        total = w.ps("total", [P, T])

        def one_hots(dve, digit_ready, steps, pe_used):
            def stage(at):
                dve.wait_ge(*digit_ready.after(at, "digit"))
                if at.has(SLOTS):
                    dve.wait_ge(*pe_used(at.back(SLOTS)))
                for j in range(B):
                    dve.tensor_scalar(one_hi[at.s][:, j, :], iota[:, 0:P], digit[at.s][:, j, 0:1], None, ALU.is_equal)
                    last = dve.tensor_scalar(one_lo[at.s][:, j, :], iota[:, 0:T], digit[at.s][:, j, 1:2], None,
                                             ALU.is_equal)
                last.then_inc(*steps.did("one_hots"))
            return stage

        act_c = w.steps("act_c", "digit")
        dve_c = w.steps("dve_c", "one_hots")
        pe_c = w.steps("pe_c", "counted")
        zeroed, scanned, offset = w.sem("zeroed"), w.sem("scanned"), w.sem("offset")
        with nc.Block() as block:

            @block.scalar
            def _(act):
                def stage(at):
                    if at.has(SLOTS):
                        act.wait_ge(*dve_c.after(at.back(SLOTS), "one_hots"))
                    act.copy(digit[at.s][:, :, :], digits[:, at.columns(), :]).then_inc(*act_c.did("digit"))
                batches(act, g.turns, (stage, 0))

            @block.vector
            def _(dve):
                batches(dve, g.turns, (one_hots(dve, act_c, dve_c, lambda at: pe_c.after(at, "counted")), 0))
                dve.wait_ge(*pe_c.after(At(g.turns - 1, SLOTS - 1), "counted"))
                dve.wait_ge(zeroed, 2)
                dve.tensor_copy(count[:, :], total[:, :]).then_inc(scanned, 1)
                dve.memset(spare[:, :], 1.0).then_inc(scanned, 1)
                dve.wait_ge(scanned, 2)
                dve.tensor_tensor_scan(upto[:, :], spare[:, :], count[:, :], 0.0, ALU.mult, ALU.add).then_inc(scanned, 1)
                dve.wait_ge(offset, 1)
                dve.wait_ge(scanned, 3)
                dve.tensor_scalar(dst_f[:, :], upto[:, :], total[:, 0:1], -1.0, ALU.add, ALU.add).then_inc(scanned, 1)
                dve.wait_ge(scanned, 4)
                dve.scalar_tensor_tensor(free[0][:, :], dst_f[:, :], 1.0, count[:, :], ALU.add, ALU.subtract).then_inc(scanned, 1)
                dve.tensor_scalar(spare[:, :], count[:, :], 0.0, None, ALU.is_equal).then_inc(scanned, 1)
                dve.tensor_scalar(upto[:, :], dst_f[:, :], -1.0, float(P * T), ALU.mult, ALU.add).then_inc(scanned, 1)
                dve.wait_ge(scanned, 7)
                dve.tensor_tensor(spare[:, :], spare[:, :], upto[:, :], ALU.mult).then_inc(scanned, 1)
                dve.wait_ge(scanned, 8)
                dve.tensor_tensor(g.end[:, :], spare[:, :], dst_f[:, :], ALU.add).then_inc(scanned, 1)

            @block.tensor
            def _(pe):
                pe.matmul(total[:, :], zeros16[:, 0:P], zeros16[:, 0:T], start=True, stop=False,
                          skip_group_check=True).then_inc(zeroed, 1)

                def stage(at):
                    pe.wait_ge(*dve_c.after(at, "one_hots"))
                    for j in range(B):
                        last = pe.matmul(total[:, :], one_hi[at.s][:, j, :], one_lo[at.s][:, j, :],
                                         start=False, stop=False, skip_group_check=True)
                    last.then_inc(*pe_c.did("counted"))
                batches(pe, g.turns, (stage, 0))
                pe.matmul(total[:, :], zeros16[:, 0:P], zeros16[:, 0:T], start=False, stop=True,
                          skip_group_check=True).then_inc(zeroed, 1)
                pe.wait_ge(scanned, 3)
                pe.matmul(total[:, 0:1], g.before[:, :], upto[:, T - 1:T], start=True, stop=True).then_inc(offset, 1)

        hi_t, hi_t16 = w.slots("hi_t", [P, B, P]), w.slots("hi_t16", [P, B, P], F16)
        pairs16 = w.slots("pairs16", [P, B, P], F16)
        row = w.slots("row", [P, B, RECORD])
        place, place_i = w.slots("place", [P, B]), w.slots("place_i", [P, B], I32)
        junk = w.sb("junk", [P, T])
        hi_ps = w.ps("hi_ps", [P, B, P], F16)
        same_ps = w.ps("same_ps", [P, B, P])
        more_ps = [w.ps(f"more_ps{k}", [P, T]) for k in range(2)]
        at_ps = [w.ps(f"at_ps{k}", [P, T]) for k in range(2)]
        act_d, act_r, act_t = w.steps("act_d", "digit"), w.steps("act_r", "row"), w.steps("act_t", "hi_t16", "hi_t")
        dve_a = w.steps("dve_a", "one_hots")
        dve_p = w.steps("dve_p", "pairs")
        dve_f = w.steps("dve_f", *[f"free{j}" for j in range(B)])
        dve_r = w.steps("dve_r", *[f"place{j}" for j in range(B)], "place_i")
        pe_t, pe_s = w.steps("pe_t", "hi_ps"), w.steps("pe_s", "same_ps")
        pe_r = w.steps("pe_r", *[f"{x}{j}" for j in range(B) for x in ("more", "at")])
        got, stored = w.moves("got", 1), w.moves("stored", B)
        gate = w.sem("gate")
        embed = Embed(w, g, *embedding)
        with nc.Block() as block:

            @block.sync
            def _(sp):
                embed.affine.load(sp)

                def load(at):
                    if at.has(SLOTS):
                        sp.wait_ge(*stored.after(at.back(SLOTS)))
                    sp.dma_start(row[at.s][:, :, FIELDS:RECORD],
                                 columns_of(edge_attr_64, T)[:, at.columns(), :]).then_inc(*got.did(at))
                batches(sp, g.turns, *embed.stages(sp, embed.sp), (load, 1))
                for stores in embed.stores:
                    stores.all_of(sp, g.turns)

            @block.scalar
            def _(act):
                def copy_digit(at):
                    if at.has(SLOTS):
                        act.wait_ge(*dve_a.after(at.back(SLOTS), "one_hots"))
                    act.copy(digit[at.s][:, :, :], digits[:, at.columns(), :]).then_inc(*act_d.did("digit"))

                def copy_hi(at):
                    act.wait_ge(*pe_t.after(at, "hi_ps"))
                    if at.has(SLOTS):
                        act.wait_ge(*pe_r.after(at.back(SLOTS), f"at{B - 1}"))
                    act.copy(hi_t16[at.s][:, :, :], hi_ps[:, :, :]).then_inc(*act_t.did("hi_t16"))
                    act.copy(hi_t[at.s][:, :, :], hi_ps[:, :, :]).then_inc(*act_t.did("hi_t"))

                def copy_row(at):
                    if at.has(SLOTS):
                        act.wait_ge(*stored.after(at.back(SLOTS)))
                    act.copy(row[at.s][:, :, 0:FIELDS], g.record[:, at.columns(), :]).then_inc(*act_r.did("row"))
                batches(act, g.turns, (copy_digit, 0), (copy_hi, 1), (copy_row, 2), *embed.stages(act, embed.act))

            @block.vector
            def _(dve):
                def pairs(at):
                    dve.wait_ge(*pe_s.after(at, "same_ps"))
                    if at.has(SLOTS):
                        dve.wait_ge(*pe_r.after(at.back(SLOTS), f"at{B - 1}"))
                    dve.tensor_tensor(pairs16[at.s][:, :, :], same_ps[:, :, :],
                                      g.before[:, :].unsqueeze(1).to_broadcast([P, B, P]),
                                      ALU.mult).then_inc(*dve_p.did("pairs"))

                def find(at, j):
                    dve.wait_ge(*pe_r.after(at, f"at{j}"))
                    if j:
                        dve.wait_ge(*dve_r.after(at, f"place{j - 1}"))
                    dve.tensor_tensor_reduce(out=junk[:, :], in0=at_ps[j % 2][:, :], in1=one_lo[at.s][:, j, :],
                                             scale=1.0, scalar=0.0, op0=ALU.mult, op1=ALU.add,
                                             accum_out=place[at.s][:, j:j + 1]).then_inc(*dve_r.did(f"place{j}"))
                    if j == B - 1:
                        if at.has(SLOTS):
                            dve.wait_ge(*stored.after(at.back(SLOTS)))
                        dve.wait_ge(*dve_r.after(at, f"place{B - 1}"))
                        dve.tensor_copy(place_i[at.s][:, :], place[at.s][:, :]).then_inc(*dve_r.did("place_i"))

                def column(at, j):
                    dve.wait_ge(*pe_r.after(at, f"more{j}"))
                    if j:
                        dve.wait_ge(*dve_f.after(at, f"free{j - 1}"))
                        dve.wait_ge(*pe_r.after(at, f"at{j - 1}"))
                    elif at.has(1):
                        dve.wait_ge(*dve_f.after(at.back(1), f"free{B - 1}"))
                        dve.wait_ge(*pe_r.after(at.back(1), f"at{B - 1}"))
                    dve.tensor_tensor(free[(j + 1) % 2][:, :], more_ps[j % 2][:, :], free[j % 2][:, :],
                                      ALU.add).then_inc(*dve_f.did(f"free{j}"))
                    if j:
                        find(at, j - 1)
                    elif at.has(1):
                        find(at.back(1), B - 1)
                for norm in embed.norms:
                    norm.prepare(dve)
                dve.wait_ge(embed.affine.loaded, 2 * 16)
                apply, shift_again, shift, add, moments = embed.stages(dve, embed.dve)
                columns = [(lambda at, j=j: column(at, j), 2) for j in range(B)]
                batches(dve, g.turns, columns[0],
                        (one_hots(dve, act_d, dve_a, lambda at: dve_r.after(at, f"place{B - 1}")), 0),
                        shift_again, shift, columns[1], apply, columns[2], add, columns[3], moments, (pairs, 1))
                find(At(g.turns - 1, SLOTS - 1), B - 1)

            @block.tensor
            def _(pe):
                def turn(at):
                    pe.wait_ge(*dve_a.after(at, "one_hots"))
                    if at.has(1):
                        pe.wait_ge(*act_t.after(at.back(1), "hi_t"))
                    for j in range(B):
                        last = pe.transpose(hi_ps[:, j, :], one_hi[at.s][:, j, :], ident16[:, :])
                    last.then_inc(*pe_t.did("hi_ps"))

                def same(at):
                    pe.wait_ge(*act_t.after(at, "hi_t16"))
                    if at.has(1):
                        pe.wait_ge(*dve_p.after(at.back(1), "pairs"))
                    for j in range(B):
                        last = pe.matmul(same_ps[:, j, :], hi_t16[at.s][:, j, :], hi_t16[at.s][:, j, :],
                                         start=True, stop=True)
                    last.then_inc(*pe_s.did("same_ps"))

                def lookup(at):
                    pe.wait_ge(*act_t.after(at, "hi_t"))
                    pe.wait_ge(*dve_p.after(at, "pairs"))
                    for j in range(B):
                        if j >= 2:
                            pe.wait_ge(*dve_f.after(at, f"free{j - 2}"))
                        elif at.has(1):
                            pe.wait_ge(*dve_f.after(at.back(1), f"free{j + B - 2}"))
                        pe.matmul(more_ps[j % 2][:, :], one_hi[at.s][:, j, :], one_lo[at.s][:, j, :],
                                  start=True, stop=True).then_inc(*pe_r.did(f"more{j}"))
                        if j:
                            pe.wait_ge(*dve_f.after(at, f"free{j - 1}"))
                        elif at.has(1):
                            pe.wait_ge(*dve_f.after(at.back(1), f"free{B - 1}"))
                        if j >= 2:
                            pe.wait_ge(*dve_r.after(at, f"place{j - 2}"))
                        elif at.has(1):
                            pe.wait_ge(*dve_r.after(at.back(1), f"place{j + B - 2}"))
                        pe.matmul(at_ps[j % 2][:, :], hi_t[at.s][:, j, :], free[j % 2][:, :], start=True, stop=False)
                        pe.matmul(at_ps[j % 2][:, :], pairs16[at.s][:, j, :], one_lo[at.s][:, j, :],
                                  start=False, stop=True).then_inc(*pe_r.did(f"at{j}"))
                batches(pe, g.turns, (same, 1), (lookup, 2), (turn, 0))

            @block.gpsimd
            def _(pool):
                def scatter(at):
                    pool.wait_ge(*act_r.after(at, "row"))
                    pool.wait_ge(*got.after(at))
                    pool.wait_ge(*dve_r.after(at, "place_i"))
                    pool.sem_inc(gate, 1)
                    for j in range(B):
                        pool.indirect_dma_start(
                            out=records[:, :], out_offset=bass.IndirectOffsetOnAxis(ap=place_i[at.s][:, j:j + 1], axis=0),
                            in_=row[at.s][:, j, :], in_offset=None).then_inc(*stored.did(at))
                batches(pool, g.turns, *embed.stages(pool, embed.pool), (scatter, 3))
                stored.all_of(pool, g.turns)


def read_order(nc, g, records):
    T = g.T
    with Pass(nc, "order") as w:
        loaded, chain, ready, spread = (w.sem(n) for n in ("loaded", "chain", "ready", "spread"))
        spare, other = w.sb("spare", [P, T]), w.sb("other", [P, T])
        place_i = w.sb("place_i", [P, 1], I32)
        place = w.sb("place", [P, 1])
        number = w.sb("number", [P, 1])
        diag = [w.sb(f"diag{k}", [P, P]) for k in range(2)]
        mask = w.sb("mask", [P, P])
        after = w.sb("after", [P, P])
        first_ps, last_ps = w.ps("first_ps", [P, P]), w.ps("last_ps", [P, P])
        with nc.Block() as block:

            @block.sync
            def _(sp):
                sp.dma_start(g.record[:, :, :], columns_of(records, T)[:, :, 0:FIELDS]).then_inc(loaded, 16)

            @block.gpsimd
            def _(pool):
                pool.iota(place_i[:, :], pattern=[[1, 1]], base=-1, channel_multiplier=T).then_inc(ready, 1)
                pool.affine_select(out=after[:, :], in_=g.ones[:, :], pattern=[[-1, P]], compare_op=ALU.is_gt,
                                   fill=0.0, base=0, channel_multiplier=1).then_inc(ready, 1)

            @block.tensor
            def _(pe):
                pe.wait_ge(spread, 1)
                pe.matmul(first_ps[:, :], g.ones[:, :], diag[0][:, :], start=True, stop=True)
                pe.matmul(last_ps[:, :], g.ones[:, :], diag[1][:, :], start=True, stop=True).then_inc(spread, 1)

            @block.vector
            def _(dve):
                n = 0

                def then(ins):
                    nonlocal n
                    n += 1
                    ins.then_inc(chain, 1)
                    dve.wait_ge(chain, n)

                dve.wait_ge(loaded, 16)
                dve.wait_ge(ready, 2)
                target = g.record[:, :, DST]
                first, last = g.record[:, 0, DST:DST + 1], g.record[:, T - 1, DST:DST + 1]
                then(dve.tensor_copy(g.src[:, :], g.record[:, :, SRC]))
                then(dve.tensor_copy(g.dst[:, :], target))
                then(dve.memset(g.record[:, 0, SAME:SAME + 1], 0.0))
                then(dve.tensor_tensor(g.record[:, 1:T, SAME], g.record[:, 1:T, DST], g.record[:, 0:T - 1, DST],
                                       ALU.is_equal))
                then(dve.tensor_scalar(g.far_flag[:, :], g.record[:, :, SAME], 1.0, FAR, ALU.subtract, ALU.mult))
                then(dve.tensor_copy(g.far_flag_back[:, 0:T - 1], g.far_flag[:, 1:T]))
                then(dve.memset(g.far_flag_back[:, T - 1:T], -FAR))
                then(dve.tensor_scalar(spare[:, :], target, first, None, ALU.is_equal))
                then(dve.tensor_scalar(other[:, :], target, last, None, ALU.is_equal))
                then(dve.tensor_reduce(number[:, :], spare[:, :], AX.X, ALU.add))
                then(dve.tensor_scalar(g.in_first[:, :], spare[:, :], 1.0, FAR, ALU.subtract, ALU.mult))
                then(dve.tensor_scalar(g.in_last[:, :], other[:, :], 1.0, FAR, ALU.subtract, ALU.mult))
                then(dve.tensor_copy(place[:, :], place_i[:, :]))
                then(dve.tensor_tensor(g.first_end[:, :], place[:, :], number[:, :], ALU.add))
                then(dve.tensor_scalar(diag[0][:, :], g.ident[:, :], first, None, ALU.mult))
                dve.tensor_scalar(diag[1][:, :], g.ident[:, :], last, None, ALU.mult).then_inc(spread, 1)
                dve.wait_ge(spread, 2)
                then(dve.scalar_tensor_tensor(g.carries[:, :], first_ps[:, :], last, g.before[:, :],
                                              ALU.is_equal, ALU.mult))
                then(dve.scalar_tensor_tensor(mask[:, :], last_ps[:, :], first, after[:, :], ALU.is_equal, ALU.mult))
                then(dve.tensor_scalar(g.far_before[:, :], mask[:, :], 1.0, FAR, ALU.subtract, ALU.mult))
                then(dve.scalar_tensor_tensor(mask[:, :], first_ps[:, :], last, g.before[:, :], ALU.is_equal, ALU.mult))
                then(dve.tensor_scalar(g.far_after[:, :], mask[:, :], 1.0, FAR, ALU.subtract, ALU.mult))


def gatherer(pool, w, g, gate, gathered, free_after, *sources):
    copied = w.steps("numbers", *[f"numbers{k}" for k in range(len(sources))])
    numbers = [w.slots(f"numbers{k}_", [P, B], I32) for k in range(len(sources))]

    def stage(at):
        if at.has(SLOTS):
            pool.wait_ge(*gathered.after(at.back(SLOTS)))
            for wait in free_after(at.back(SLOTS)):
                pool.wait_ge(*wait)
            pool.sem_inc(gate, 1)
        for k, (_, rows, _, _, _) in enumerate(sources):
            pool.tensor_copy(numbers[k][at.s][:, :], rows[:, at.columns()]).then_inc(*copied.did(f"numbers{k}"))
        pool.wait_ge(*copied.after(at, f"numbers{len(sources) - 1}"))
        pool.sem_inc(gate, 1)
        for j in range(B):
            for k, (table, _, slots, a, b) in enumerate(sources):
                pool.indirect_dma_start(
                    out=slots[at.s][:, j, a:b], out_offset=None, in_=table[:, :],
                    in_offset=bass.IndirectOffsetOnAxis(ap=numbers[k][at.s][:, j:j + 1], axis=0),
                ).then_inc(*gathered.did(at))
    return stage


def record_copier(act, g, fields, copied, free_after):

    def stage(at):
        if at.has(SLOTS):
            act.wait_ge(*free_after(at.back(SLOTS)))
        act.copy(fields[at.s][:, :, :], g.record[:, at.columns(), :]).then_inc(*copied.did("record"))
    return stage


def running_sums(dve, at, sums, fields, message, did, after):
    for j in range(B):
        if j:
            before = sums[at.s][:, j - 1, :]
            dve.wait_ge(*after(at, f"sum{j - 1}"))
        else:
            before = sums[at.s - 1][:, B - 1, :]
            if at.has(1):
                dve.wait_ge(*after(at.back(1), f"sum{B - 1}"))
        dve.scalar_tensor_tensor(sums[at.s][:, j, :], before, fields[at.s][:, j, SAME:SAME + 1], message(j),
                                 ALU.mult, ALU.add).then_inc(*did(f"sum{j}"))


SUMS = tuple(f"sum{j}" for j in range(B))


def carry_over(nc, w, g, tail, sums_table, width, carry_ps):
    fixed = w.sb("fixed", [P, width])
    summed, got, fix, put = (w.sem(n) for n in ("summed", "got", "fix", "put"))
    with nc.Block() as block:

        @block.tensor
        def _(pe):
            pe.matmul(carry_ps, g.carries[:, :], tail, start=True, stop=True).then_inc(summed, 1)

        @block.gpsimd
        def _(pool):
            pool.indirect_dma_start(out=fixed[:, :], out_offset=None, in_=sums_table[:, :],
                                    in_offset=bass.IndirectOffsetOnAxis(ap=g.first_end[:, :], axis=0)).then_inc(got, 16)
            pool.wait_ge(fix, 1)
            pool.indirect_dma_start(out=sums_table[:, :],
                                    out_offset=bass.IndirectOffsetOnAxis(ap=g.first_end[:, :], axis=0),
                                    in_=fixed[:, :], in_offset=None).then_inc(put, 16)
            pool.wait_ge(put, 16)

        @block.vector
        def _(dve):
            dve.wait_ge(got, 16)
            dve.wait_ge(summed, 1)
            dve.tensor_tensor(fixed[:, :], carry_ps, fixed[:, :], ALU.add).then_inc(fix, 1)


def clear_row(nc, w, g, table, width):
    zero = w.sb("zero", [1, width])
    set_, stored = w.sem("zero_set"), w.sem("zero_stored")
    with nc.Block() as block:

        @block.vector
        def _(dve):
            dve.memset(zero[:, :], 0.0).then_inc(set_, 1)

        @block.sync
        def _(sp):
            sp.wait_ge(set_, 1)
            sp.dma_start(table[P * g.T:P * g.T + 1, :], zero[:, :]).then_inc(stored, 16)
            sp.wait_ge(stored, 16)


def relational_sums(nc, name, g, table, weights, sums_table):
    T = g.T
    groups = ((2, 5), (5, RELATIONS))
    with Pass(nc, name) as w:
        clear_row(nc, w, g, sums_table, D)
        wide = w.sb("weights", [P, RELATIONS, D])
        rows, rows_t = w.slots("rows", [P, B, D]), w.slots("rows_t", [P, B, D])
        fields, sums = w.slots("fields", [P, B, FIELDS]), w.slots("sums", [P, B, D])
        starts, aside = w.slots("starts", [P, B, D]), w.slots("aside", [P, B, D])
        messages = w.slots("messages", [P, B, D])
        t_ps = [w.ps(f"t_ps{s}", [P, B, D]) for s in range(2)]
        scaled_ps = [w.ps(f"scaled_ps{k}", [P, 2, 2, D]) for k in range(2)]
        y_ps = [[w.ps(f"y_ps{h}{k}", [P, 3, D]) for k in range(2)] for h in range(2)]
        loaded, cleared, gate = w.sem("loaded"), w.sem("cleared"), w.sem("gate")
        gathered, stored = w.moves("gathered", B), w.moves("stored", 1)
        act_s = w.steps("act", "record")
        act_t = w.steps("act_t", "rows_t")
        pe_t = w.steps("pe_t", "t_ps")
        pe_y = w.steps("pe_y", *[f"{n}{c}" for c in (0, 2) for n in ("scaled", "first", "second")])
        names = []
        for c in (0, 2):
            for h in range(2):
                names += [f"part{c + k}_{r}" for r in range(*groups[h]) for k in range(2)]
        dve_m = w.steps("dve_m", *names)
        dve_s = w.steps("dve_s", *SUMS)
        act_r = w.steps("act_r", "start0", "aside0", "start2", "aside2")
        pool_m = w.steps("pool_m", "message")
        with nc.Block() as block:

            @block.sync
            def _(sp):
                sp.dma_start(wide[:, :, :], weights.rearrange("r k f -> k r f")).then_inc(loaded, 16)

                def store(at):
                    sp.wait_ge(*dve_s.after(at, SUMS[-1]))
                    sp.dma_start(columns_of(sums_table, T)[:, at.columns(), :], sums[at.s][:, :, :]).then_inc(*stored.did(at))
                batches(sp, g.turns, (store, 0))
                stored.all_of(sp, g.turns)

            @block.gpsimd
            def _(pool):
                gather = gatherer(pool, w, g, gate, gathered, lambda at: [pe_t.after(at, "t_ps")],
                                  (table, g.src, rows, 0, D))

                def add_aside(at):
                    pool.wait_ge(*act_r.after(at, "aside2"))
                    pool.wait_ge(*dve_m.after(at, f"part{B - 1}_{RELATIONS - 1}"))
                    pool.tensor_tensor(messages[at.s][:, :, :], messages[at.s][:, :, :], aside[at.s][:, :, :],
                                       ALU.add).then_inc(*pool_m.did("message"))
                batches(pool, g.turns, (gather, 0), (add_aside, 3))

            @block.tensor
            def _(pe):
                def turn(at):
                    pe.wait_ge(*gathered.after(at))
                    if at.has(2):
                        pe.wait_ge(*act_t.after(at.back(2), "rows_t"))
                    for j in range(B):
                        last = pe.transpose(t_ps[at.s % 2][:, j, :], rows[at.s][:, j, :], g.ident[:, :])
                    last.then_inc(*pe_t.did("t_ps"))

                def products(at):
                    pe.wait_ge(loaded, 16)
                    pe.wait_ge(*act_t.after(at, "rows_t"))
                    for c in (0, 2):
                        if at.has(1):
                            pe.wait_ge(*act_r.after(at.back(1), f"aside{c}"))
                        for k in range(2):
                            last = pe.matmul(scaled_ps[c // 2][:, k, :, :], rows_t[at.s][:, c + k, :],
                                             wide[:, 0:2, :], start=True, stop=True, skip_group_check=True)
                        last.then_inc(*pe_y.did(f"scaled{c}"))
                        for h, (a, b) in enumerate(groups):
                            done = f"part{(c + 2) % 4 + 1}_{b - 1}"
                            if c:
                                pe.wait_ge(*dve_m.after(at, done))
                            elif at.has(1):
                                pe.wait_ge(*dve_m.after(at.back(1), done))
                            for k in range(2):
                                last = pe.matmul(y_ps[h][k][:, :, :], rows_t[at.s][:, c + k, :],
                                                 wide[:, a:b, :], start=True, stop=True)
                            last.then_inc(*pe_y.did(f"{('first', 'second')[h]}{c}"))
                batches(pe, g.turns, (turn, 0), (products, 1))

            @block.scalar
            def _(act):
                def transposed(at):
                    act.wait_ge(*pe_t.after(at, "t_ps"))
                    if at.has(SLOTS):
                        act.wait_ge(*pe_y.after(at.back(SLOTS), "second2"))
                    act.copy(rows_t[at.s][:, :, :], t_ps[at.s % 2][:, :, :]).then_inc(*act_t.did("rows_t"))

                def scaled(at):
                    if at.has(SLOTS):
                        act.wait_ge(*pool_m.after(at.back(SLOTS), "message"))
                    for c in (0, 2):
                        act.wait_ge(*pe_y.after(at, f"scaled{c}"))
                        for r, name_, out in ((0, "start", starts), (1, "aside", aside)):
                            for k in range(2):
                                last = act.activation(out[at.s][:, c + k, :], scaled_ps[c // 2][:, k, r, :], ACT.Copy,
                                                      scale=fields[at.s][:, c + k, REL + r:REL + r + 1])
                            last.then_inc(*act_r.did(f"{name_}{c}"))
                batches(act, g.turns, (scaled, 1), (record_copier(act, g, fields, act_s, lambda at: dve_s.after(at, SUMS[-1])), 0),
                        (transposed, 0))

            @block.vector
            def _(dve):
                dve.memset(sums[SLOTS - 1][:, B - 1, :], 0.0).then_inc(cleared, 1)
                dve.wait_ge(cleared, 1)

                def relations(at):
                    dve.wait_ge(*act_s.after(at, "record"))
                    for c in (0, 2):
                        for h, (a, b) in enumerate(groups):
                            dve.wait_ge(*pe_y.after(at, f"{('first', 'second')[h]}{c}"))
                            for rel in range(a, b):
                                for k in range(2):
                                    j = c + k
                                    message = messages[at.s][:, j, :]
                                    if rel == 2:
                                        before = starts[at.s][:, j, :]
                                        dve.wait_ge(*act_r.after(at, f"start{c}"))
                                    else:
                                        before = message
                                        dve.wait_ge(*dve_m.after(at, f"part{j}_{rel - 1}"))
                                    dve.scalar_tensor_tensor(
                                        message, y_ps[h][k][:, rel - a, :], fields[at.s][:, j, REL + rel:REL + rel + 1],
                                        before, ALU.mult, ALU.add).then_inc(*dve_m.did(f"part{j}_{rel}"))

                def add_up(at):
                    dve.wait_ge(*pool_m.after(at, "message"))
                    if at.has(SLOTS):
                        dve.wait_ge(*stored.after(at.back(SLOTS)))
                    running_sums(dve, at, sums, fields, lambda j: messages[at.s][:, j, :], dve_s.did, dve_s.after)
                batches(dve, g.turns, (add_up, 3), (relations, 0))
        carry_over(nc, w, g, sums[SLOTS - 1][:, B - 1, :], sums_table, D, t_ps[0][:, 0, :])


def row_sums(nc, name, g, sources, loads, width, sums_table, product=None):
    T = g.T
    with Pass(nc, name) as w:
        clear_row(nc, w, g, sums_table, width)
        got_width = max(source[-1] for source in sources + loads)
        rows = w.slots("rows", [P, B, got_width])
        messages = w.slots("messages", [P, B, width]) if product else rows
        fields, sums = w.slots("fields", [P, B, FIELDS]), w.slots("sums", [P, B, width])
        cleared, gate = w.sem("cleared"), w.sem("gate")
        gathered, stored = w.moves("gathered", B * len(sources)), w.moves("stored", 1)
        got = w.moves("got", len(loads))
        act_s = w.steps("act", "record")
        dve_s = w.steps("dve_s", *SUMS)
        dve_m = w.steps("dve_m", "message")

        def used(at):
            return dve_m.after(at, "message") if product else dve_s.after(at, SUMS[-1])

        with nc.Block() as block:

            @block.sync
            def _(sp):
                def load(at):
                    if at.has(SLOTS):
                        sp.wait_ge(*used(at.back(SLOTS)))
                    for table, a, b in loads:
                        sp.dma_start(rows[at.s][:, :, a:b], table[:, at.columns(), :]).then_inc(*got.did(at))

                def store(at):
                    sp.wait_ge(*dve_s.after(at, SUMS[-1]))
                    sp.dma_start(columns_of(sums_table, T)[:, at.columns(), :], sums[at.s][:, :, :]).then_inc(*stored.did(at))
                batches(sp, g.turns, (store, 2), *([(load, 0)] if loads else []))
                stored.all_of(sp, g.turns)

            if sources:
                @block.gpsimd
                def _(pool):
                    batches(pool, g.turns, (gatherer(
                        pool, w, g, gate, gathered, lambda at: [used(at)],
                        *[(table, numbers, rows, a, b) for table, numbers, a, b in sources]), 0))

            @block.scalar
            def _(act):
                batches(act, g.turns, (record_copier(act, g, fields, act_s, lambda at: dve_s.after(at, SUMS[-1])), 0))

            @block.vector
            def _(dve):
                dve.memset(sums[SLOTS - 1][:, B - 1, :], 0.0).then_inc(cleared, 1)
                dve.wait_ge(cleared, 1)

                def stage(at):
                    dve.wait_ge(*act_s.after(at, "record"))
                    if sources:
                        dve.wait_ge(*gathered.after(at))
                    if loads:
                        dve.wait_ge(*got.after(at))
                    if product:
                        if at.has(SLOTS):
                            dve.wait_ge(*dve_s.after(at.back(SLOTS), SUMS[-1]))
                        product(dve, at, rows[at.s], fields[at.s], messages[at.s]).then_inc(*dve_m.did("message"))
                        dve.wait_ge(*dve_m.after(at, "message"))
                    if at.has(SLOTS):
                        dve.wait_ge(*stored.after(at.back(SLOTS)))
                    running_sums(dve, at, sums, fields, lambda j: messages[at.s][:, j, :], dve_s.did, dve_s.after)
                batches(dve, g.turns, (stage, 0))
        carry_over(nc, w, g, sums[SLOTS - 1][:, B - 1, :], sums_table, width, w.ps("carry_ps", [P, width])[:, :])


def attended_message(g):

    def product(dve, at, rows, fields, message):
        share = g.attention[:, at.columns(), :]
        dve.tensor_tensor(message[:, :, 0:D].rearrange("p b (h d) -> p b h d", h=HEADS),
                          rows[:, :, :].rearrange("p b (h d) -> p b h d", h=HEADS),
                          share.unsqueeze(3).to_broadcast([P, B, HEADS, HEAD_DIM]), ALU.mult)
        dve.tensor_copy(message[:, :, D:D + HEADS], share)
        return dve.tensor_copy(message[:, :, D + HEADS:D + HEADS + 1], fields[:, :, WEIGHT:WEIGHT + 1])
    return product


def weighted_message(dve, at, rows, fields, message):
    for j in range(B):
        last = dve.tensor_scalar(message[:, j, :], rows[:, j, :], fields[:, j, WEIGHT:WEIGHT + 1], None, ALU.mult)
    return last


def edge_scores(nc, g, queries, keys_values, edge_values):
    T = g.T
    with Pass(nc, "scores") as w:
        q, kv = w.slots("q", [P, B, D]), w.slots("kv", [P, B, 2 * D])
        both = w.slots("both", [P, B, D])
        gate, gathered, stored = w.sem("gate"), w.moves("gathered", 2 * B), w.moves("stored", 1)
        dve_s = w.steps("dve", "product", "score")
        with nc.Block() as block:

            @block.gpsimd
            def _(pool):
                batches(pool, g.turns, (gatherer(pool, w, g, gate, gathered,
                                                 lambda at: [dve_s.after(at, "product"), stored.after(at)],
                                                 (queries, g.dst, q, 0, D), (keys_values, g.src, kv, 0, 2 * D)), 0))

            @block.sync
            def _(sp):
                def store(at):
                    sp.wait_ge(*gathered.after(at))
                    sp.dma_start(columns_of(edge_values, T)[:, at.columns(), :], kv[at.s][:, :, D:2 * D]).then_inc(*stored.did(at))
                batches(sp, g.turns, (store, 0))
                stored.all_of(sp, g.turns)

            @block.vector
            def _(dve):
                def multiply(at):
                    dve.wait_ge(*gathered.after(at))
                    if at.has(SLOTS):
                        dve.wait_ge(*dve_s.after(at.back(SLOTS), "score"))
                    dve.tensor_tensor(both[at.s][:, :, :], q[at.s][:, :, :], kv[at.s][:, :, 0:D],
                                      ALU.mult).then_inc(*dve_s.did("product"))
                    dve.wait_ge(*dve_s.after(at, "product"))
                    dve.tensor_reduce(g.attention[:, at.columns(), :].rearrange("p b h -> p (b h)"),
                                      both[at.s][:, :, :].rearrange("p b (h d) -> p (b h) d", h=HEADS),
                                      AX.X, ALU.add).then_inc(*dve_s.did("score"))
                batches(dve, g.turns, (multiply, 0))


def softmax_weights(nc, g, edge_bias):
    T = g.T
    with Pass(nc, "softmax") as w:
        bias = w.sb("bias", [P, HEADS, HEADS])
        is_type = w.sb("is_type", [P, T])
        forth, back = w.sb("forth", [P, T]), w.sb("back", [P, T])
        diag, seen = w.sb("diag", [P, P]), w.sb("seen", [P, P])
        carry = w.sb("carry", [P, 1])
        loaded, chain, spread, ready = (w.sem(n) for n in ("loaded", "chain", "spread", "ready"))
        tails_ps = w.ps("tails_ps", [P, P])
        with nc.Block() as block:

            @block.sync
            def _(sp):
                sp.dma_start(bias[:, :, :], edge_bias.partition_broadcast(P)).then_inc(loaded, 16)

            @block.tensor
            def _(pe):
                for n in range(2 * HEADS):
                    pe.wait_ge(ready, n + 1)
                    pe.matmul(tails_ps[:, :], g.ones[:, :], diag[:, :], start=True, stop=True).then_inc(spread, 1)

            @block.vector
            def _(dve):
                n = 0

                def then(ins):
                    nonlocal n
                    n += 1
                    ins.then_inc(chain, 1)
                    dve.wait_ge(chain, n)

                dve.wait_ge(loaded, 16)
                then(dve.tensor_scalar(g.attention[:, :, :], g.attention[:, :, :], HEAD_DIM ** -0.5, None, ALU.mult))
                for kind in range(8):
                    then(dve.tensor_scalar(is_type[:, :], g.record[:, :, TYPE], float(kind), None, ALU.is_equal))
                    for h in range(HEADS):
                        score = g.attention[:, :, h]
                        then(dve.scalar_tensor_tensor(score, is_type[:, :], bias[:, kind, h:h + 1], score,
                                                      ALU.mult, ALU.add))
                seen_tails = 0
                for h in range(HEADS):
                    score = g.attention[:, :, h]
                    then(dve.tensor_tensor_scan(forth[:, :], g.far_flag[:, :], score, -FAR, ALU.add, ALU.max))
                    then(dve.tensor_tensor_scan(back[:, ::-1], g.far_flag_back[:, ::-1], score[:, ::-1], -FAR,
                                                ALU.add, ALU.max))
                    for largest, end, far, where in ((forth, T - 1, g.far_before, g.in_first),
                                                     (back, 0, g.far_after, g.in_last)):
                        dve.tensor_scalar(diag[:, :], g.ident[:, :], largest[:, end:end + 1], None,
                                          ALU.mult).then_inc(ready, 1)
                        seen_tails += 1
                        dve.wait_ge(spread, seen_tails)
                        then(dve.tensor_tensor(seen[:, :], tails_ps[:, :], far[:, :], ALU.add))
                        then(dve.tensor_reduce(carry[:, :], seen[:, :], AX.X, ALU.max))
                        then(dve.scalar_tensor_tensor(largest[:, :], where[:, :], carry[:, 0:1], largest[:, :],
                                                      ALU.add, ALU.max))
                    then(dve.tensor_tensor(forth[:, :], forth[:, :], back[:, :], ALU.max))
                    then(dve.tensor_tensor(score, score, forth[:, :], ALU.subtract))
                dve.wait_ge(chain, n)
                dve.sem_inc(ready, 1)

            @block.scalar
            def _(act):
                act.wait_ge(ready, 2 * HEADS + 1)
                act.activation(g.attention[:, :, :], g.attention[:, :, :], ACT.Exp).then_inc(spread, 1)
                act.wait_ge(spread, 2 * HEADS + 1)


class Norm:

    def __init__(self, w, name, factors=None):
        self.factors = factors
        self.stats = w.slots(f"{name}_stats", [P, B, 6])
        self.moments = w.slots(f"{name}_moments", [P, B, 2])
        self.variance = w.slots(f"{name}_variance", [P, B])
        self.scale = w.slots(f"{name}_scale", [P, B])
        self.shift = w.slots(f"{name}_shift", [P, B])
        self.minus_half = w.sb(f"{name}_minus_half", [P, B])
        self.gate, self.set = w.sem(f"{name}_gate"), w.sem(f"{name}_set")
        self.measured = w.steps(f"{name}_measured", "stats", "moments", "variance")
        self.rooted = w.steps(f"{name}_rooted", "scale")
        self.shifted = w.steps(f"{name}_shifted", *(["shift"] if factors is None else ["factor", "shift"]))

    def prepare(self, dve):
        dve.memset(self.minus_half[:, :], -0.5).then_inc(self.set, 1)

    def take_stats(self, dve, at, rows):
        for j in range(B):
            last = dve.bn_stats(self.stats[at.s][:, j, :], rows[:, j, :])
        last.then_inc(*self.measured.did("stats"))

    def aggregate(self, dve, at):
        dve.wait_ge(*self.measured.after(at, "stats"))
        dve.sem_inc(self.gate, 1)
        for j in range(B):
            last = dve.bn_aggr(self.moments[at.s][:, j, :], self.stats[at.s][:, j, :])
        last.then_inc(*self.measured.did("moments"))

    def add_eps(self, dve, at):
        dve.wait_ge(*self.measured.after(at, "moments"))
        if at.has(SLOTS):
            dve.wait_ge(*self.rooted.after(at.back(SLOTS), "scale"))
        dve.tensor_scalar(self.variance[at.s][:, :], self.moments[at.s][:, :, 1], EPS, None,
                          ALU.add).then_inc(*self.measured.did("variance"))

    def take_moments(self, dve, at, rows):
        self.take_stats(dve, at, rows)
        self.aggregate(dve, at)
        self.add_eps(dve, at)

    def root(self, pool, at, scale_used):
        if at.has(SLOTS):
            pool.wait_ge(*scale_used(at.back(SLOTS)))
        else:
            pool.wait_ge(self.set, 1)
        pool.wait_ge(*self.measured.after(at, "variance"))
        pool.tensor_tensor(self.scale[at.s][:, :], self.variance[at.s][:, :], self.minus_half[:, :],
                           ALU.pow).then_inc(*self.rooted.did("scale"))

    def make_shift(self, dve, at, shift_used):
        dve.wait_ge(*self.rooted.after(at, "scale"))
        if at.has(SLOTS):
            dve.wait_ge(*shift_used(at.back(SLOTS)))
        if self.factors is not None:
            dve.tensor_tensor(self.scale[at.s][:, :], self.scale[at.s][:, :], self.factors[:, at.columns()],
                              ALU.mult).then_inc(*self.shifted.did("factor"))
            dve.wait_ge(*self.shifted.after(at, "factor"))
        dve.scalar_tensor_tensor(self.shift[at.s][:, :], self.moments[at.s][:, :, 0], -1.0, self.scale[at.s][:, :],
                                 ALU.mult, ALU.mult).then_inc(*self.shifted.did("shift"))

    def relu(self, act, at, out, rows):
        act.wait_ge(*self.shifted.after(at, "shift"))
        for j in range(B):
            last = act.activation(out[:, j, :], rows[:, j, :], ACT.Relu, bias=self.shift[at.s][:, j:j + 1],
                                  scale=self.scale[at.s][:, j:j + 1])
        return last


class Affine:

    def __init__(self, w, name, norm, gain, offset):
        self.norm, self.source = norm, (gain, offset)
        self.gain, self.offset = w.sb(f"{name}_gain", [P, D]), w.sb(f"{name}_offset", [P, D])
        self.loaded = w.sem(f"{name}_loaded")
        self.scaled, self.gained = w.steps(f"{name}_scaled", "scaled"), w.steps(f"{name}_gained", "gained")
        self.moved = w.steps(f"{name}_moved", "offset")

    def load(self, sp):
        for out, vector in zip((self.gain, self.offset), self.source):
            sp.dma_start(out[:, :], vector.partition_broadcast(P)).then_inc(self.loaded, 16)

    def scale(self, act, at, out, rows):
        act.wait_ge(*self.norm.shifted.after(at, "shift"))
        for j in range(B):
            last = act.activation(out[:, j, :], rows[:, j, :], ACT.Identity, bias=self.norm.shift[at.s][:, j:j + 1],
                                  scale=self.norm.scale[at.s][:, j:j + 1])
        last.then_inc(*self.scaled.did("scaled"))

    def apply_gain(self, dve, at, out):
        dve.wait_ge(*self.scaled.after(at, "scaled"))
        dve.tensor_tensor(out[:, :, :], out[:, :, :], over_batch(self.gain), ALU.mult).then_inc(*self.gained.did("gained"))

    def apply_offset(self, dve, at, out):
        dve.wait_ge(*self.gained.after(at, "gained"))
        dve.tensor_tensor(out[:, :, :], out[:, :, :], over_batch(self.offset), ALU.add).then_inc(*self.moved.did("offset"))


def over_batch(vector):
    return vector[:, :].unsqueeze(1).to_broadcast([P, B, vector.shape[-1]])


def transpose_rows(pe, g, out, rows, width=D):
    for j in range(B):
        last = pe.transpose(out[:, j, :], rows[:, j, :], g.ident[:, :])
    return last


class Bias:

    def __init__(self, w, name, width):
        self.width = width
        self.raw, self.sum = w.sb(f"{name}_raw", [3, width]), w.sb(f"{name}_sum", [3, width])
        self.part, self.parts = w.sb(f"{name}_part", [3, width], BF16), w.sb(f"{name}_parts", [3, width], BF16)
        self.ones = w.sb(f"{name}_ones", [3, P], BF16)
        self.loaded, self.split_up, self.ready = (w.sem(f"{name}_{n}") for n in ("loaded", "split_up", "ready"))
        self.loads = 0

    def load(self, sp, vector, first=0, times=1):
        n = vector.shape[0]
        for k in range(times):
            sp.dma_start(self.raw[:, first + k * n:first + (k + 1) * n],
                         vector.partition_broadcast(3)).then_inc(self.loaded, 16)
        self.loads += times

    def split(self, dve, g):
        n = 0

        def then(ins):
            nonlocal n
            n += 1
            ins.then_inc(self.split_up, 1)
            dve.wait_ge(self.split_up, n)

        dve.wait_ge(self.loaded, 16 * self.loads)
        then(dve.memset(self.ones[:, :], 1.0))
        then(dve.memset(self.sum[:, :], 0.0))
        for k in range(3):
            then(dve.tensor_copy(self.part[:, :], self.raw[:, :]))
            then(dve.tensor_tensor(self.raw[:, :], self.raw[:, :], self.part[:, :], ALU.subtract))
            then(dve.scalar_tensor_tensor(self.sum[:, :], self.part[:, :], g.ident[0:3, k:k + 1], self.sum[:, :],
                                          ALU.mult, ALU.add))
        dve.tensor_copy(self.parts[:, :], self.sum[:, :]).then_inc(self.ready, 1)

    def start(self, pe, out):
        return pe.matmul(out, self.ones[:, :], self.parts[:, :], start=True, stop=False, skip_group_check=True)


def rows_times(pe, out, rows_t, weight, bias):
    bias.start(pe, out[:, :, :].rearrange("p b f -> p (b f)"))
    for j in range(B):
        last = pe.matmul(out[:, j, :], rows_t[:, j, :], weight, start=False, stop=True, skip_group_check=True)
    return last


class Embed:

    def __init__(self, w, g, x, gain, offset, x_plus_h, table):
        T = self.T = g.T
        rows, h, both = w.slots("rows", [P, B, D]), w.slots("h", [P, B, D]), w.slots("both", [P, B, D])
        out, inner = w.slots("out", [P, B, D]), w.slots("inner", [P, B, D])
        first, second = Norm(w, "first"), Norm(w, "second")
        affine = self.affine = Affine(w, "affine", second, gain, offset)
        got, stored, stored_out = w.moves("got_x", 1), w.moves("stored_both", 1), w.moves("stored_out", 1)
        act_h, act_o = w.steps("act_h", "h"), w.steps("act_o", "out")
        dve_b = w.steps("dve_b", "both")
        self.norms, self.stores = (first, second), (stored, stored_out)

        def load(sp, at):
            if at.has(SLOTS):
                sp.wait_ge(*dve_b.after(at.back(SLOTS), "both"))
            sp.dma_start(rows[at.s][:, :, :], columns_of(x, T)[:, at.columns(), :]).then_inc(*got.did(at))

        def store_both(sp, at):
            sp.wait_ge(*dve_b.after(at, "both"))
            sp.dma_start(columns_of(x_plus_h, T)[:, at.columns(), :], both[at.s][:, :, :]).then_inc(*stored.did(at))

        def store_out(sp, at):
            sp.wait_ge(*act_o.after(at, "out"))
            sp.dma_start(columns_of(table, T)[:, at.columns(), :], out[at.s][:, :, :]).then_inc(*stored_out.did(at))

        def moments(dve, at):
            dve.wait_ge(*got.after(at))
            first.take_moments(dve, at, rows[at.s])

        def shift(dve, at):
            first.make_shift(dve, at, lambda a: act_h.after(a, "h"))

        def add(dve, at):
            dve.wait_ge(*act_h.after(at, "h"))
            if at.has(SLOTS):
                dve.wait_ge(*stored.after(at.back(SLOTS)))
            dve.tensor_tensor(both[at.s][:, :, :], rows[at.s][:, :, :], h[at.s][:, :, :],
                              ALU.add).then_inc(*dve_b.did("both"))
            second.take_moments(dve, at, h[at.s])

        def shift_again(dve, at):
            second.make_shift(dve, at, lambda a: affine.scaled.after(a, "scaled"))

        def apply(dve, at):
            affine.apply_gain(dve, at, inner[at.s])
            affine.apply_offset(dve, at, inner[at.s])

        def relu(act, at):
            if at.has(SLOTS):
                act.wait_ge(*dve_b.after(at.back(SLOTS), "both"))
                act.wait_ge(*second.measured.after(at.back(SLOTS), "stats"))
            first.relu(act, at, h[at.s], rows[at.s]).then_inc(*act_h.did("h"))

        def scale(act, at):
            affine.scale(act, at, inner[at.s], h[at.s])

        def gelu(act, at):
            act.wait_ge(*affine.moved.after(at, "offset"))
            if at.has(SLOTS):
                act.wait_ge(*stored_out.after(at.back(SLOTS)))
            act.activation(out[at.s][:, :, :], inner[at.s][:, :, :], ACT.Gelu).then_inc(*act_o.did("out"))

        def root(pool, at):
            first.root(pool, at, lambda a: act_h.after(a, "h"))

        def root_again(pool, at):
            second.root(pool, at, lambda a: affine.scaled.after(a, "scaled"))

        self.sp = (load, 0), (store_both, 3), (store_out, 5)
        self.dve = (apply, 4), (shift_again, 3), (shift, 1), (add, 2), (moments, 0)
        self.act = (gelu, 4), (relu, 1), (scale, 3)
        self.pool = (root_again, 2), (root, 0)

    def stages(self, eng, which):
        return [(lambda at, stage=stage: stage(eng, at), lag) for stage, lag in which]


def between(nc, g, sums_table, table, root, bias, gain, offset, out_table):
    T = g.T
    with Pass(nc, "between") as w:
        weight, added = w.sb("root", [P, D]), Bias(w, "bias", B * D)
        sums, rows, rows_t = (w.slots(n, [P, B, D]) for n in ("sums", "rows", "rows_t"))
        conv, inner, out = (w.slots(n, [P, B, D]) for n in ("conv", "inner", "out"))
        t_ps = [w.ps(f"t_ps{k}", [P, B, D]) for k in range(2)]
        root_ps = [w.ps(f"root_ps{k}", [P, B, D]) for k in range(2)]
        norm = Norm(w, "norm")
        affine = Affine(w, "affine", norm, gain, offset)
        got, stored, gathered = w.moves("got", 1), w.moves("stored", 1), w.moves("gathered", B)
        loaded, gate = w.sem("loaded"), w.sem("gate")
        pe_s = w.steps("pe_t", "t_ps")
        pe_r = w.steps("pe_r", "root_ps")
        act_t, act_o = w.steps("act_t", "rows_t"), w.steps("act_o", "out")
        dve_c = w.steps("dve", "conv")
        with nc.Block() as block:

            @block.sync
            def _(sp):
                affine.load(sp)
                sp.dma_start(weight[:, :], root).then_inc(loaded, 16)
                added.load(sp, bias, 0, B)

                def load(at):
                    if at.has(SLOTS):
                        sp.wait_ge(*pe_s.after(at.back(SLOTS), "t_ps"))
                    sp.dma_start(rows[at.s][:, :, :], columns_of(table, T)[:, at.columns(), :]).then_inc(*got.did(at))

                def store(at):
                    sp.wait_ge(*act_o.after(at, "out"))
                    sp.dma_start(columns_of(out_table, T)[:, at.columns(), :], out[at.s][:, :, :]).then_inc(*stored.did(at))
                batches(sp, g.turns, (load, 0), (store, 5))
                stored.all_of(sp, g.turns)

            @block.gpsimd
            def _(pool):
                gather = gatherer(pool, w, g, gate, gathered, lambda at: [dve_c.after(at, "conv")],
                                  (sums_table, g.end, sums, 0, D))
                batches(pool, g.turns, (gather, 0),
                        (lambda at: norm.root(pool, at, lambda a: affine.scaled.after(a, "scaled")), 3))

            @block.tensor
            def _(pe):
                def turn(at):
                    pe.wait_ge(*got.after(at))
                    if at.has(2):
                        pe.wait_ge(*act_t.after(at.back(2), "rows_t"))
                    transpose_rows(pe, g, t_ps[at.s % 2], rows[at.s]).then_inc(*pe_s.did("t_ps"))

                def product(at):
                    pe.wait_ge(loaded, 16)
                    pe.wait_ge(added.ready, 1)
                    pe.wait_ge(*act_t.after(at, "rows_t"))
                    if at.has(2):
                        pe.wait_ge(*dve_c.after(at.back(2), "conv"))
                    rows_times(pe, root_ps[at.s % 2], rows_t[at.s], weight[:, :], added).then_inc(*pe_r.did("root_ps"))
                batches(pe, g.turns, (turn, 0), (product, 1))

            @block.scalar
            def _(act):
                def copy(at):
                    act.wait_ge(*pe_s.after(at, "t_ps"))
                    if at.has(SLOTS):
                        act.wait_ge(*pe_r.after(at.back(SLOTS), "root_ps"))
                    act.copy(rows_t[at.s][:, :, :], t_ps[at.s % 2][:, :, :]).then_inc(*act_t.did("rows_t"))

                def scale(at):
                    affine.scale(act, at, inner[at.s], conv[at.s])

                def gelu(at):
                    act.wait_ge(*affine.moved.after(at, "offset"))
                    if at.has(SLOTS):
                        act.wait_ge(*stored.after(at.back(SLOTS)))
                    act.activation(out[at.s][:, :, :], inner[at.s][:, :, :], ACT.Gelu).then_inc(*act_o.did("out"))
                batches(act, g.turns, (copy, 0), (gelu, 5), (scale, 4))

            @block.vector
            def _(dve):
                norm.prepare(dve)
                added.split(dve, g)
                dve.wait_ge(affine.loaded, 2 * 16)

                def add(at):
                    dve.wait_ge(*pe_r.after(at, "root_ps"))
                    dve.wait_ge(*gathered.after(at))
                    if at.has(SLOTS):
                        dve.wait_ge(*affine.scaled.after(at.back(SLOTS), "scaled"))
                    dve.tensor_tensor(conv[at.s][:, :, :], root_ps[at.s % 2][:, :, :], sums[at.s][:, :, :],
                                      ALU.add).then_inc(*dve_c.did("conv"))
                    dve.wait_ge(*dve_c.after(at, "conv"))
                    norm.take_moments(dve, at, conv[at.s])

                def shift(at):
                    norm.make_shift(dve, at, lambda a: affine.scaled.after(a, "scaled"))

                def apply(at):
                    affine.apply_gain(dve, at, inner[at.s])
                    affine.apply_offset(dve, at, inner[at.s])
                batches(dve, g.turns, (apply, 5), (shift, 4), (add, 1))


def project(nc, g, sums_table, table, root, bias, x_plus_h, w_qkv, b_qkv, x_table, h_table, q_table, kv_table):
    T = g.T
    with Pass(nc, "project") as w:
        weight, added = w.sb("root", [P, D]), Bias(w, "bias", B * D)
        wide, wide_bias = w.sb("w_qkv", [P, 3 * D]), w.sb("b_qkv", [P, 3 * D])
        sums, rows, rows_t, old = (w.slots(n, [P, B, D]) for n in ("sums", "rows", "rows_t", "old"))
        new, h, h_t = (w.slots(n, [P, B, D]) for n in ("new", "h", "h_t"))
        qkv = w.slots("qkv", [P, B, 3 * D])
        t_ps, h_ps = (w.ps(n, [P, B, D]) for n in ("t_ps", "h_ps"))
        root_ps = [w.ps(f"root_ps{k}", [P, B, D]) for k in range(2)]
        qkv_ps = [w.ps(f"qkv_ps{j}", [P, 3 * D]) for j in range(B)]
        norm = Norm(w, "norm")
        got, gathered = w.moves("got", 2), w.moves("gathered", B)
        stored, stored_h, stored_q = w.moves("stored", 1), w.moves("stored_h", 1), w.moves("stored_q", 2)
        loaded, gate = w.sem("loaded"), w.sem("gate")
        pe_t, pe_r, pe_h = w.steps("pe_t", "t_ps"), w.steps("pe_r", "root_ps"), w.steps("pe_h", "h_ps")
        pe_q = w.steps("pe_q", *[f"qkv_ps{j}" for j in range(B)])
        act_t, act_h, act_ht = w.steps("act_t", "rows_t"), w.steps("act_h", "h"), w.steps("act_ht", "h_t")
        dve_x = w.steps("dve_x", "conv", "new")
        dve_q = w.steps("dve_q", *[f"qkv{j}" for j in range(B)])
        with nc.Block() as block:

            @block.sync
            def _(sp):
                sp.dma_start(weight[:, :], root).then_inc(loaded, 16)
                added.load(sp, bias, 0, B)
                for k in range(3):
                    sp.dma_start(wide[:, k * D:(k + 1) * D], w_qkv[k]).then_inc(loaded, 16)
                    sp.dma_start(wide_bias[:, k * D:(k + 1) * D], b_qkv[k].partition_broadcast(P)).then_inc(loaded, 16)

                def load(at):
                    if at.has(SLOTS):
                        sp.wait_ge(*pe_t.after(at.back(SLOTS), "t_ps"))
                    sp.dma_start(rows[at.s][:, :, :], columns_of(table, T)[:, at.columns(), :]).then_inc(*got.did(at))
                    if at.has(SLOTS):
                        sp.wait_ge(*dve_x.after(at.back(SLOTS), "new"))
                    sp.dma_start(old[at.s][:, :, :], columns_of(x_plus_h, T)[:, at.columns(), :]).then_inc(*got.did(at))

                def store(at):
                    sp.wait_ge(*dve_x.after(at, "new"))
                    sp.dma_start(columns_of(x_table, T)[:, at.columns(), :], new[at.s][:, :, :]).then_inc(*stored.did(at))

                def store_h(at):
                    sp.wait_ge(*act_h.after(at, "h"))
                    sp.dma_start(columns_of(h_table, T)[:, at.columns(), :], h[at.s][:, :, :]).then_inc(*stored_h.did(at))

                def store_q(at):
                    sp.wait_ge(*dve_q.after(at, f"qkv{B - 1}"))
                    for out, a, b in ((q_table, 0, D), (kv_table, D, 3 * D)):
                        sp.dma_start(columns_of(out, T)[:, at.columns(), :], qkv[at.s][:, :, a:b]).then_inc(*stored_q.did(at))
                batches(sp, g.turns, (load, 0), (store, 2), (store_h, 5), (store_q, 8))
                for moves in (stored, stored_h, stored_q):
                    moves.all_of(sp, g.turns)

            @block.gpsimd
            def _(pool):
                gather = gatherer(pool, w, g, gate, gathered, lambda at: [dve_x.after(at, "conv")],
                                  (sums_table, g.end, sums, 0, D))
                batches(pool, g.turns, (gather, 0), (lambda at: norm.root(pool, at, lambda a: act_h.after(a, "h")), 3))

            @block.tensor
            def _(pe):
                def turn(at):
                    pe.wait_ge(*got.after(at))
                    if at.has(1):
                        pe.wait_ge(*act_t.after(at.back(1), "rows_t"))
                    transpose_rows(pe, g, t_ps, rows[at.s]).then_inc(*pe_t.did("t_ps"))

                def product(at):
                    pe.wait_ge(loaded, 7 * 16)
                    pe.wait_ge(added.ready, 1)
                    pe.wait_ge(*act_t.after(at, "rows_t"))
                    if at.has(2):
                        pe.wait_ge(*dve_x.after(at.back(2), "conv"))
                    rows_times(pe, root_ps[at.s % 2], rows_t[at.s], weight[:, :], added).then_inc(*pe_r.did("root_ps"))

                def turn_h(at):
                    pe.wait_ge(*act_h.after(at, "h"))
                    if at.has(1):
                        pe.wait_ge(*act_ht.after(at.back(1), "h_t"))
                    transpose_rows(pe, g, h_ps, h[at.s]).then_inc(*pe_h.did("h_ps"))

                def heads(at):
                    pe.wait_ge(*act_ht.after(at, "h_t"))
                    for j in range(B):
                        if at.has(1):
                            pe.wait_ge(*dve_q.after(at.back(1), f"qkv{j}"))
                        pe.matmul(qkv_ps[j][:, :], h_t[at.s][:, j, :], wide[:, :], start=True,
                                  stop=True).then_inc(*pe_q.did(f"qkv_ps{j}"))
                batches(pe, g.turns, (turn, 0), (product, 1), (turn_h, 5), (heads, 6))

            @block.scalar
            def _(act):
                def copy(at):
                    act.wait_ge(*pe_t.after(at, "t_ps"))
                    if at.has(SLOTS):
                        act.wait_ge(*pe_r.after(at.back(SLOTS), "root_ps"))
                    act.copy(rows_t[at.s][:, :, :], t_ps[:, :, :]).then_inc(*act_t.did("rows_t"))

                def relu(at):
                    if at.has(SLOTS):
                        act.wait_ge(*stored_h.after(at.back(SLOTS)))
                        act.wait_ge(*pe_h.after(at.back(SLOTS), "h_ps"))
                    norm.relu(act, at, h[at.s], new[at.s]).then_inc(*act_h.did("h"))

                def copy_h(at):
                    act.wait_ge(*pe_h.after(at, "h_ps"))
                    if at.has(SLOTS):
                        act.wait_ge(*pe_q.after(at.back(SLOTS), f"qkv_ps{B - 1}"))
                    act.copy(h_t[at.s][:, :, :], h_ps[:, :, :]).then_inc(*act_ht.did("h_t"))
                batches(act, g.turns, (copy, 0), (relu, 4), (copy_h, 5))

            @block.vector
            def _(dve):
                norm.prepare(dve)
                dve.wait_ge(loaded, 7 * 16)
                added.split(dve, g)

                def add(at):
                    dve.wait_ge(*pe_r.after(at, "root_ps"))
                    dve.wait_ge(*gathered.after(at))
                    dve.wait_ge(*got.after(at))
                    if at.has(SLOTS):
                        dve.wait_ge(*stored.after(at.back(SLOTS)))
                        dve.wait_ge(*act_h.after(at.back(SLOTS), "h"))
                    dve.tensor_tensor(new[at.s][:, :, :], root_ps[at.s % 2][:, :, :], sums[at.s][:, :, :],
                                      ALU.add).then_inc(*dve_x.did("conv"))
                    dve.wait_ge(*dve_x.after(at, "conv"))
                    dve.tensor_tensor(new[at.s][:, :, :], new[at.s][:, :, :], old[at.s][:, :, :],
                                      ALU.add).then_inc(*dve_x.did("new"))
                    dve.wait_ge(*dve_x.after(at, "new"))
                    norm.take_moments(dve, at, new[at.s])

                def shift(at):
                    norm.make_shift(dve, at, lambda a: act_h.after(a, "h"))

                def evacuate(at):
                    if at.has(SLOTS):
                        dve.wait_ge(*stored_q.after(at.back(SLOTS)))
                    for j in range(B):
                        dve.wait_ge(*pe_q.after(at, f"qkv_ps{j}"))
                        dve.tensor_tensor(qkv[at.s][:, j, :], qkv_ps[j][:, :], wide_bias[:, :],
                                          ALU.add).then_inc(*dve_q.did(f"qkv{j}"))
                batches(dve, g.turns, (evacuate, 7), (shift, 4), (add, 1))


def attend(nc, g, sums_table, h_table, x_table, wo, bo, w1, b1, w2, b2, g1, be1, g2, be2, new_x, new_h):
    T, width = g.T, D + HEADS + 1
    with Pass(nc, "attend") as w:
        wo_sb, w1_sb, w2_sb = (w.sb(n, [P, D]) for n in ("wo", "w1", "w2"))
        bo_added, b2_added, b1_col = Bias(w, "bo", B * D), Bias(w, "b2", B * D), w.sb("b1", [P, 1])
        sums = w.slots("sums", [P, B, width])
        share = w.slots("share", [P, B, HEADS])
        heads, heads_t, h_in, x_in = (w.slots(n, [P, B, D]) for n in ("heads", "heads_t", "h_in", "x_in"))
        pre_y, y, y_t, u_t = (w.slots(n, [P, B, D]) for n in ("pre_y", "y", "y_t", "u_t"))
        pre_z, z, x_out, h_out = (w.slots(n, [P, B, D]) for n in ("pre_z", "z", "x_out", "h_out"))
        heads_ps, o_ps, y_ps, u_ps, v_ps = (w.ps(n, [P, B, D]) for n in ("heads_ps", "o_ps", "y_ps", "u_ps", "v_ps"))
        norm_y, norm_z, norm_x = Norm(w, "norm_y"), Norm(w, "norm_z"), Norm(w, "norm_x")
        to_y, to_z = Affine(w, "to_y", norm_y, g1, be1), Affine(w, "to_z", norm_z, g2, be2)
        got_h, got_x, gathered = w.moves("got_h", 1), w.moves("got_x", 1), w.moves("gathered", B)
        stored_x, stored_h = w.moves("stored_x", 1), w.moves("stored_h", 1)
        loaded, gate = w.sem("loaded"), w.sem("gate")
        dve_h = w.steps("dve_h", "degree", "guarded", "share", "heads")
        pool_x = w.steps("pool_x", "with_offset")
        dve_y, dve_z, dve_x = w.steps("dve_y", "pre_y"), w.steps("dve_z", "pre_z"), w.steps("dve_x", "x_out")
        pe_h, pe_o, pe_y = w.steps("pe_h", "heads_ps"), w.steps("pe_o", "o_ps"), w.steps("pe_y", "y_ps")
        pe_u, pe_v = w.steps("pe_u", "u_ps"), w.steps("pe_v", "v_ps")
        act_h, act_y, act_u, act_x = (w.steps(f"act_{n}", n) for n in ("heads_t", "y_t", "u_t", "h_out"))
        with nc.Block() as block:

            @block.sync
            def _(sp):
                to_y.load(sp)
                to_z.load(sp)
                for out, weight in ((wo_sb, wo), (w1_sb, w1), (w2_sb, w2)):
                    sp.dma_start(out[:, :], weight).then_inc(loaded, 16)
                bo_added.load(sp, bo, 0, B)
                b2_added.load(sp, b2, 0, B)
                sp.dma_start(b1_col[:, :], b1.unsqueeze(1)).then_inc(loaded, 16)

                def load_h(at):
                    if at.has(SLOTS):
                        sp.wait_ge(*dve_y.after(at.back(SLOTS), "pre_y"))
                    sp.dma_start(h_in[at.s][:, :, :], columns_of(h_table, T)[:, at.columns(), :]).then_inc(*got_h.did(at))

                def load_x(at):
                    if at.has(SLOTS):
                        sp.wait_ge(*dve_x.after(at.back(SLOTS), "x_out"))
                    sp.dma_start(x_in[at.s][:, :, :], columns_of(x_table, T)[:, at.columns(), :]).then_inc(*got_x.did(at))

                def store_x(at):
                    sp.wait_ge(*dve_x.after(at, "x_out"))
                    sp.dma_start(columns_of(new_x, T)[:, at.columns(), :], x_out[at.s][:, :, :]).then_inc(*stored_x.did(at))

                def store_h(at):
                    sp.wait_ge(*act_x.after(at, "h_out"))
                    sp.dma_start(columns_of(new_h, T)[:, at.columns(), :], h_out[at.s][:, :, :]).then_inc(*stored_h.did(at))
                batches(sp, g.turns, (load_h, 1), (load_x, 4), (store_x, 7), (store_h, 8))
                stored_x.all_of(sp, g.turns)
                stored_h.all_of(sp, g.turns)

            @block.gpsimd
            def _(pool):
                gather = gatherer(pool, w, g, gate, gathered, lambda at: [dve_h.after(at, "heads")],
                                  (sums_table, g.end, sums, 0, width))
                def with_offset(at):
                    pool.wait_ge(*got_x.after(at))
                    pool.wait_ge(to_z.loaded, 2 * 16)
                    pool.tensor_tensor(x_in[at.s][:, :, :], x_in[at.s][:, :, :], over_batch(to_z.offset),
                                       ALU.add).then_inc(*pool_x.did("with_offset"))
                batches(pool, g.turns, (with_offset, 5), (gather, 0),
                        (lambda at: norm_x.root(pool, at, lambda a: act_x.after(a, "h_out")), 7),
                        (lambda at: norm_z.root(pool, at, lambda a: to_z.scaled.after(a, "scaled")), 5),
                        (lambda at: norm_y.root(pool, at, lambda a: to_y.scaled.after(a, "scaled")), 2))

            @block.tensor
            def _(pe):
                def turn_heads(at):
                    pe.wait_ge(*dve_h.after(at, "heads"))
                    if at.has(1):
                        pe.wait_ge(*act_h.after(at.back(1), "heads_t"))
                    transpose_rows(pe, g, heads_ps, heads[at.s]).then_inc(*pe_h.did("heads_ps"))

                def times_wo(at):
                    pe.wait_ge(loaded, 4 * 16)
                    pe.wait_ge(bo_added.ready, 1)
                    pe.wait_ge(b2_added.ready, 1)
                    pe.wait_ge(*act_h.after(at, "heads_t"))
                    if at.has(1):
                        pe.wait_ge(*dve_y.after(at.back(1), "pre_y"))
                    rows_times(pe, o_ps, heads_t[at.s], wo_sb[:, :], bo_added).then_inc(*pe_o.did("o_ps"))

                def turn_y(at):
                    pe.wait_ge(*to_y.moved.after(at, "offset"))
                    if at.has(1):
                        pe.wait_ge(*act_y.after(at.back(1), "y_t"))
                    transpose_rows(pe, g, y_ps, y[at.s]).then_inc(*pe_y.did("y_ps"))

                def times_w1(at):
                    pe.wait_ge(*act_y.after(at, "y_t"))
                    if at.has(1):
                        pe.wait_ge(*act_u.after(at.back(1), "u_t"))
                    pe.matmul(u_ps[:, :, :], w1_sb[:, :], y_t[at.s][:, :, :], start=True, stop=True).then_inc(*pe_u.did("u_ps"))

                def times_w2(at):
                    pe.wait_ge(*act_u.after(at, "u_t"))
                    if at.has(1):
                        pe.wait_ge(*dve_z.after(at.back(1), "pre_z"))
                    rows_times(pe, v_ps, u_t[at.s], w2_sb[:, :], b2_added).then_inc(*pe_v.did("v_ps"))
                batches(pe, g.turns, (times_w2, 5), (times_wo, 2), (turn_heads, 1), (turn_y, 4), (times_w1, 4))

            @block.scalar
            def _(act):
                def copy_heads(at):
                    act.wait_ge(*pe_h.after(at, "heads_ps"))
                    if at.has(SLOTS):
                        act.wait_ge(*pe_o.after(at.back(SLOTS), "o_ps"))
                    act.copy(heads_t[at.s][:, :, :], heads_ps[:, :, :]).then_inc(*act_h.did("heads_t"))

                def copy_y(at):
                    act.wait_ge(*pe_y.after(at, "y_ps"))
                    if at.has(SLOTS):
                        act.wait_ge(*pe_u.after(at.back(SLOTS), "u_ps"))
                    act.copy(y_t[at.s][:, :, :], y_ps[:, :, :]).then_inc(*act_y.did("y_t"))

                def gelu(at):
                    act.wait_ge(loaded, 4 * 16)
                    act.wait_ge(*pe_u.after(at, "u_ps"))
                    if at.has(SLOTS):
                        act.wait_ge(*pe_v.after(at.back(SLOTS), "v_ps"))
                    act.activation(u_t[at.s][:, :, :], u_ps[:, :, :], ACT.Gelu, bias=b1_col[:, :]).then_inc(*act_u.did("u_t"))

                def scale_y(at):
                    if at.has(SLOTS):
                        act.wait_ge(*dve_z.after(at.back(SLOTS), "pre_z"))
                    to_y.scale(act, at, y[at.s], pre_y[at.s])

                def scale_z(at):
                    if at.has(SLOTS):
                        act.wait_ge(*dve_x.after(at.back(SLOTS), "x_out"))
                    to_z.scale(act, at, z[at.s], pre_z[at.s])

                def relu(at):
                    if at.has(SLOTS):
                        act.wait_ge(*stored_h.after(at.back(SLOTS)))
                    norm_x.relu(act, at, h_out[at.s], x_out[at.s]).then_inc(*act_x.did("h_out"))
                batches(act, g.turns, (relu, 8), (scale_z, 6), (scale_y, 3), (copy_heads, 1), (copy_y, 4), (gelu, 4))

            @block.vector
            def _(dve):
                for norm in (norm_y, norm_z, norm_x):
                    norm.prepare(dve)
                for added in (bo_added, b2_added):
                    added.split(dve, g)
                for affine in (to_y, to_z):
                    dve.wait_ge(affine.loaded, 2 * 16)

                def guard(at):
                    dve.wait_ge(*gathered.after(at))
                    if at.has(SLOTS):
                        dve.wait_ge(*pe_h.after(at.back(SLOTS), "heads_ps"))
                    dve.tensor_copy(g.degree[:, at.columns()], sums[at.s][:, :, D + HEADS]).then_inc(*dve_h.did("degree"))
                    dve.tensor_scalar(share[at.s][:, :, :], sums[at.s][:, :, D:D + HEADS], 1e-16, None,
ALU.add).then_inc(*dve_h.did("guarded"))

                def divide(at):
                    dve.wait_ge(*dve_h.after(at, "guarded"))
                    dve.reciprocal(share[at.s][:, :, :], share[at.s][:, :, :]).then_inc(*dve_h.did("share"))

                def mean_of_values(at):
                    dve.wait_ge(*dve_h.after(at, "share"))
                    dve.tensor_tensor(heads[at.s][:, :, :].rearrange("p b (h d) -> p b h d", h=HEADS),
                                      sums[at.s][:, :, 0:D].rearrange("p b (h d) -> p b h d", h=HEADS),
                                      share[at.s][:, :, :].unsqueeze(3).to_broadcast([P, B, HEADS, HEAD_DIM]),
                                      ALU.mult).then_inc(*dve_h.did("heads"))

                def add_h(at):
                    dve.wait_ge(*pe_o.after(at, "o_ps"))
                    dve.wait_ge(*got_h.after(at))
                    if at.has(SLOTS):
                        dve.wait_ge(*to_y.scaled.after(at.back(SLOTS), "scaled"))
                    dve.tensor_tensor(pre_y[at.s][:, :, :], o_ps[:, :, :], h_in[at.s][:, :, :],
                                      ALU.add).then_inc(*dve_y.did("pre_y"))

                def stats_y(at):
                    dve.wait_ge(*dve_y.after(at, "pre_y"))
                    norm_y.take_stats(dve, at, pre_y[at.s])

                def add_y(at):
                    dve.wait_ge(*pe_v.after(at, "v_ps"))
                    dve.wait_ge(*to_y.moved.after(at, "offset"))
                    if at.has(SLOTS):
                        dve.wait_ge(*to_z.scaled.after(at.back(SLOTS), "scaled"))
                    dve.tensor_tensor(pre_z[at.s][:, :, :], v_ps[:, :, :], y[at.s][:, :, :],
                                      ALU.add).then_inc(*dve_z.did("pre_z"))

                def stats_z(at):
                    dve.wait_ge(*dve_z.after(at, "pre_z"))
                    norm_z.take_stats(dve, at, pre_z[at.s])

                def make_x(at):
                    dve.wait_ge(*to_z.gained.after(at, "gained"))
                    dve.wait_ge(*pool_x.after(at, "with_offset"))
                    if at.has(SLOTS):
                        dve.wait_ge(*stored_x.after(at.back(SLOTS)))
                        dve.wait_ge(*act_x.after(at.back(SLOTS), "h_out"))
                    dve.tensor_tensor(x_out[at.s][:, :, :], x_in[at.s][:, :, :], z[at.s][:, :, :],
                                      ALU.add).then_inc(*dve_x.did("x_out"))

                def stats_x(at):
                    dve.wait_ge(*dve_x.after(at, "x_out"))
                    norm_x.take_stats(dve, at, x_out[at.s])

                def shift_y(at):
                    norm_y.make_shift(dve, at, lambda a: to_y.scaled.after(a, "scaled"))

                def shift_z(at):
                    norm_z.make_shift(dve, at, lambda a: to_z.scaled.after(a, "scaled"))

                def shift_x(at):
                    norm_x.make_shift(dve, at, lambda a: act_x.after(a, "h_out"))
                batches(dve, g.turns, (shift_x, 8), (guard, 1),
                        (lambda at: to_y.apply_gain(dve, at, y[at.s]), 4), (divide, 1),
                        (lambda at: to_z.apply_gain(dve, at, z[at.s]), 7),
                        (lambda at: to_y.apply_offset(dve, at, y[at.s]), 4),
                        (shift_z, 6), (mean_of_values, 1), (make_x, 7), (shift_y, 3), (add_y, 5), (stats_x, 7), (stats_z, 5),
                        (lambda at: norm_x.aggregate(dve, at), 7), (add_h, 2), (lambda at: norm_z.aggregate(dve, at), 5),
                        (lambda at: norm_x.add_eps(dve, at), 7), (stats_y, 2), (lambda at: norm_z.add_eps(dve, at), 5),
                        (lambda at: norm_y.aggregate(dve, at), 2), (lambda at: norm_y.add_eps(dve, at), 2))


def gated_unit(nc, name, g, sums_table, width, edge_sums, h_table, w_msg_t, w_ih_t, w_hh_t, b_ih, b_hh, out_table,
               x_table=None, inverse_root=None, new_x=None):
    T = g.T
    first = width > D
    with Pass(nc, name) as w:
        msg_x, msg_e = w.sb("msg_x", [P, D]), w.sb("msg_e", [EDGE_DIM, D])
        w_ih, w_hh = w.sb("w_ih", [P, 3 * D]), w.sb("w_hh", [P, 3 * D])
        bias, bias_h = Bias(w, "bias", 4 * D), w.sb("bias_h", [3, 2 * D])
        sums, h = w.slots("sums", [P, B, width]), w.slots("h", [P, B, D])
        h_again = w.slots("h_again", [P, B, D])
        edges = None if first else w.slots("edges", [P, B, EDGE_DIM])
        s_t, h_t, m_t = (w.slots(n, [P, B, D]) for n in ("s_t", "h_t", "m_t"))
        e_t = w.slots("e_t", [EDGE_DIM, B, D])
        gates_sb = w.slots("gates", [P, B, 2 * D])
        inner, cand, out = (w.slots(n, [P, B, D]) for n in ("inner", "cand", "out"))
        s_ps, h_ps, m_ps = (w.ps(n, [P, B, D]) for n in ("s_ps", "h_ps", "m_ps"))
        e_ps = w.ps("e_ps", [EDGE_DIM, B, D])
        g_ps = [w.ps(f"g_ps{half}", [P, B // 2, 4 * D]) for half in range(2)]
        got, got_again, got_e = w.moves("got", 1), w.moves("got_again", 1), w.moves("got_e", 1)
        gathered, stored, stored_e = w.moves("gathered", B), w.moves("stored", 1), w.moves("stored_e", 1)
        loaded, gate, summed = w.sem("loaded"), w.sem("gate"), w.sem("summed")
        pe_t, pe_m = w.steps("pe_t", "s_ps", "h_ps", "e_ps"), w.steps("pe_m", "m_ps")
        pe_g = w.steps("pe_g", "gates0", "gates1")
        act_t, act_m = w.steps("act_t", "s_t", "e_t"), w.steps("act_m", "m_t")
        act_g, act_c = w.steps("act_g", "gates0", "gates1"), w.steps("act_c", "cand")
        dve_h, dve_i = w.steps("dve_h", "h_t"), w.steps("dve_i", "gated0", "inner0", "gated1", "inner1")
        dve_o = w.steps("dve_o", "apart", "kept", "out")
        n_loads = 5
        if not first:
            x = w.slots("x", [P, B, D])
            got_x, stored_x = w.moves("got_x", 1), w.moves("stored_x", 1)
            dve_x, act_r = w.steps("dve_x", "x"), w.steps("act_r", "rows")
            norm = Norm(w, "norm", inverse_root)

        with nc.Block() as block:

            @block.sync
            def _(sp):
                sp.dma_start(msg_x[:, :], w_msg_t[0:D, :]).then_inc(loaded, 16)
                sp.dma_start(msg_e[:, :], w_msg_t[D:D + EDGE_DIM, :]).then_inc(loaded, 16)
                sp.dma_start(w_ih[:, :], w_ih_t).then_inc(loaded, 16)
                sp.dma_start(w_hh[:, :], w_hh_t).then_inc(loaded, 16)
                bias.load(sp, b_ih)
                bias.load(sp, b_hh[2 * D:3 * D], 3 * D)
                sp.dma_start(bias_h[:, :], b_hh[0:2 * D].partition_broadcast(3)).then_inc(loaded, 16)

                def load(at):
                    if at.has(SLOTS):
                        sp.wait_ge(*pe_t.after(at.back(SLOTS), "e_ps"))
                    sp.dma_start(h[at.s][:, :, :], columns_of(h_table, T)[:, at.columns(), :]).then_inc(*got.did(at))
                    if not first:
                        sp.dma_start(edges[at.s][:, :, :], columns_of(edge_sums, T)[:, at.columns(), :]).then_inc(*got_e.did(at))

                def load_again(at):
                    if at.has(SLOTS):
                        sp.wait_ge(*dve_o.after(at.back(SLOTS), "apart"))
                    sp.dma_start(h_again[at.s][:, :, :], columns_of(h_table, T)[:, at.columns(), :]).then_inc(*got_again.did(at))

                def store_edges(at):
                    sp.wait_ge(*gathered.after(at))
                    sp.dma_start(columns_of(edge_sums, T)[:, at.columns(), :], sums[at.s][:, :, D:width]).then_inc(*stored_e.did(at))

                def load_x(at):
                    if at.has(SLOTS):
                        sp.wait_ge(*stored_x.after(at.back(SLOTS)))
                        sp.wait_ge(*act_r.after(at.back(SLOTS), "rows"))
                    sp.dma_start(x[at.s][:, :, :], columns_of(x_table, T)[:, at.columns(), :]).then_inc(*got_x.did(at))

                def store_x(at):
                    sp.wait_ge(*dve_x.after(at, "x"))
                    sp.dma_start(columns_of(new_x, T)[:, at.columns(), :], x[at.s][:, :, :]).then_inc(*stored_x.did(at))

                def store(at):
                    sp.wait_ge(*(dve_o.after(at, "out") if first else act_r.after(at, "rows")))
                    sp.dma_start(columns_of(out_table, T)[:, at.columns(), :], out[at.s][:, :, :]).then_inc(*stored.did(at))
                if first:
                    batches(sp, g.turns, (load, 0), (load_again, 2), (store, 5), (store_edges, 1))
                    stored_e.all_of(sp, g.turns)
                else:
                    batches(sp, g.turns, (load, 0), (load_again, 2), (load_x, 3), (store_x, 5), (store, 7))
                    stored_x.all_of(sp, g.turns)
                stored.all_of(sp, g.turns)

            @block.gpsimd
            def _(pool):
                free = lambda at: [pe_t.after(at, "e_ps")] + ([stored_e.after(at)] if first else [])
                gather = gatherer(pool, w, g, gate, gathered, free, (sums_table, g.end, sums, 0, width))
                if first:
                    batches(pool, g.turns, (gather, 0))
                else:
                    batches(pool, g.turns, (gather, 0),
                            (lambda at: norm.root(pool, at, lambda a: act_r.after(a, "rows")), 5))

            @block.tensor
            def _(pe):
                def turn(at):
                    pe.wait_ge(*gathered.after(at))
                    if at.has(1):
                        pe.wait_ge(*act_t.after(at.back(1), "s_t"))
                    for j in range(B):
                        last = pe.transpose(s_ps[:, j, :], sums[at.s][:, j, 0:D], g.ident[:, :])
                    last.then_inc(*pe_t.did("s_ps"))
                    pe.wait_ge(*got.after(at))
                    if at.has(1):
                        pe.wait_ge(*dve_h.after(at.back(1), "h_t"))
                    transpose_rows(pe, g, h_ps, h[at.s]).then_inc(*pe_t.did("h_ps"))
                    if at.has(1):
                        pe.wait_ge(*act_t.after(at.back(1), "e_t"))
                    if not first:
                        pe.wait_ge(*got_e.after(at))
                    pe.sem_inc(gate, 1)
                    for j in range(B):
                        last = pe.transpose(e_ps[:, j, :],
                                            sums[at.s][:, j, D:width] if first else edges[at.s][:, j, :], g.ident[:, :])
                    last.then_inc(*pe_t.did("e_ps"))

                def message(at):
                    pe.wait_ge(loaded, n_loads * 16)
                    pe.wait_ge(*act_t.after(at, "e_t"))
                    if at.has(1):
                        pe.wait_ge(*act_m.after(at.back(1), "m_t"))
                    pe.matmul(m_ps[:, :, :], msg_x[:, :], s_t[at.s][:, :, :], start=True, stop=False)
                    pe.matmul(m_ps[:, :, :], msg_e[:, :], e_t[at.s][:, :, :], start=False, stop=True).then_inc(*pe_m.did("m_ps"))

                def gates(at):
                    pe.wait_ge(bias.ready, 1)
                    pe.wait_ge(*dve_h.after(at, "h_t"))
                    pe.wait_ge(*act_m.after(at, "m_t"))
                    for half in range(2):
                        if at.has(1):
                            pe.wait_ge(*act_g.after(at.back(1), f"gates{half}"))
                            pe.wait_ge(*dve_i.after(at.back(1), f"inner{half}"))
                        pe.sem_inc(gate, 1)
                        for k in range(B // 2):
                            bank, j = g_ps[half][:, k, :], half * (B // 2) + k
                            bias.start(pe, bank)
                            for columns, rows_t, weight in ((slice(0, 3 * D), m_t, w_ih[:, :]),
                                                            (slice(0, 2 * D), h_t, w_hh[:, 0:2 * D]),
                                                            (slice(3 * D, 4 * D), h_t, w_hh[:, 2 * D:3 * D])):
                                last = pe.matmul(bank[:, columns], rows_t[at.s][:, j, :], weight,
                                                 start=False, stop=True, skip_group_check=True)
                        last.then_inc(*pe_g.did(f"gates{half}"))
                batches(pe, g.turns, (turn, 0), (message, 1), (gates, 2))

            @block.scalar
            def _(act):
                def copy(at):
                    act.wait_ge(*pe_t.after(at, "s_ps"))
                    if at.has(SLOTS):
                        act.wait_ge(*pe_m.after(at.back(SLOTS), "m_ps"))
                    act.copy(s_t[at.s][:, :, :], s_ps[:, :, :]).then_inc(*act_t.did("s_t"))
                    act.wait_ge(*pe_t.after(at, "e_ps"))
                    act.copy(e_t[at.s][:, :, :], e_ps[:, :, :]).then_inc(*act_t.did("e_t"))

                def copy_m(at):
                    act.wait_ge(*pe_m.after(at, "m_ps"))
                    if at.has(SLOTS):
                        act.wait_ge(*pe_g.after(at.back(SLOTS), "gates1"))
                    act.copy(m_t[at.s][:, :, :], m_ps[:, :, :]).then_inc(*act_m.did("m_t"))

                def squash(at):
                    if at.has(SLOTS):
                        act.wait_ge(*dve_o.after(at.back(SLOTS), "kept"))
                    for half in range(2):
                        act.wait_ge(*pe_g.after(at, f"gates{half}"))
                        act.activation(gates_sb[at.s][:, half * (B // 2):(half + 1) * (B // 2), :], g_ps[half][:, :, 0:2 * D],
                                       ACT.Sigmoid).then_inc(*act_g.did(f"gates{half}"))

                def candidate(at):
                    act.wait_ge(*dve_i.after(at, "inner1"))
                    if at.has(SLOTS):
                        act.wait_ge(*dve_o.after(at.back(SLOTS), "out"))
                    act.activation(cand[at.s][:, :, :], inner[at.s][:, :, :], ACT.Tanh).then_inc(*act_c.did("cand"))

                def relu(at):
                    norm.relu(act, at, out[at.s], x[at.s]).then_inc(*act_r.did("rows"))
                if first:
                    batches(act, g.turns, (copy, 0), (copy_m, 1), (candidate, 3), (squash, 2))
                else:
                    batches(act, g.turns, (copy, 0), (copy_m, 1), (candidate, 3), (relu, 6), (squash, 2))

            @block.vector
            def _(dve):
                dve.wait_ge(loaded, n_loads * 16)
                dve.wait_ge(bias.loaded, bias.loads * 16)
                dve.tensor_tensor(bias.raw[:, 0:2 * D], bias.raw[:, 0:2 * D], bias_h[:, :], ALU.add).then_inc(summed, 1)
                dve.wait_ge(summed, 1)
                bias.split(dve, g)
                if not first:
                    norm.prepare(dve)

                def copy(at):
                    dve.wait_ge(*pe_t.after(at, "h_ps"))
                    if at.has(SLOTS):
                        dve.wait_ge(*pe_g.after(at.back(SLOTS), "gates1"))
                    dve.tensor_copy(h_t[at.s][:, :, :], h_ps[:, :, :]).then_inc(*dve_h.did("h_t"))

                def gated(at):
                    if at.has(SLOTS):
                        dve.wait_ge(*act_c.after(at.back(SLOTS), "cand"))
                    for half in range(2):
                        columns = slice(half * (B // 2), (half + 1) * (B // 2))
                        dve.wait_ge(*act_g.after(at, f"gates{half}"))
                        dve.tensor_tensor(inner[at.s][:, columns, :], g_ps[half][:, :, 3 * D:4 * D],
                                          gates_sb[at.s][:, columns, 0:D], ALU.mult).then_inc(*dve_i.did(f"gated{half}"))
                        dve.wait_ge(*dve_i.after(at, f"gated{half}"))
                        dve.tensor_tensor(inner[at.s][:, columns, :], g_ps[half][:, :, 2 * D:3 * D],
                                          inner[at.s][:, columns, :], ALU.add).then_inc(*dve_i.did(f"inner{half}"))

                def mix(at):
                    dve.wait_ge(*act_c.after(at, "cand"))
                    dve.wait_ge(*got_again.after(at))
                    if at.has(SLOTS):
                        dve.wait_ge(*stored.after(at.back(SLOTS)))
                    dve.tensor_tensor(out[at.s][:, :, :], h_again[at.s][:, :, :], cand[at.s][:, :, :],
                                      ALU.subtract).then_inc(*dve_o.did("apart"))
                    dve.wait_ge(*dve_o.after(at, "apart"))
                    dve.tensor_tensor(out[at.s][:, :, :], out[at.s][:, :, :], gates_sb[at.s][:, :, D:2 * D],
                                      ALU.mult).then_inc(*dve_o.did("kept"))
                    dve.wait_ge(*dve_o.after(at, "kept"))
                    dve.tensor_tensor(out[at.s][:, :, :], out[at.s][:, :, :], cand[at.s][:, :, :],
                                      ALU.add).then_inc(*dve_o.did("out"))

                def add_x(at):
                    dve.wait_ge(*dve_o.after(at, "out"))
                    dve.wait_ge(*got_x.after(at))
                    dve.tensor_tensor(x[at.s][:, :, :], x[at.s][:, :, :], out[at.s][:, :, :],
                                      ALU.add).then_inc(*dve_x.did("x"))
                    dve.wait_ge(*dve_x.after(at, "x"))
                    norm.take_moments(dve, at, x[at.s])

                def shift(at):
                    norm.make_shift(dve, at, lambda a: act_r.after(a, "rows"))
                if first:
                    batches(dve, g.turns, (copy, 0), (mix, 4), (gated, 2))
                else:
                    batches(dve, g.turns, (copy, 0), (shift, 6), (mix, 4), (add_x, 4), (gated, 2))


def evolve_weight(nc, g, w0, w0_t, w_ih_t, w_hh_t, b_ih, b_hh, weight, inverse_root):
    T = g.T
    with Pass(nc, "evolve") as w:
        w0_sb, w0_t_sb = w.sb("w0", [P, D]), w.sb("w0_t", [P, D])
        w_ih, w_hh = w.sb("w_ih", [P, 3 * D]), w.sb("w_hh", [P, 3 * D])
        bias_i, bias_h = w.sb("bias_i", [P, 3 * D]), w.sb("bias_h", [P, 3 * D])
        gate_i, gate_h = w.sb("gate_i", [P, 3 * D]), w.sb("gate_h", [P, 3 * D])
        cand = w.sb("cand", [P, D])
        power, some = w.sb("power", [P, T]), w.sb("some", [P, T])
        i_ps, h_ps = w.ps("i_ps", [P, 3 * D]), w.ps("h_ps", [P, 3 * D])
        loaded, chain, product, ready, squashed, rooted = (w.sem(n) for n in (
            "loaded", "chain", "product", "ready", "squashed", "rooted"))
        with nc.Block() as block:

            @block.sync
            def _(sp):
                for out, table in ((w0_sb, w0), (w0_t_sb, w0_t), (w_ih, w_ih_t), (w_hh, w_hh_t)):
                    sp.dma_start(out[:, :], table).then_inc(loaded, 16)
                for out, vector in ((bias_i, b_ih), (bias_h, b_hh)):
                    sp.dma_start(out[:, :], vector.partition_broadcast(P)).then_inc(loaded, 16)

            @block.tensor
            def _(pe):
                pe.wait_ge(loaded, 6 * 16)
                pe.matmul(i_ps[:, :], w0_t_sb[:, :], w_ih[:, :], start=True, stop=True)
                pe.matmul(h_ps[:, :], w0_t_sb[:, :], w_hh[:, :], start=True, stop=True).then_inc(product, 1)

            @block.gpsimd
            def _(pool):
                pool.wait_ge(ready, 2)
                pool.tensor_tensor(inverse_root[:, :], g.degree[:, :], power[:, :], ALU.pow).then_inc(rooted, 1)

            @block.scalar
            def _(act):
                act.wait_ge(ready, 3)
                act.activation(gate_i[:, 0:2 * D], gate_i[:, 0:2 * D], ACT.Sigmoid).then_inc(squashed, 1)
                act.wait_ge(ready, 4)
                act.activation(cand[:, :], cand[:, :], ACT.Tanh).then_inc(squashed, 1)

            @block.vector
            def _(dve):
                n = 0

                def then(ins):
                    nonlocal n
                    n += 1
                    ins.then_inc(chain, 1)
                    dve.wait_ge(chain, n)

                then(dve.tensor_scalar(g.degree[:, :], g.degree[:, :], 1.0, None, ALU.add))
                then(dve.tensor_scalar(some[:, :], g.degree[:, :], 0.0, None, ALU.is_gt))
                dve.memset(power[:, :], -0.5).then_inc(ready, 1)
                dve.tensor_scalar(g.degree[:, :], g.degree[:, :], 1e-30, None, ALU.max).then_inc(ready, 1)
                dve.wait_ge(rooted, 1)
                then(dve.tensor_tensor(inverse_root[:, :], inverse_root[:, :], some[:, :], ALU.mult))
                dve.wait_ge(product, 1)
                dve.wait_ge(loaded, 6 * 16)
                then(dve.tensor_tensor(gate_i[:, :], i_ps[:, :], bias_i[:, :], ALU.add))
                then(dve.tensor_tensor(gate_h[:, :], h_ps[:, :], bias_h[:, :], ALU.add))
                dve.tensor_tensor(gate_i[:, 0:2 * D], gate_i[:, 0:2 * D], gate_h[:, 0:2 * D], ALU.add).then_inc(ready, 1)
                dve.wait_ge(squashed, 1)
                then(dve.tensor_tensor(cand[:, :], gate_i[:, 0:D], gate_h[:, 2 * D:3 * D], ALU.mult))
                dve.tensor_tensor(cand[:, :], cand[:, :], gate_i[:, 2 * D:3 * D], ALU.add).then_inc(ready, 1)
                dve.wait_ge(squashed, 2)
                then(dve.tensor_tensor(weight[:, :], w0_sb[:, :], cand[:, :], ALU.subtract))
                then(dve.tensor_tensor(weight[:, :], weight[:, :], gate_i[:, D:2 * D], ALU.mult))
                then(dve.tensor_tensor(weight[:, :], weight[:, :], cand[:, :], ALU.add))


def finish(nc, g, sums_table, rows_table, x_table, weight, inverse_root, lin_w_t, lin_b, out):
    T = g.T
    with Pass(nc, "finish") as w:
        lin, bias = w.sb("lin", [P, D]), w.sb("bias", [P, D])
        sums, own, old, both, h_t, a_t, new = (w.slots(n, [P, B, D]) for n in
                                               ("sums", "own", "old", "both", "h_t", "a_t", "new"))
        h_ps, a_ps = ([w.ps(f"{n}{k}", [P, B, D]) for k in range(2)] for n in ("h_ps", "a_ps"))
        out_ps = [w.ps(f"out_ps{k}", [P, B, D]) for k in range(2)]
        loaded, gate = w.sem("loaded"), w.sem("gate")
        got_own, got_old = w.moves("got_own", 1), w.moves("got_old", 1)
        gathered, stored = w.moves("gathered", B), w.moves("stored", 1)
        pe_h, pe_a, pe_o = w.steps("pe_h", "h_ps"), w.steps("pe_a", "a_ps"), w.steps("pe_o", "out_ps")
        act_a, act_t = w.steps("act_a", "a_t"), w.steps("act_t", "h_t")
        dve_b, dve_n = w.steps("dve_b", "both"), w.steps("dve_n", "with_bias", "new")
        with nc.Block() as block:

            @block.sync
            def _(sp):
                sp.dma_start(lin[:, :], lin_w_t).then_inc(loaded, 16)
                sp.dma_start(bias[:, :], lin_b.partition_broadcast(P)).then_inc(loaded, 16)

                def load_own(at):
                    if at.has(SLOTS):
                        sp.wait_ge(*dve_b.after(at.back(SLOTS), "both"))
                    sp.dma_start(own[at.s][:, :, :], columns_of(rows_table, T)[:, at.columns(), :]).then_inc(*got_own.did(at))

                def load_old(at):
                    if at.has(SLOTS):
                        sp.wait_ge(*dve_n.after(at.back(SLOTS), "new"))
                    sp.dma_start(old[at.s][:, :, :], columns_of(x_table, T)[:, at.columns(), :]).then_inc(*got_old.did(at))

                def store(at):
                    sp.wait_ge(*dve_n.after(at, "new"))
                    sp.dma_start(columns_of(out, T)[:, at.columns(), :], new[at.s][:, :, :]).then_inc(*stored.did(at))
                batches(sp, g.turns, (load_own, 0), (load_old, 2), (store, 4))
                stored.all_of(sp, g.turns)

            @block.gpsimd
            def _(pool):
                batches(pool, g.turns, (gatherer(pool, w, g, gate, gathered, lambda at: [dve_b.after(at, "both")],
                                                 (sums_table, g.end, sums, 0, D)), 0))

            @block.tensor
            def _(pe):
                def turn(at):
                    pe.wait_ge(*dve_b.after(at, "both"))
                    if at.has(2):
                        pe.wait_ge(*act_t.after(at.back(2), "h_t"))
                    transpose_rows(pe, g, h_ps[at.s % 2], both[at.s]).then_inc(*pe_h.did("h_ps"))

                def times_weight(at):
                    pe.wait_ge(*act_t.after(at, "h_t"))
                    if at.has(2):
                        pe.wait_ge(*act_a.after(at.back(2), "a_t"))
                    pe.matmul(a_ps[at.s % 2][:, :, :], weight[:, :], h_t[at.s][:, :, :], start=True,
                              stop=True).then_inc(*pe_a.did("a_ps"))

                def times_lin(at):
                    pe.wait_ge(loaded, 2 * 16)
                    pe.wait_ge(*act_a.after(at, "a_t"))
                    if at.has(2):
                        pe.wait_ge(*dve_n.after(at.back(2), "new"))
                    for j in range(B):
                        last = pe.matmul(out_ps[at.s % 2][:, j, :], a_t[at.s][:, j, :], lin[:, :], start=True, stop=True)
                    last.then_inc(*pe_o.did("out_ps"))
                batches(pe, g.turns, (times_lin, 2), (times_weight, 1), (turn, 0))

            @block.scalar
            def _(act):
                def copy(at):
                    act.wait_ge(*pe_h.after(at, "h_ps"))
                    if at.has(SLOTS):
                        act.wait_ge(*pe_a.after(at.back(SLOTS), "a_ps"))
                    act.copy(h_t[at.s][:, :, :], h_ps[at.s % 2][:, :, :]).then_inc(*act_t.did("h_t"))

                def relu(at):
                    act.wait_ge(*pe_a.after(at, "a_ps"))
                    if at.has(SLOTS):
                        act.wait_ge(*pe_o.after(at.back(SLOTS), "out_ps"))
                    act.activation(a_t[at.s][:, :, :], a_ps[at.s % 2][:, :, :], ACT.Relu).then_inc(*act_a.did("a_t"))
                batches(act, g.turns, (relu, 1), (copy, 0))

            @block.vector
            def _(dve):
                dve.wait_ge(loaded, 2 * 16)

                def add(at):
                    dve.wait_ge(*gathered.after(at))
                    dve.wait_ge(*got_own.after(at))
                    if at.has(SLOTS):
                        dve.wait_ge(*pe_h.after(at.back(SLOTS), "h_ps"))
                    dve.tensor_tensor(both[at.s][:, :, :], sums[at.s][:, :, :], own[at.s][:, :, :],
                                      ALU.add).then_inc(*dve_b.did("both"))

                def add_x(at):
                    dve.wait_ge(*got_old.after(at))
                    dve.tensor_tensor(old[at.s][:, :, :], old[at.s][:, :, :], over_batch(bias),
                                      ALU.add).then_inc(*dve_n.did("with_bias"))
                    dve.wait_ge(*dve_n.after(at, "with_bias"))
                    dve.wait_ge(*pe_o.after(at, "out_ps"))
                    if at.has(SLOTS):
                        dve.wait_ge(*stored.after(at.back(SLOTS)))
                    for j in range(B):
                        last = dve.scalar_tensor_tensor(new[at.s][:, j, :], out_ps[at.s % 2][:, j, :],
                                                        inverse_root[:, bass.ds(at.b * B + j, 1)], old[at.s][:, j, :],
                                                        ALU.mult, ALU.add)
                    last.then_inc(*dve_n.did("new"))
                batches(dve, g.turns, (add_x, 3), (add, 0))


def graph_layers(nc, a, T, out):
    rows = P * T

    def table(name, width, more=0):
        return nc.dram_tensor(name, (rows + more, width), F32, kind="Internal").ap()

    with ExitStack() as ctx:
        g = Graph(nc, ctx, T)
        weight = ctx.enter_context(nc.sbuf_tensor("evolved_weight", [P, D], F32))
        inverse_root = ctx.enter_context(nc.sbuf_tensor("inverse_root", [P, T], F32))
        records = table("records", RECORD)
        x_plus_h, conv1, conv2 = (table(n, D) for n in ("x_plus_h", "conv1", "conv2"))
        sort_edges(nc, g, a["src"], a["dst"], a["edge_type_8"], a["edge_weight"], a["edge_attr_8"], a["edge_attr_64"],
                   records, (a["x"], a["L0_gnn_ln1_g"], a["L0_gnn_ln1_b"], x_plus_h, conv1))
        read_order(nc, g, records)

        sums_a, sums_b = table("sums_a", D, 1), table("sums_b", D, 1)
        relational_sums(nc, "conv_a", g, conv1, a["L0_gnn_W1"], sums_a)
        between(nc, g, sums_a, conv1, a["L0_gnn_root1"], a["L0_gnn_b1"], a["L0_gnn_ln2_g"], a["L0_gnn_ln2_b"], conv2)
        relational_sums(nc, "conv_b", g, conv2, a["L0_gnn_W2"], sums_b)

        x1, h1, queries, edge_values = (table(n, D) for n in ("x1", "h1", "queries", "edge_values"))
        keys_values = table("keys_values", 2 * D)
        project(nc, g, sums_b, conv2, a["L0_gnn_root2"], a["L0_gnn_b2"], x_plus_h,
                [a["L1_gnn_Wq"], a["L1_gnn_Wk"], a["L1_gnn_Wv"]], [a["L1_gnn_bq"], a["L1_gnn_bk"], a["L1_gnn_bv"]],
                x1, h1, queries, keys_values)
        edge_scores(nc, g, queries, keys_values, edge_values)
        softmax_weights(nc, g, a["L1_gnn_edge_bias"])
        attended = table("attended", D + HEADS + 1, 1)
        row_sums(nc, "attended", g, [], [(columns_of(edge_values, T), 0, D)], D + HEADS + 1, attended, attended_message(g))
        x2, h2 = table("x2", D), table("h2", D)
        attend(nc, g, attended, h1, x1, *[a[f"L1_gnn_{n}"] for n in ("Wo", "bo", "W1", "b1", "W2", "b2", "g1", "be1", "g2", "be2")],
               x2, h2)

        evolve_weight(nc, g, a["L3_gnn_W0"], a["W0_t"], a["L3_gnn_gru_w_ih"], a["L3_gnn_gru_w_hh"],
                      a["L3_gnn_gru_b_ih"], a["L3_gnn_gru_b_hh"], weight, inverse_root)
        wide, narrow = table("sums_wide", D + EDGE_DIM, 1), table("sums_narrow", D, 1)
        edge_sums, unit1 = table("edge_sums", EDGE_DIM), table("unit1", D)
        x3, scaled, sums_e = table("x3", D), table("scaled", D), table("sums_e", D, 1)
        row_sums(nc, "passed_a", g, [(h2, g.src, 0, D)],
                 [(columns_of(records, T)[:, :, FIELDS:RECORD], D, D + EDGE_DIM)], D + EDGE_DIM, wide)
        gated_unit(nc, "unit_a", g, wide, D + EDGE_DIM, edge_sums, h2,
                   *[a[f"L2_gnn_{n}1"] for n in ("W_msg", "Wih", "Whh", "bih", "bhh")], unit1)
        row_sums(nc, "passed_b", g, [(unit1, g.src, 0, D)], [], D, narrow)
        gated_unit(nc, "unit_b", g, narrow, D, edge_sums, unit1,
                   *[a[f"L2_gnn_{n}2"] for n in ("W_msg", "Wih", "Whh", "bih", "bhh")], scaled,
                   x2, inverse_root, x3)

        row_sums(nc, "evolved", g, [(scaled, g.src, 0, D)], [], D, sums_e, weighted_message)
        finish(nc, g, sums_e, scaled, x3, weight, inverse_root, a["L3_gnn_lin_w"], a["L3_gnn_lin_b"], out)


def laid_out(inputs):
    import numpy as np

    a = {k: np.asarray(v) for k, v in inputs.items()}
    nodes, edges = a["x"].shape[0], a["src"].shape[0]
    assert a["x"].shape[1] == D and a["edge_attr_8"].shape[1] == RELATIONS and a["edge_attr_64"].shape[1] == EDGE_DIM
    unit = SLOTS * B
    T = -(-max(nodes + 1, edges) // (P * unit)) * unit
    for k in ("x", "src", "dst", "edge_type_8", "edge_weight", "edge_attr_8", "edge_attr_64"):
        padded = np.zeros((P * T,) + a[k].shape[1:], a[k].dtype)
        padded[:len(a[k])] = a[k]
        a[k] = padded
    a["dst"][edges:] = P * T - 1
    a["W0_t"] = a["L3_gnn_W0"].T
    for k in ("L2_gnn_W_msg1", "L2_gnn_W_msg2", "L2_gnn_Wih1", "L2_gnn_Wih2", "L2_gnn_Whh1", "L2_gnn_Whh2",
              "L3_gnn_gru_w_ih", "L3_gnn_gru_w_hh", "L3_gnn_lin_w"):
        a[k] = a[k].T
    return {k: np.ascontiguousarray(v) for k, v in a.items()}, T


def kernel(**inputs):
    import concourse.bacc as bacc
    from concourse.bass_utils import run_bass_kernel_spmd

    arrays, T = laid_out(inputs)
    nc = bacc.Bacc("TRN2", target_bir_lowering=False, num_devices=1)
    a = {k: nc.dram_tensor(f"in_{k}", v.shape, mybir.dt.from_np(v.dtype), kind="ExternalInput").ap()
         for k, v in arrays.items()}
    out = nc.dram_tensor("out", (P * T, D), F32, kind="ExternalOutput").ap()
    graph_layers(nc, a, T, out)
    result = run_bass_kernel_spmd(nc, [{f"in_{k}": v for k, v in arrays.items()}], core_ids=[0])
    return result.results[0]["out"][:inputs["x"].shape[0]]
```
